# Optimizing a Trainium2 kernel written in Bass

```python
import numpy as np
import jax
import jax.numpy as jnp

def _softmax(x, axis=-1):
    return jax.nn.softmax(x, axis=axis)

def _gelu(x):
    return jax.nn.gelu(x, approximate=True)

def _silu(x):
    return jax.nn.silu(x)

def _sigmoid(x):
    return jax.nn.sigmoid(x)

def _layernorm(x, axis=-1, eps=1e-05):
    m = jnp.mean(x, axis=axis, keepdims=True)
    v = jnp.var(x, axis=axis, keepdims=True)
    return (x - m) / jnp.sqrt(v + eps)

def _scatter_add(tgt, idx, src, axis=0):
    return tgt.at[idx].add(src)

def _segment_sum(src, seg, n):
    return jax.ops.segment_sum(src, seg, n)
kernel_name = 'mk_decoder_postln_d1_seqx_r8_c405ce'

def setup_inputs(seed: int=0):
    np.random.seed(seed)
    _w = jnp.asarray

    def _rec_inputs():
        import jax
        import jax.numpy as jnp
        _rk = jax.random.key(seed)
        x = -0.0003929 + 0.9999 * jax.random.normal(jax.random.fold_in(_rk, 1), (8, 56, 256), jnp.float32)
        _lenS = 56 - jax.random.randint(jax.random.fold_in(_rk, 7), (8,), 0, max(1, 56 // 4) + 1, jnp.int32)
        _lenS2 = 1500 - jax.random.randint(jax.random.fold_in(_rk, 8), (8,), 0, max(1, 1500 // 4) + 1, jnp.int32)
        _ctx_1024P = jax.random.normal(jax.random.fold_in(_rk, 11), (8, 16, 128), jnp.float32)
        _ctx_1024c = jax.random.dirichlet(jax.random.fold_in(_rk, 511), 0.3 * jnp.ones((16,), jnp.float32), (8, 1500))
        _ctx_1024t = jnp.einsum('bsk,bkd->bsd', _ctx_1024c, _ctx_1024P)
        _ctx_1024t = _ctx_1024t * jax.lax.rsqrt(jnp.mean(jnp.square(_ctx_1024t)) + 1e-12) * 0.953939
        ctx_1024 = -0.000494167 + 1.00018 * (_ctx_1024t + 0.3 * jax.random.normal(jax.random.fold_in(_rk, 611), (8, 1500, 128), jnp.float32))
        _validS = jnp.arange(56)[None, :] < _lenS[:, None]
        _validS2 = jnp.arange(1500)[None, :] < _lenS2[:, None]
        _causal = jnp.tril(jnp.ones((56, 56), dtype=bool))
        mask_BxS2_bf1 = jnp.ones((8, 1500), dtype=bool)
        return (x, ctx_1024, mask_BxS2_bf1)
    x, ctx_1024, mask_BxS2_bf1 = _rec_inputs()

    def _L0_attn_setup():
        import jax, jax.numpy as jnp
        import numpy as np
        EPS = 1e-15
        HEAD_DIM = 32
        PAD_VAL = 1.0
        key = jax.random.key(seed)
        k1, k2, k3, k4 = jax.random.split(key, 4)
        B, N, C = (2, 512, 256)
        s = 1.0 / np.sqrt(C).astype(np.float32)
        x = jax.random.normal(k1, (B, N, C), jnp.float32)
        w_qkv = jax.random.normal(k2, (3 * C, C), jnp.float32) * s
        w_proj = jax.random.normal(k3, (C, C), jnp.float32) * s
        b_proj = jax.random.normal(k4, (C,), jnp.float32) * 0.01
        return {'x': x, 'w_qkv': w_qkv, 'w_proj': w_proj, 'b_proj': b_proj}
    _L0_attn_all = _L0_attn_setup()
    _L0_attn_in = {k: v for k, v in _L0_attn_all.items() if k in ('w_qkv', 'w_proj', 'b_proj')}
    del _L0_attn_all

    def _L0_xattn_setup():
        import jax, jax.numpy as jnp
        import numpy as np
        N_HEADS = 16
        N_KV_HEADS = 8
        HEAD_DIM = 128
        D_TEXT = 256
        D_VISION = 128
        GROUPS = N_HEADS // N_KV_HEADS
        key = jax.random.key(seed)
        ks = jax.random.split(key, 6)
        B, T_text, T_vis = (4, 256, 72)
        text_hidden = jax.random.normal(ks[0], (B, T_text, D_TEXT), dtype=jnp.float32)
        vision_tokens = jax.random.normal(ks[1], (B, T_vis, D_VISION), dtype=jnp.float32)
        vision_mask = jnp.ones((B, T_vis), dtype=bool)
        s = 0.02
        Wq = jax.random.normal(ks[2], (D_TEXT, N_HEADS * HEAD_DIM), dtype=jnp.float32) * s
        Wk = jax.random.normal(ks[3], (D_VISION, N_KV_HEADS * HEAD_DIM), dtype=jnp.float32) * s
        Wv = jax.random.normal(ks[4], (D_VISION, N_KV_HEADS * HEAD_DIM), dtype=jnp.float32) * s
        Wo = jax.random.normal(ks[5], (N_HEADS * HEAD_DIM, D_TEXT), dtype=jnp.float32) * s
        return {'text_hidden': text_hidden, 'vision_tokens': vision_tokens, 'vision_mask': vision_mask, 'Wq': Wq, 'Wk': Wk, 'Wv': Wv, 'Wo': Wo}
    _L0_xattn_all = _L0_xattn_setup()
    _L0_xattn_in = {k: v for k, v in _L0_xattn_all.items() if k in ('Wq', 'Wk', 'Wv', 'Wo')}
    del _L0_xattn_all

    def _L0_ffn_setup():
        import jax, jax.numpy as jnp
        import numpy as np
        E, K, H, F = (64, 6, 256, 96)
        G, KG = (8, 4)
        SHARED_F = 96
        SCALE = 2.5
        T = 2 * 128
        CAP = 2 * (T * K // E)

        def _grouped_topk(logits, bias):
            scores = jax.nn.sigmoid(logits.astype(jnp.float32))
            scores_b = scores + bias[None, :]
            gs = scores_b.reshape(-1, G, E // G)
            group_scores = jnp.sum(jax.lax.top_k(gs, 2)[0], axis=-1)
            gidx = jax.lax.top_k(group_scores, KG)[1]
            rows = jnp.arange(group_scores.shape[0])[:, None]
            group_mask = jnp.zeros_like(group_scores).at[rows, gidx].set(1.0)
            score_mask = jnp.repeat(group_mask, E // G, axis=-1) > 0
            tmp = jnp.where(score_mask, scores_b, -jnp.inf)
            topk_ids = jax.lax.top_k(tmp, K)[1]
            topk_w = jnp.take_along_axis(scores, topk_ids, axis=-1)
            topk_w = topk_w / jnp.sum(topk_w, axis=-1, keepdims=True)
            return (topk_w * SCALE, topk_ids)

        def _routed_moe(x, topk_w, topk_ids, w_gate, w_up, w_down):
            Tn = x.shape[0]
            flat_e = topk_ids.reshape(-1)
            order = jnp.argsort(flat_e)
            se = flat_e[order]
            pos = jnp.arange(Tn * K) - jnp.searchsorted(se, se, side='left')
            tok = order // K
            valid = pos < CAP
            slot = jnp.where(valid, pos, CAP)
            buf = jnp.zeros((E, CAP + 1, H), x.dtype).at[se, slot].set(x[tok])[:, :CAP]
            h = jax.nn.silu(jnp.einsum('ech,ehf->ecf', buf, w_gate)) * jnp.einsum('ech,ehf->ecf', buf, w_up)
            out = jnp.einsum('ecf,efh->ech', h, w_down)
            gathered = out[se, jnp.minimum(pos, CAP - 1)] * valid.astype(x.dtype)[:, None]
            w = topk_w.reshape(-1)[order].astype(x.dtype)[:, None]
            return jax.ops.segment_sum(gathered * w, tok, num_segments=Tn)
        key = jax.random.key(seed)
        ks = jax.random.split(key, 9)
        s = 0.02
        return dict(hidden_states=jax.random.normal(ks[0], (2, 128, H), jnp.float32), gate_w=jax.random.normal(ks[1], (H, E), jnp.float32) * s, bias=jax.random.normal(ks[2], (E,), jnp.float32) * s, w_gate=jax.random.normal(ks[3], (E, H, F), jnp.float32) * s, w_up=jax.random.normal(ks[4], (E, H, F), jnp.float32) * s, w_down=jax.random.normal(ks[5], (E, F, H), jnp.float32) * s, ws_gate=jax.random.normal(ks[6], (H, SHARED_F), jnp.float32) * s, ws_up=jax.random.normal(ks[7], (H, SHARED_F), jnp.float32) * s, ws_down=jax.random.normal(ks[8], (SHARED_F, H), jnp.float32) * s)
    _L0_ffn_all = _L0_ffn_setup()
    _L0_ffn_in = {k: v for k, v in _L0_ffn_all.items() if k in ('gate_w', 'bias', 'w_gate', 'w_up', 'w_down', 'ws_gate', 'ws_up', 'ws_down')}
    del _L0_ffn_all
    return {'x': x, 'ctx_1024': ctx_1024, 'mask_BxS2_bf1': mask_BxS2_bf1, 'L0_attn_w_qkv': _L0_attn_in['w_qkv'], 'L0_attn_w_proj': _L0_attn_in['w_proj'], 'L0_attn_b_proj': _L0_attn_in['b_proj'], 'L0_xattn_Wq': _L0_xattn_in['Wq'], 'L0_xattn_Wk': _L0_xattn_in['Wk'], 'L0_xattn_Wv': _L0_xattn_in['Wv'], 'L0_xattn_Wo': _L0_xattn_in['Wo'], 'L0_ffn_gate_w': _L0_ffn_in['gate_w'], 'L0_ffn_bias': _L0_ffn_in['bias'], 'L0_ffn_w_gate': _L0_ffn_in['w_gate'], 'L0_ffn_w_up': _L0_ffn_in['w_up'], 'L0_ffn_w_down': _L0_ffn_in['w_down'], 'L0_ffn_ws_gate': _L0_ffn_in['ws_gate'], 'L0_ffn_ws_up': _L0_ffn_in['ws_up'], 'L0_ffn_ws_down': _L0_ffn_in['ws_down']}

def reference(x, ctx_1024, mask_BxS2_bf1, L0_attn_w_qkv, L0_attn_w_proj, L0_attn_b_proj, L0_xattn_Wq, L0_xattn_Wk, L0_xattn_Wv, L0_xattn_Wo, L0_ffn_gate_w, L0_ffn_bias, L0_ffn_w_gate, L0_ffn_w_up, L0_ffn_w_down, L0_ffn_ws_gate, L0_ffn_ws_up, L0_ffn_ws_down):
    import jax
    import jax.numpy as jnp

    def _L0_attn_ref(x, w_qkv, w_proj, b_proj):
        import jax, jax.numpy as jnp
        import numpy as np
        EPS = 1e-15
        HEAD_DIM = 32
        PAD_VAL = 1.0
        B, N, C = x.shape
        d = HEAD_DIM
        h = C // d
        qkv = (x @ w_qkv.T).reshape(B, N, 3, C)
        q, k, v = (qkv[:, :, 0], qkv[:, :, 1], qkv[:, :, 2])

        def to_heads(t):
            return t.reshape(B, N, h, d).transpose(0, 2, 3, 1)
        q = jax.nn.relu(to_heads(q))
        k = jax.nn.relu(to_heads(k))
        v = to_heads(v)
        v_pad = jnp.pad(v, ((0, 0), (0, 0), (0, 1), (0, 0)), constant_values=PAD_VAL)
        vk = jnp.einsum('bhen,bhdn->bhed', v_pad, k)
        out = jnp.einsum('bhed,bhdn->bhen', vk, q)
        out = out[:, :, :-1] / (out[:, :, -1:] + EPS)
        out = out.reshape(B, C, N).transpose(0, 2, 1)
        return out @ w_proj.T + b_proj

    def _L0_xattn_ref(text_hidden, vision_tokens, vision_mask, Wq, Wk, Wv, Wo):
        import jax, jax.numpy as jnp
        import numpy as np
        N_HEADS = 16
        N_KV_HEADS = 8
        HEAD_DIM = 128
        D_TEXT = 256
        D_VISION = 128
        GROUPS = N_HEADS // N_KV_HEADS
        B, T_text, _ = text_hidden.shape
        T_vis = vision_tokens.shape[1]
        scale = jnp.float32(np.sqrt(HEAD_DIM))
        q = (text_hidden @ Wq).reshape(B, T_text, N_HEADS, HEAD_DIM).transpose(0, 2, 1, 3)
        k = (vision_tokens @ Wk).reshape(B, T_vis, N_KV_HEADS, HEAD_DIM).transpose(0, 2, 1, 3)
        v = (vision_tokens @ Wv).reshape(B, T_vis, N_KV_HEADS, HEAD_DIM).transpose(0, 2, 1, 3)
        k = jnp.repeat(k, GROUPS, axis=1)
        v = jnp.repeat(v, GROUPS, axis=1)
        scores = jnp.einsum('bhtd,bhsd->bhts', q, k) / scale
        mask = vision_mask[:, None, None, :]
        scores = jnp.where(mask, scores, -jnp.inf)
        attn = jax.nn.softmax(scores, axis=-1)
        attn = jnp.nan_to_num(attn, nan=0.0)
        out = jnp.einsum('bhts,bhsd->bhtd', attn, v)
        out = out.transpose(0, 2, 1, 3).reshape(B, T_text, N_HEADS * HEAD_DIM)
        return out @ Wo

    def _L0_ffn_ref(hidden_states, gate_w, bias, w_gate, w_up, w_down, ws_gate, ws_up, ws_down):
        import jax, jax.numpy as jnp
        import numpy as np
        E, K, H, F = (64, 6, 256, 96)
        G, KG = (8, 4)
        SHARED_F = 96
        SCALE = 2.5
        T = 2 * 128
        CAP = 2 * (T * K // E)

        def _grouped_topk(logits, bias):
            scores = jax.nn.sigmoid(logits.astype(jnp.float32))
            scores_b = scores + bias[None, :]
            gs = scores_b.reshape(-1, G, E // G)
            group_scores = jnp.sum(jax.lax.top_k(gs, 2)[0], axis=-1)
            gidx = jax.lax.top_k(group_scores, KG)[1]
            rows = jnp.arange(group_scores.shape[0])[:, None]
            group_mask = jnp.zeros_like(group_scores).at[rows, gidx].set(1.0)
            score_mask = jnp.repeat(group_mask, E // G, axis=-1) > 0
            tmp = jnp.where(score_mask, scores_b, -jnp.inf)
            topk_ids = jax.lax.top_k(tmp, K)[1]
            topk_w = jnp.take_along_axis(scores, topk_ids, axis=-1)
            topk_w = topk_w / jnp.sum(topk_w, axis=-1, keepdims=True)
            return (topk_w * SCALE, topk_ids)

        def _routed_moe(x, topk_w, topk_ids, w_gate, w_up, w_down):
            Tn = x.shape[0]
            flat_e = topk_ids.reshape(-1)
            order = jnp.argsort(flat_e)
            se = flat_e[order]
            pos = jnp.arange(Tn * K) - jnp.searchsorted(se, se, side='left')
            tok = order // K
            valid = pos < CAP
            slot = jnp.where(valid, pos, CAP)
            buf = jnp.zeros((E, CAP + 1, H), x.dtype).at[se, slot].set(x[tok])[:, :CAP]
            h = jax.nn.silu(jnp.einsum('ech,ehf->ecf', buf, w_gate)) * jnp.einsum('ech,ehf->ecf', buf, w_up)
            out = jnp.einsum('ecf,efh->ech', h, w_down)
            gathered = out[se, jnp.minimum(pos, CAP - 1)] * valid.astype(x.dtype)[:, None]
            w = topk_w.reshape(-1)[order].astype(x.dtype)[:, None]
            return jax.ops.segment_sum(gathered * w, tok, num_segments=Tn)
        orig_shape = hidden_states.shape
        x = hidden_states.reshape(-1, H)
        router_logits = x @ gate_w
        topk_w, topk_ids = _grouped_topk(router_logits, bias)
        y = _routed_moe(x, topk_w, topk_ids, w_gate, w_up, w_down)
        shared = jax.nn.silu(x @ ws_gate) * (x @ ws_up) @ ws_down
        return (y + shared).reshape(orig_shape)
    x = _layernorm(x + _L0_attn_ref(x, L0_attn_w_qkv, L0_attn_w_proj, L0_attn_b_proj), axis=-1)
    x = _layernorm(x + _L0_xattn_ref(x, ctx_1024, mask_BxS2_bf1, L0_xattn_Wq, L0_xattn_Wk, L0_xattn_Wv, L0_xattn_Wo), axis=-1)
    x = _layernorm(x + _L0_ffn_ref(x, L0_ffn_gate_w, L0_ffn_bias, L0_ffn_w_gate, L0_ffn_w_up, L0_ffn_w_down, L0_ffn_ws_gate, L0_ffn_ws_up, L0_ffn_ws_down), axis=-1)
    return x

_drawn_inputs = setup_inputs


def setup_inputs(seed=0):
    import zlib

    import numpy as np

    out = dict(_drawn_inputs(seed))
    spreads = {}
    factors = {'L0_attn_b_proj': 6.147,
     'L0_xattn_Wq': 8.0,
     'L0_xattn_Wk': 8.0,
     'L0_ffn_gate_w': 6.068,
     'L0_ffn_bias': 8.0,
     'L0_ffn_w_gate': 5.841,
     'L0_ffn_w_up': 5.78,
     'L0_ffn_w_down': 5.772,
     'L0_ffn_ws_gate': 5.559,
     'L0_ffn_ws_up': 5.542,
     'L0_ffn_ws_down': 5.514}
    for name, (base, spread) in spreads.items():
        noise = np.random.default_rng([zlib.crc32(name.encode()), seed]).standard_normal(out[name].shape)
        drawn = base * np.exp(spread * noise) if base else spread * noise
        out[name] = jnp.asarray(drawn.astype(out[name].dtype))
    for name, factor in factors.items():
        out[name] = (out[name] * factor).astype(out[name].dtype)
    return out
```

```python
from contextlib import ExitStack

import concourse.bass as bass
from concourse import mybir

F32 = mybir.dt.float32
F16 = mybir.dt.float16
BF16 = mybir.dt.bfloat16
U8 = mybir.dt.uint8
I32 = mybir.dt.int32
ALU = mybir.AluOpType
ACT = mybir.ActivationFunctionType
AX = mybir.AxisListType

P = 128
B, N, C = 8, 56, 256
NT = B // 2
HALF = 64
CC = C // P
HD = 32
LH = C // HD
HC = P // HD
VW = HD + 1
SK, D = 1500, 128
KT, KP = 12, 125
QH, GH = 16, 8
NQ = N * QH
QT = NQ // P
NB = 3
KB = SK // NB
TB = KT // NB
PAIR = 2 * QT
TILES = B * QT
E, TOPK, G, KG, F = 64, 6, 8, 4, 96
EG = E // G
CAP = 48
SLOT = 64
GE = 8
NG = E // GE
GP = GE // 2
PAIRS = E // 2
SCALE = 2.5
LN_EPS, DEN_EPS = 1e-5, 1e-15
BIG = 1e30
LOG_P = 6.931471805599453

FRONT = [("xT", 2, "va"), ("wqkvT", 4, "va"), ("qT", 2, "va"), ("kv", 4, "b"), ("wpT", 1, "a"),
         ("WkT", 2, "va"), ("WqT", 8, "av"), ("G", 8, "v"), ("M", 8, "av"), ("lin", 4, "v"),
         ("WvT", 2, "a"), ("aoT", 2, "va"), ("proj", 4, "v"), ("W2", 8, "av"), ("x1T", 2, "va"),
         ("Qt", 16, "b"), ("cT", NB, "av")]
MID = [("x2T", 2, "va"), ("logit", 1, "a"), ("shgu", 4, "b"), ("shT", 1, "v"), ("shy", 4, "v"), ("pos", 1, "v")]


class Fills:

    def __init__(self, plan):
        self.first, self.by = {}, []
        for name, n, engines in plan:
            self.first[name] = len(self.by)
            self.by += [engines[i % len(engines)] for i in range(n)]

    def at(self, name, i=0):
        return self.first[name] + i

    def emptied(self, engine, f):
        return sum(e in (engine, "b") for e in self.by[:f + 1])

    def takes(self, engine, f):
        return self.by[f] in (engine, "b")


def decoder_kernel(nc, x, ctx, mask, w_qkv, w_proj, b_proj, Wq, Wk, Wv, Wo, gate_w, bias,
                   w_gate, w_up, w_down, ws_gate, ws_up, ws_down, out):
    with ExitStack() as stack:
        def sb(name, shape, dt):
            return stack.enter_context(nc.sbuf_tensor(name, shape, dt))

        def sem(name):
            return stack.enter_context(nc.semaphore(name))

        def carver(region):
            at = [0]

            def carve(shape, dt, size):
                n = 1
                for s in shape:
                    n *= s
                words = (n * size + 3) // 4
                v = region[:, at[0]:at[0] + words]
                at[0] += words
                if dt != F32:
                    v = v.bitcast(dt)
                names = "abcde"[:len(shape)]
                if len(shape) > 1:
                    v = v.rearrange(f"p ({' '.join(names)}) -> p {' '.join(names)}",
                                    **{c: s for c, s in zip(names, shape)})
                return v
            return carve

        ra = sb("ra", [P, 76 * 256], F32)
        cut = carver(ra)
        wq_in = cut([CC, QH * D], F32, 4)
        wqT = cut([QH, CC, P], F32, 4)
        wo_in = cut([QH, C], F32, 4)
        wqkv_in = cut([6, C], F32, 4)
        wqkvT = cut([CC, 3 * C], F32, 4)
        wk_in = cut([GH, D], F32, 4)
        wv_in = cut([GH, D], F32, 4)
        wkT = cut([GH, D], F32, 4)
        wvT = cut([GH, D], F32, 4)
        M = wq_in.rearrange("p a (h b c) -> p (a h) b c", b=CC, c=D)
        cut = carver(ra)
        sc = cut([2, SK], F32, 4)
        pT = cut([2, 2, KT * P], F16, 2)
        w_gu = cut([2, 2, GE, CC * F], F32, 4)
        w_dn = cut([2, GE, C], F32, 4)
        rb = sb("rb", [P, 29 * 256], F32)
        cut = carver(rb)
        qT = cut([CC, NT * P], F32, 4)
        k_sb = cut([NT, C], F32, 4)
        v_aug = cut([NT, LH, VW], F32, 4)
        kvm = cut([B, CC * HC * VW], F32, 4)
        ao = cut([NT, C], F32, 4)
        aoT = cut([CC, NT * P], F32, 4)
        cut = carver(rb)
        cT = cut([2, 2, SK], F16, 2)
        oT = cut([2, HALF * QH], F32, 4)
        q_st = cut([2, 2, NQ], F16, 2)
        rc = sb("rc", [P, 30 * 256], F32)
        cut = carver(rc)
        Qt = cut([2, B, NQ], F16, 2)
        cut = carver(rc)
        x2h = cut([2, NT, CC, P], F16, 2)
        disp = cut([2, NT, GE, SLOT], F16, 2)
        xs = cut([2, CC, GE, SLOT], F32, 4)
        dispT = cut([GP, NT * P], F16, 2)
        w_grp = cut([2, NT, GE, 2], F16, 2)
        ws_slot = cut([2, GP], F32, 4)
        yT_sb = cut([CC, NT * P], F32, 4)
        c_in = sb("c_in", [KP, KT, D], F32)
        c16 = sb("c16", [KP, 2, KT, 2, D], F16)
        m_in = sb("m_in", [P, SK], U8)
        mb = sb("mb", [P, 2, SK], BF16)
        W2 = sb("W2", [P, QH, C], F32)
        x_sb = sb("x_sb", [P, NT, C], F32)
        xT = sb("xT", [P, CC, NT * P], F32)
        x1 = sb("x1", [P, NT, C], F32)
        x1T = sb("x1T", [P, CC, NT * P], F32)
        wp_in = sb("wp_in", [P, CC, C], F32)
        wpT = sb("wpT", [P, CC, C], F32)
        bproj = sb("bproj", [P, C], F32)
        ident = sb("ident", [P, P], F32)
        ident16 = sb("ident16", [P, P], F16)
        ones16 = sb("ones16", [P, P], F16)
        before = sb("before", [P, P], F16)
        zero16 = sb("zero16", [P, NT * P], F16)
        headmask = sb("headmask", [P, HC, VW], F32)
        slots_i = sb("slots_i", [P, CAP], I32)
        slots = sb("slots", [P, CAP], F16)
        in_batch = sb("in_batch", [P, 2], F32)
        valid = sb("valid", [P, 1], F32)
        mx3 = sb("mx3", [P, 2, NB], F32)
        mxa = sb("mxa", [P, 2], F32)
        nb = sb("nb", [P, 2], F32)
        rs = sb("rs", [P, 2], F32)
        rinv = sb("rinv", [P, 2], F32)
        rr = sb("rr", [P, 2], F32)
        o2 = sb("o2", [P, 2, D], F32)
        on = sb("on", [P, 2, D], F32)
        den = sb("den", [P, 2 * NT, LH], F32)
        st = sb("st", [P, NT, 6], F32)
        mv = sb("mv", [P, NT, 2], F32)
        ve = sb("ve", [P, NT], F32)
        sd = sb("sd", [P, NT], F32)
        rstd = sb("rstd", [P, NT], F32)
        gw = sb("gw", [P, CC, E], F32)
        gbias = sb("gbias", [P, E], F32)
        wsgu = sb("wsgu", [P, CC, 2, F], F32)
        wsd = sb("wsd", [F, C], F32)
        cut = carver(rb)
        r1 = cut([NT, E], F32, 4)
        r2 = cut([NT, E], F32, 4)
        r3 = cut([NT, E + 2], F32, 4)
        r4 = cut([NT, E + 2], F32, 4)
        m8 = cut([NT * G, 8], F32, 4)
        gs = cut([NT, G + KG], F32, 4)
        gsr = cut([NT, G + KG], F32, 4)
        t8 = cut([NT, 8], F32, 4)
        t6 = cut([NT, 8], F32, 4)
        gsel = cut([NT, G], F32, 4)
        gpen = cut([NT, G], F32, 4)
        sel16 = cut([NT, E], F16, 2)
        w16 = cut([NT, E + GE, 2], F16, 2)
        posm = cut([NT, E + GE], F16, 2)
        wsum = cut([NT], F32, 4)
        wrec = cut([NT], F32, 4)
        sh_g = cut([2, F], F32, 4)
        sh_h = cut([NT, F], F32, 4)
        sh_hT = cut([NT * P], F32, 4)[0:F]
        act_g = cut([2, F], F32, 4)
        h_sb = cut([2, F], F32, 4)
        hT = cut([2, P], F32, 4)[0:F]
        o_hl = cut([2, 2, C], F16, 2)

        ps = stack.enter_context(nc.psum_tensor("ps", [P, 8, 512], F32))

        x_in, wqkv_dma, wp_dma, wk_dma, wq_dma, wv_dma, wo_dma, small_dma = (
            sem(n) for n in ("x_in", "wqkv_dma", "wp_dma", "wk_dma", "wq_dma", "wv_dma", "wo_dma", "small_dma"))
        bproj_dma = sem("bproj_dma")
        ctx_dma, mask_dma = sem("ctx_dma"), sem("mask_dma")
        ew_dma = [sem("ew_dma0"), sem("ew_dma1")]
        out_dma = sem("out_dma")
        pads_zero = sem("pads_zero")
        const_step = sem("const_step")
        consts_set = sem("consts_set")
        dve_const = sem("dve_const")
        filled, emptied_v, emptied_a = sem("filled"), sem("emptied_v"), sem("emptied_a")
        filled2, emptied2_v, emptied2_a = sem("filled2"), sem("emptied2_v"), sem("emptied2_a")
        dve_step = sem("dve_step")
        act_step = sem("act_step")
        ln_var, ln_std, ln_out = sem("ln_var"), sem("ln_std"), sem("ln_out")
        ao_ready = sem("ao_ready")
        ctx_high = sem("ctx_high")
        ctx_split, mask_bias, q_staged, oT_zero = sem("ctx_split"), sem("mask_bias"), sem("q_staged"), sem("oT_zero")
        scored, p_trans, pv_done, o_trans, cT_trans, proj_done = (
            sem(n) for n in ("scored", "p_trans", "pv_done", "o_trans", "cT_trans", "proj_done"))
        masked, row_max, bias_ready, p_low, recip1, recip_ready, o_norm, pair_sum = (
            sem(n) for n in ("masked", "row_max", "bias_ready", "p_low", "recip1", "recip_ready", "o_norm", "pair_sum"))
        exp_done, p_high, o2_done, oT_copied, cT_copied = (
            sem(n) for n in ("exp_done", "p_high", "o2_done", "oT_copied", "cT_copied"))
        x2_split, routed, sh_act, sh_done = sem("x2_split"), sem("routed"), sem("sh_act"), sem("sh_done")
        disp_built, xs_filled, xs_a, xs_v, w_filled, w_copied = (
            sem(n) for n in ("disp_built", "xs_filled", "xs_a", "xs_v", "w_filled", "w_copied"))
        dT_filled, dT_copied, gu_filled, silu_done, h_ready, hT_filled, hT_copied, dn_filled, o_high, o_low, comb_done = (
            sem(n) for n in ("dT_filled", "dT_copied", "gu_filled", "silu_done", "h_ready", "hT_filled", "hT_copied",
                             "dn_filled", "o_high", "o_low", "comb_done"))
        y_filled, y_copied, y_copied_a, yb_filled = sem("y_filled"), sem("y_copied"), sem("y_copied_a"), sem("yb_filled")

        front, mid = Fills(FRONT), Fills(MID)

        def front_wait(eng, name, i=0):
            f = front.at(name, i)
            if front.takes("v", f):
                eng.wait_ge(emptied_v, front.emptied("v", f))
            if front.takes("a", f):
                eng.wait_ge(emptied_a, front.emptied("a", f))

        def mid_wait(eng, name, i=0):
            f = mid.at(name, i)
            if mid.takes("v", f):
                eng.wait_ge(emptied2_v, mid.emptied("v", f))
            if mid.takes("a", f):
                eng.wait_ge(emptied2_a, mid.emptied("a", f))

        def wait_alone(eng, semaphore, value):
            value = value if isinstance(value, int) else eng.to_reg(value)
            eng.wait_ge(consts_set, 8)
            eng.wait_ge(semaphore, value)

        block = stack.enter_context(nc.Block())

        @block.sync
        def _(sp):
            sp.wait_ge(pads_zero, 1)
            for k in range(2):
                sp.dma_start(x_sb[HALF * k:HALF * k + N, :, :],
                             x.rearrange("(j k) n c -> k n j c", k=2)[k]).then_inc(x_in, 16)
            sp.dma_start(wqkv_in, w_qkv.rearrange("(g p) c -> p g c", p=P)).then_inc(wqkv_dma, 16)
            sp.dma_start(wp_in[:], w_proj.rearrange("(g p) c -> p g c", p=P)).then_inc(wp_dma, 16)
            sp.dma_start(wk_in, Wk.rearrange("e (g d) -> e g d", d=D)).then_inc(wk_dma, 16)
            sp.dma_start(wq_in, Wq.rearrange("(k p) n -> p k n", p=P)).then_inc(wq_dma, 16)
            sp.dma_start(bproj[:], b_proj.rearrange("(a c) -> a c", a=1).to_broadcast([P, C])).then_inc(bproj_dma, 16)
            sp.dma_start(wv_in, Wv.rearrange("e (g d) -> e g d", d=D)).then_inc(wv_dma, 16)
            sp.dma_start(wo_in, Wo.rearrange("(h v) n -> v h n", v=D)).then_inc(wo_dma, 16)

            def load_batch(b):
                if b >= 1:
                    sp.wait_ge(ctx_split, b)
                    sp.wait_ge(mask_bias, b)
                s = b % B
                sp.dma_start(c_in[:], ctx[s].rearrange("(c p) d -> p c d", p=KP)).then_inc(ctx_dma, 16)
                sp.dma_start(m_in[:], mask[s:s + 1, :].to_broadcast([P, SK])).then_inc(mask_dma, 16)

            load_batch(0)
            sp.dma_start(gw[:], gate_w.rearrange("(k p) e -> p k e", p=P)).then_inc(small_dma, 16)
            sp.dma_start(gbias[:], bias.rearrange("(a e) -> a e", a=1).to_broadcast([P, E])).then_inc(small_dma, 16)
            sp.dma_start(wsgu[:, :, 0, :], ws_gate.rearrange("(k p) f -> p k f", p=P)).then_inc(small_dma, 16)
            sp.dma_start(wsgu[:, :, 1, :], ws_up.rearrange("(k p) f -> p k f", p=P)).then_inc(small_dma, 16)
            sp.dma_start(wsd[:], ws_down).then_inc(small_dma, 16)
            load_batch(1)

            def load_experts(g):
                e = slice(GE * g, GE * (g + 1))
                s = ew_dma[g % 2]
                sp.dma_start(w_gu[:, g % 2, 0], w_gate[e].rearrange("e (p k) f -> p e (k f)", k=CC)).then_inc(s, 16)
                sp.dma_start(w_gu[:, g % 2, 1], w_up[e].rearrange("e (p k) f -> p e (k f)", k=CC)).then_inc(s, 16)
                sp.dma_start(w_dn[0:F, g % 2], w_down[e].rearrange("e f h -> f e h")).then_inc(s, 16)

            sp.wait_ge(scored, 1)
            load_experts(0)
            load_experts(1)
            for b in range(2, B + 1):
                load_batch(b)
            for g in range(2, NG):
                sp.wait_ge(dn_filled, GP * (g - 1))
                load_experts(g)
            sp.wait_ge(ln_out, 3 * NT)
            for k in range(2):
                sp.dma_start(out.rearrange("(j k) n c -> k n j c", k=2)[k],
                             x1[HALF * k:HALF * k + N, :, :]).then_inc(out_dma, 16)
            sp.wait_ge(out_dma, 32)

        @block.gpsimd
        def _(pool):
            steps = [0]

            def chained(ins):
                steps[0] += 1
                ins.then_inc(const_step, 1)
                pool.wait_ge(const_step, steps[0])

            nc.gpsimd.memset(ident[:], 0.0).then_inc(const_step, 1)
            nc.gpsimd.memset(ident16[:], 0.0).then_inc(const_step, 1)
            nc.gpsimd.memset(before[:], 1.0).then_inc(const_step, 1)
            nc.gpsimd.memset(headmask[:], 1.0).then_inc(const_step, 1)
            nc.gpsimd.memset(in_batch[:], 1.0).then_inc(const_step, 1)
            steps[0] = 5
            chained(nc.gpsimd.iota(slots_i[:], pattern=[[1, CAP]], base=0, channel_multiplier=0))
            nc.gpsimd.memset(ones16[:], 1.0).then_inc(consts_set, 1)
            nc.gpsimd.memset(zero16[:], 0.0).then_inc(consts_set, 1)
            for m in (ident, ident16):
                nc.gpsimd.affine_select(out=m[:], in_=m[:], compare_op=ALU.not_equal, fill=1.0, base=0,
                                        pattern=[[-1, P]], channel_multiplier=1).then_inc(consts_set, 1)
            nc.gpsimd.affine_select(out=before[:], in_=before[:], compare_op=ALU.is_gt, fill=0.0, base=0,
                                    pattern=[[1, P]], channel_multiplier=-1).then_inc(consts_set, 1)
            nc.gpsimd.tensor_copy(slots[:], slots_i[:]).then_inc(consts_set, 1)
            chained(nc.gpsimd.affine_select(out=in_batch[:], in_=in_batch[:], compare_op=ALU.is_ge, fill=0.0, base=N - 1,
                                            pattern=[[HALF, 2]], channel_multiplier=-1))
            chained(nc.gpsimd.affine_select(out=in_batch[:], in_=in_batch[:], compare_op=ALU.is_ge, fill=0.0, base=0,
                                            pattern=[[-HALF, 2]], channel_multiplier=1))
            nc.gpsimd.tensor_tensor(valid[:], in_batch[:, 0:1], in_batch[:, 1:2], ALU.add).then_inc(consts_set, 1)
            chained(nc.gpsimd.affine_select(out=headmask[:], in_=headmask[:], compare_op=ALU.is_ge, fill=0.0, base=0,
                                            pattern=[[-HD, HC], [0, VW]], channel_multiplier=1))
            nc.gpsimd.affine_select(out=headmask[:], in_=headmask[:], compare_op=ALU.is_ge, fill=0.0, base=HD - 1,
                                    pattern=[[HD, HC], [0, VW]], channel_multiplier=-1).then_inc(consts_set, 1)

            def split_ctx(b, parity):
                wait_alone(pool, ctx_dma, 16 * (b + 1))
                nc.gpsimd.tensor_copy(c16[:, parity, :, 0, :], c_in[:]).then_inc(ctx_high, 1)
                wait_alone(pool, ctx_high, b + 1)
                nc.gpsimd.tensor_tensor(c16[:, parity, :, 1, :], c_in[:], c16[:, parity, :, 0, :],
                                        ALU.subtract).then_inc(ctx_split, 1)
                wait_alone(pool, mask_dma, 16 * (b + 1))
                nc.gpsimd.tensor_scalar(mb[:, parity, :], m_in[:], BIG, -BIG, ALU.mult, ALU.add).then_inc(mask_bias, 1)

            def stage_q(b, parity):
                for hl in range(2):
                    nc.gpsimd.tensor_copy(q_st[:, parity, hl, :],
                                          Qt[:, hl, bass.ds(b, 1), :].rearrange("p a q -> p (a q)")).then_inc(q_staged, 1)

            split_ctx(0, 0)
            front_wait(pool, "x1T", 1)
            nc.gpsimd.memset(oT, 0.0).then_inc(oT_zero, 1)
            front_wait(pool, "Qt", QH - 1)
            stage_q(0, 0)
            split_ctx(1, 1)
            stage_q(1, 1)

            def pair_body(i):
                for k in range(2):
                    wait_alone(pool, pv_done, PAIR * i + QT * (k + 1))
                    split_ctx(2 * i + 2 + k, k)
                    stage_q(2 * i + 2 + k, k)
            with pool.Fori(0, NT - 1) as i:
                pair_body(i)
            pool.wait_ge(pv_done, PAIR * (NT - 1) + QT)
            split_ctx(B, 0)

        @block.tensor
        def _(pe):
            pe.wait_ge(consts_set, 8)

            def fill(name, i=0):
                f = front.at(name, i)
                if f >= 8:
                    g = f - 8
                    if front.takes("v", g):
                        pe.wait_ge(emptied_v, front.emptied("v", g))
                    if front.takes("a", g):
                        pe.wait_ge(emptied_a, front.emptied("a", g))
                return ps[:, f % 8, :]

            pe.wait_ge(x_in, 32)
            for c in range(CC):
                o = fill("xT", c)
                for j in range(NT):
                    last = nc.tensor.transpose(o[:, P * j:P * (j + 1)], x_sb[:, j, P * c:P * (c + 1)], ident[:])
                last.then_inc(filled, 1)
            pe.wait_ge(wqkv_dma, 16)
            for i in range(4):
                c, half = i // 2, i % 2
                o = fill("wqkvT", i)
                for g in range(3):
                    last = nc.tensor.transpose(o[:, P * g:P * (g + 1)],
                                               wqkv_in[:, 3 * half + g, P * c:P * (c + 1)], ident[:])
                last.then_inc(filled, 1)
            for c in range(CC):
                front_wait(pe, "xT", c)
            for i in range(4):
                front_wait(pe, "wqkvT", i)
            for o_c in range(CC):
                o = fill("qT", o_c)
                for c in range(CC):
                    last = nc.tensor.matmul(o, wqkvT[:, c, P * o_c:P * (o_c + 1)], xT[:, c, :],
                                            start=(c == 0), stop=(c == CC - 1))
                last.then_inc(filled, 1)
            for j in range(NT):
                o = fill("kv", j)
                for c in range(CC):
                    last = nc.tensor.matmul(o, xT[:, c, P * j:P * (j + 1)], wqkvT[:, c, C:3 * C],
                                            start=(c == 0), stop=(c == CC - 1))
                last.then_inc(filled, 1)
            pe.wait_ge(wp_dma, 16)
            o = fill("wpT")
            for c in range(CC):
                for g in range(CC):
                    last = nc.tensor.transpose(o[:, C * c + P * g:C * c + P * (g + 1)],
                                               wp_in[:, g, P * c:P * (c + 1)], ident[:])
            last.then_inc(filled, 1)
            pe.wait_ge(wk_dma, 16)
            for i in range(2):
                o = fill("WkT", i)
                for g in range(4):
                    last = nc.tensor.transpose(o[:, D * g:D * (g + 1)], wk_in[:, 4 * i + g, :], ident[:])
                last.then_inc(filled, 1)
            pe.wait_ge(wq_dma, 16)
            for i in range(8):
                o = fill("WqT", i)
                for n in range(4):
                    h, c = 2 * i + n // 2, n % 2
                    last = nc.tensor.transpose(o[:, P * n:P * (n + 1)], wq_in[:, c, D * h:D * (h + 1)], ident[:])
                last.then_inc(filled, 1)
            for b in range(B):
                front_wait(pe, "kv", b // 2)
                o = fill("G", b)
                r = HALF * (b % 2)
                for c in range(CC):
                    last = nc.tensor.matmul(o[:, HC * VW * c:HC * VW * (c + 1)],
                                            k_sb[r:r + N, b // 2, P * c:P * (c + 1)],
                                            v_aug[r:r + N, b // 2, HC * c:HC * (c + 1), :], start=True, stop=True)
                last.then_inc(filled, 1)
            front_wait(pe, "WkT", 0)
            front_wait(pe, "WkT", 1)
            front_wait(pe, "WqT", 6)
            front_wait(pe, "WqT", 7)
            for i in range(8):
                o = fill("M", i)
                for n in range(4):
                    h, c = 2 * i + n // 2, n % 2
                    last = nc.tensor.matmul(o[:, D * n:D * (n + 1)], wqT[:, h, c, :], wkT[:, h // 2, :],
                                            start=True, stop=True)
                last.then_inc(filled, 1)
            front_wait(pe, "qT", 0)
            front_wait(pe, "qT", 1)
            for j in range(NT):
                o = fill("lin", j)
                for k in range(2):
                    b = 2 * j + k
                    front_wait(pe, "G", b)
                    for c in range(CC):
                        last = nc.tensor.matmul(o[HALF * k:HALF * (k + 1), HC * VW * c:HC * VW * (c + 1)],
                                                qT[:, c, HALF * b:HALF * (b + 1)],
                                                kvm[:, b, HC * VW * c:HC * VW * (c + 1)], start=True, stop=True)
                last.then_inc(filled, 1)
            pe.wait_ge(wv_dma, 16)
            for i in range(2):
                o = fill("WvT", i)
                for g in range(4):
                    last = nc.tensor.transpose(o[:, D * g:D * (g + 1)], wv_in[:, 4 * i + g, :], ident[:])
                last.then_inc(filled, 1)
            pe.wait_ge(ao_ready, 1)
            for c in range(CC):
                o = fill("aoT", c)
                for j in range(NT):
                    last = nc.tensor.transpose(o[:, P * j:P * (j + 1)], ao[:, j, P * c:P * (c + 1)], ident[:])
                last.then_inc(filled, 1)
            front_wait(pe, "wpT")
            front_wait(pe, "aoT", 0)
            front_wait(pe, "aoT", 1)
            for j in range(NT):
                o = fill("proj", j)
                for c in range(CC):
                    last = nc.tensor.matmul(o[:, 0:C], aoT[:, c, P * j:P * (j + 1)], wpT[:, c, :],
                                            start=(c == 0), stop=(c == CC - 1))
                last.then_inc(filled, 1)
            front_wait(pe, "WvT", 0)
            front_wait(pe, "WvT", 1)
            pe.wait_ge(wo_dma, 16)
            for i in range(8):
                o = fill("W2", i)
                for n in range(2):
                    h = 2 * i + n
                    last = nc.tensor.matmul(o[:, C * n:C * (n + 1)], wvT[:, h // 2, :], wo_in[:, h, :],
                                            start=True, stop=True)
                last.then_inc(filled, 1)
            pe.wait_ge(ln_out, NT)
            for c in range(CC):
                o = fill("x1T", c)
                for j in range(NT):
                    last = nc.tensor.transpose(o[:, P * j:P * (j + 1)], x1[:, j, P * c:P * (c + 1)], ident[:])
                last.then_inc(filled, 1)
            front_wait(pe, "M", 6)
            front_wait(pe, "M", 7)
            front_wait(pe, "x1T", 0)
            front_wait(pe, "x1T", 1)
            for h in range(QH):
                o = fill("Qt", h)
                for c in range(CC):
                    last = nc.tensor.matmul(o[:, 0:B * N], M[:, h, c, :],
                                            x1T[:, c, :].rearrange("p (b t) -> p b t", t=HALF)[:, :, 0:N],
                                            start=(c == 0), stop=(c == CC - 1))
                last.then_inc(filled, 1)
            pe.wait_ge(ctx_split, 1)
            def transpose_ctx(o, parity, u):
                for hl in range(2):
                    for t in range(TB):
                        at = 512 * hl + P * t
                        last = nc.tensor.transpose(o[:, at:at + KP], c16[:, parity, TB * u + t, hl, :],
                                                   ident16[0:KP, 0:KP])
                return last

            for u in range(NB):
                transpose_ctx(fill("cT", u).bitcast(F16), 0, u).then_inc(filled, 1)

            score, prob_t, o_bank, misc = ps[:, 0:NB], ps[:, NB:2 * NB], ps[:, 6], ps[:, 7]

            def project(i, o_read):
                pe.wait_ge(oT_copied, PAIR * (i + 1))
                pe.wait_ge(o_norm, o_read)
                if not (isinstance(i, int) and i == 0):
                    pe.wait_ge(pair_sum, i)
                for h in range(QH):
                    last = nc.tensor.matmul(o_bank[:, C:2 * C],
                                            oT.rearrange("p b (t h) -> p (b t) h", h=QH)[:, :, h], W2[:, h, :],
                                            start=(h == 0), stop=(h == QH - 1))
                last.then_inc(proj_done, 1)

            def tile_step(i, j, first=False, parts="STPOC"):
                n = PAIR * i + j
                b, par = 2 * i + j // QT, (j // QT) % 2
                cols = slice(P * (j % QT), P * (j % QT + 1))
                u = j % QT - (QT - NB)
                if "C" in parts and u >= 0:
                    if u == 0:
                        pe.wait_ge(ctx_split, b + 2)
                    if not (first and j < 4):
                        pe.wait_ge(oT_copied, n - 3)
                    transpose_ctx(misc.bitcast(F16), 1 - par, u).then_inc(cT_trans, 1)
                if "S" in parts:
                    if j % QT == 0:
                        pe.wait_ge(q_staged, 2 * (b + 1))
                        pe.wait_ge(cT_copied, NB * (b + 1))
                    for k in range(NB):
                        if not (first and j == 0):
                            pe.wait_ge(masked, NB * (n - 1) + k + 1)
                        keys = slice(KB * k, KB * (k + 1))
                        o = score[:, k, 0:KB]
                        nc.tensor.matmul(o, q_st[:, par, 0, cols], cT[:, par, 0, keys], start=True, stop=False)
                        nc.tensor.matmul(o, q_st[:, par, 0, cols], cT[:, par, 1, keys], start=False, stop=False)
                        nc.tensor.matmul(o, q_st[:, par, 1, cols], cT[:, par, 0, keys],
                                         start=False, stop=True).then_inc(scored, 1)
                if "T" in parts and not (first and j < 1):
                    pe.wait_ge(exp_done, n)
                    for k in range(NB):
                        if not (first and j < 2):
                            pe.wait_ge(p_high, NB * (n - 2) + k + 1)
                            pe.wait_ge(p_low, NB * (n - 2) + k + 1)
                        for t in range(TB):
                            kt = TB * k + t
                            last = nc.tensor.transpose(prob_t[0:KP, k, P * t:P * (t + 1)],
                                                       sc[:, (j - 1) % 2, KP * kt:KP * (kt + 1)], ident[:])
                        last.then_inc(p_trans, 1)
                if "P" in parts and not (first and j < 2):
                    if not (first and j < 3):
                        pe.wait_ge(o_norm, n - 2)
                        if j == 4 and not first:
                            pe.wait_ge(pair_sum, i)
                    pe.wait_ge(p_high, NB * (n - 1))
                    pe.wait_ge(p_low, NB * (n - 1))
                    cp = ((j - 2) // QT) % 2
                    for kt in range(KT):
                        for hl in range(2):
                            last = nc.tensor.matmul(
                                o_bank[:, 0:(2 - hl) * D], pT[0:KP, j % 2, hl, P * kt:P * (kt + 1)],
                                c16[:, cp, kt, 0:2 - hl, :], start=(kt == 0 and hl == 0),
                                stop=(kt == KT - 1 and hl == 1))
                    last.then_inc(pv_done, 1)
                if j == 3 and not first and "O" in parts:
                    project(i - 1, n - 1)
                if "O" in parts and not (first and j < 3):
                    pe.wait_ge(o_norm, n - 2)
                    if not (first and j < 4):
                        pe.wait_ge(oT_copied, n - 3)
                    if "C" in parts and u >= 0:
                        pe.wait_ge(cT_copied, NB * (b + 1) + u + 1)
                    nc.tensor.transpose(misc[:, 0:P], on[:, (j - 3) % 2, :], ident[:]).then_inc(o_trans, 1)

            for u in range(NB):
                front_wait(pe, "cT", u)
            front_wait(pe, "Qt", QH - 1)
            for j in range(PAIR):
                tile_step(0, j, first=True)
            with pe.Fori(1, NT) as i:
                for j in range(PAIR):
                    tile_step(i, j)
            for j, parts in ((0, "TPO"), (1, "PO"), (2, "O")):
                tile_step(NT, j, parts=parts)
            project(NT - 1, TILES)

            def fill2(name, i=0):
                f = mid.at(name, i)
                if f >= 8:
                    g = f - 8
                    if mid.takes("v", g):
                        pe.wait_ge(emptied2_v, mid.emptied("v", g))
                    if mid.takes("a", g):
                        pe.wait_ge(emptied2_a, mid.emptied("a", g))
                return ps[:, f % 8, :]

            pe.wait_ge(ln_out, 2 * NT)
            for c in range(CC):
                o = fill2("x2T", c)
                for j in range(NT):
                    last = nc.tensor.transpose(o[:, P * j:P * (j + 1)], x1[:, j, P * c:P * (c + 1)], ident[:])
                last.then_inc(filled2, 1)
            pe.wait_ge(small_dma, 16 * 5)
            mid_wait(pe, "x2T", 0)
            mid_wait(pe, "x2T", 1)
            o = fill2("logit")
            for j in range(NT):
                for c in range(CC):
                    last = nc.tensor.matmul(o[:, E * j:E * (j + 1)], x1T[:, c, P * j:P * (j + 1)], gw[:, c, :],
                                            start=(c == 0), stop=(c == CC - 1))
            last.then_inc(filled2, 1)
            for j in range(NT):
                o = fill2("shgu", j)
                for c in range(CC):
                    last = nc.tensor.matmul(o[:, 0:2 * F], x1T[:, c, P * j:P * (j + 1)], wsgu[:, c, :, :],
                                            start=(c == 0), stop=(c == CC - 1))
                last.then_inc(filled2, 1)
            o = fill2("shT")
            mid_wait(pe, "shgu", NT - 1)
            for j in range(NT):
                last = nc.tensor.transpose(o[0:F, P * j:P * (j + 1)], sh_h[:, j, :], ident[:])
            last.then_inc(filled2, 1)
            mid_wait(pe, "shT")
            for j in range(NT):
                o = fill2("shy", j)
                last = nc.tensor.matmul(o[:, 0:C], sh_hT[:, P * j:P * (j + 1)], wsd[:], start=True, stop=True)
                last.then_inc(filled2, 1)
            pe.wait_ge(routed, 1)
            o = fill2("pos")
            for j in range(NT):
                for k in range(j + 1):
                    last = nc.tensor.matmul(o[:, E * j:E * (j + 1)], (before if k == j else ones16)[:],
                                            sel16[:, k, :], start=(k == 0), stop=(k == j))
            last.then_inc(filled2, 1)

            mid_wait(pe, "pos")
            mid_wait(pe, "shy", NT - 1)
            y_acc, xs_bank, gu_bank, misc2, dn_bank, dT_bank = ps[:, 0:2], ps[:, 2], ps[:, 3:5], ps[:, 5], ps[:, 6], ps[:, 7]
            for c in range(CC):
                nc.tensor.matmul(y_acc[:, c, :], zero16[:, 0:P], zero16[:], start=True, stop=False,
                                 skip_group_check=True)

            def dispatch(g, par, c, first):
                if c == 0:
                    pe.wait_ge(disp_built, g + 1)
                    if not first:
                        pe.wait_ge(xs_v, g)
                else:
                    pe.wait_ge(xs_a, g + 1)
                for j in range(NT):
                    for hl in range(2):
                        last = nc.tensor.matmul(xs_bank[:, 0:GE * CAP], x2h[:, hl, j, c, :],
                                                disp[:, par, j, :, 0:CAP], start=(j == 0 and hl == 0),
                                                stop=(j == NT - 1 and hl == 1))
                last.then_inc(xs_filled, 1)

            def slot_weights(g, par, first, n):
                if not first:
                    pe.wait_ge(hT_copied, n)
                for q in range(GP):
                    for j in range(NT):
                        last = nc.tensor.matmul(misc2[:, C + 4 * q:C + 4 * (q + 1)],
                                                disp[:, par, j, 2 * q:2 * q + 2, :].rearrange("p e s -> p (e s)"),
                                                w_grp[:, par, j, 2 * q:2 * q + 2, :].rearrange("p e s -> p (e s)"),
                                                start=(j == 0), stop=(j == NT - 1))
                last.then_inc(w_filled, 1)

            def pair_step(i, q, first=False, parts="DGTCN"):
                n = 2 * GP * i + q
                g, par, gq = 2 * i + q // GP, (q // GP) % 2, q % GP
                if "G" in parts:
                    if not (first and q < 1):
                        pe.wait_ge(dT_copied, n)
                    o = dT_bank.bitcast(F16)[:, 512 * (q % 2):512 * (q % 2 + 1)]
                    for j in range(NT):
                        last = nc.tensor.transpose(o[:, P * j:P * (j + 1)],
                                                   disp[:, par, j, 2 * gq:2 * gq + 2, :].rearrange("p e s -> p (e s)"),
                                                   ident16[:])
                    last.then_inc(dT_filled, 1)
                    if gq == 0:
                        pe.wait_ge(xs_a, g + 1)
                        pe.wait_ge(xs_v, g + 1)
                        pe.wait_ge(ew_dma[par], 48 * (i + 1))
                    if not (first and q < 2):
                        pe.wait_ge(h_ready, n - 1)
                    for c in range(CC):
                        for s in range(2):
                            e = 2 * gq + s
                            last = nc.tensor.matmul(gu_bank[SLOT * s:SLOT * (s + 1), q % 2, 0:2 * F],
                                                    xs[:, par, c, e, :], w_gu[:, par, :, e, F * c:F * (c + 1)],
                                                    start=(c == 0), stop=(c == CC - 1))
                    last.then_inc(gu_filled, 1)
                if "T" in parts and not (first and q < 1):
                    pe.wait_ge(h_ready, n)
                    if not (first and q < 2):
                        pe.wait_ge(hT_copied, n - 1)
                    if (q - 1) % GP == 2:
                        pe.wait_ge(w_copied, 2 * i + (q - 1) // GP + 2)
                    nc.tensor.transpose(misc2[0:F, 0:P], h_sb[:, (q - 1) % 2, :], ident[:]).then_inc(hT_filled, 1)
                if "C" in parts and not (first and q < 2):
                    pe.wait_ge(o_high, n - 1)
                    pe.wait_ge(o_low, n - 1)
                    pe.wait_ge(dT_copied, n - 1)
                    for c in range(CC):
                        for hl in range(2):
                            last = nc.tensor.matmul(y_acc[:, c, :], o_hl[:, q % 2, hl, P * c:P * (c + 1)],
                                                    dispT[:, (q - 2) % GP, :], start=False, stop=False,
                                                    skip_group_check=True)
                    last.then_inc(comb_done, 1)
                if "N" in parts and not (first and q < 1):
                    pe.wait_ge(hT_copied, n)
                    if not (first and q < 2):
                        pe.wait_ge(o_high, n - 1)
                        pe.wait_ge(o_low, n - 1)
                    dq, dp = (q - 1) % GP, ((q - 1) // GP) % 2
                    for s in range(2):
                        last = nc.tensor.matmul(dn_bank[SLOT * s:SLOT * (s + 1), 0:C],
                                                hT[:, (q - 1) % 2, SLOT * s:SLOT * (s + 1)],
                                                w_dn[0:F, dp, 2 * dq + s, :], start=True, stop=True)
                    last.then_inc(dn_filled, 1)
                if "D" in parts and gq == 1:
                    dispatch(g + 1, 1 - par, 0, False)
                if "D" in parts and gq == 2:
                    dispatch(g + 1, 1 - par, 1, False)
                    slot_weights(g + 1, 1 - par, False, n)

            dispatch(0, 0, 0, True)
            dispatch(0, 0, 1, True)
            slot_weights(0, 0, True, 0)
            pe.wait_ge(w_copied, 1)
            for q in range(2 * GP):
                pair_step(0, q, first=True)
            with pe.Fori(1, NG // 2) as i:
                for q in range(2 * GP):
                    pair_step(i, q)
            pair_step(NG // 2, 0, parts="TCN")
            pair_step(NG // 2, 1, parts="C")
            for c in range(CC):
                nc.tensor.matmul(y_acc[:, c, :], zero16[:, 0:P], zero16[:], start=False, stop=True,
                                 skip_group_check=True).then_inc(y_filled, 1)
            pe.wait_ge(y_copied, 1)
            pe.wait_ge(y_copied_a, 1)
            for j in range(NT):
                for c in range(CC):
                    last = nc.tensor.transpose(ps[:, 2 + j // 2, C * (j % 2) + P * c:C * (j % 2) + P * (c + 1)],
                                               yT_sb[:, c, P * j:P * (j + 1)], ident[:])
            last.then_inc(yb_filled, 1)

        @block.scalar
        def _(act):
            def take(name, i=0):
                f = front.at(name, i)
                act.wait_ge(filled, f + 1)
                return ps[:, f % 8, :]

            def mine(name):
                return [i for i in range(dict((p[0], p[1]) for p in FRONT)[name]) if front.takes("a", front.at(name, i))]

            def std(k):
                act.wait_ge(ln_var, k)
                nc.scalar.activation(sd[:], ve[:], ACT.Sqrt).then_inc(ln_std, 1)

            for c in mine("xT"):
                nc.scalar.copy(xT[:, c, :], take("xT", c)).then_inc(emptied_a, 1)
            for i in mine("wqkvT"):
                nc.scalar.copy(wqkvT[:, i // 2, 384 * (i % 2):384 * (i % 2 + 1)],
                               take("wqkvT", i)[:, 0:384]).then_inc(emptied_a, 1)
            for c in mine("qT"):
                nc.scalar.activation(qT[:, c, :], take("qT", c), ACT.Relu).then_inc(emptied_a, 1)
            for j in mine("kv"):
                nc.scalar.copy(v_aug[:, j, :, 0:HD],
                               take("kv", j)[:, C:2 * C].rearrange("p (h d) -> p h d", d=HD)).then_inc(emptied_a, 1)
            nc.scalar.copy(wpT[:].rearrange("p a b -> p (a b)"), take("wpT")).then_inc(emptied_a, 1)
            for i in mine("WkT"):
                nc.scalar.copy(wkT[:, 4 * i:4 * i + 4, :].rearrange("p a b -> p (a b)"),
                               take("WkT", i)).then_inc(emptied_a, 1)
            for i in mine("WqT"):
                nc.scalar.copy(wqT[:, 2 * i:2 * i + 2].rearrange("p a b c -> p (a b c)"),
                               take("WqT", i)).then_inc(emptied_a, 1)
            for i in mine("M"):
                nc.scalar.mul(M[:, 2 * i:2 * i + 2].rearrange("p a b c -> p (a b c)"), take("M", i),
                              D ** -0.5).then_inc(emptied_a, 1)
            for i in mine("WvT"):
                nc.scalar.copy(wvT[:, 4 * i:4 * i + 4, :].rearrange("p a b -> p (a b)"),
                               take("WvT", i)).then_inc(emptied_a, 1)
            for c in mine("aoT"):
                nc.scalar.copy(aoT[:, c, :], take("aoT", c)).then_inc(emptied_a, 1)
            for i in mine("W2"):
                nc.scalar.copy(W2[:, 2 * i:2 * i + 2, :].rearrange("p a b -> p (a b)"),
                               take("W2", i)).then_inc(emptied_a, 1)
            std(1)
            for c in mine("x1T"):
                nc.scalar.copy(x1T[:, c, :], take("x1T", c)).then_inc(emptied_a, 1)
            for h in range(QH):
                nc.scalar.copy(Qt[:, 0].rearrange("p b (t h) -> p b t h", h=QH)[:, :, :, h],
                               take("Qt", h)[:, 0:B * N].rearrange("p (b t) -> p b t", t=N)).then_inc(emptied_a, 1)

            def copy_cT(dst_par, u, bank16):
                return nc.scalar.copy(
                    cT[:, dst_par, :, KB * u:KB * (u + 1)].rearrange("p s (t k) -> p s t k", k=KP),
                    bank16.rearrange("p (s t k) -> p s t k", s=2, k=P)[:, :, :, 0:KP])

            for u in mine("cT"):
                copy_cT(0, u, take("cT", u).bitcast(F16)).then_inc(emptied_a, 1)

            prob_t, o_bank, misc = ps[:, NB:2 * NB], ps[:, 6], ps[:, 7]

            def tile_step(i, j, first=False, parts="HEOC"):
                n = PAIR * i + j
                b = 2 * i + j // QT
                u = j % QT - (QT - NB)
                if "C" in parts and u >= 0:
                    act.wait_ge(cT_trans, NB * b + u + 1)
                    copy_cT((j // QT + 1) % 2, u, misc.bitcast(F16)).then_inc(cT_copied, 1)
                if "H" in parts and not (first and j < 1):
                    if not (first and j < 3):
                        act.wait_ge(pv_done, n - 2)
                    for k in range(NB):
                        act.wait_ge(p_trans, NB * (n - 1) + k + 1)
                        nc.scalar.copy(pT[0:KP, (j - 1) % 2, 0, 512 * k:512 * (k + 1)],
                                       prob_t[0:KP, k, :]).then_inc(p_high, 1)
                if "E" in parts:
                    act.wait_ge(bias_ready, n + 1)
                    if not (first and j < 2):
                        act.wait_ge(recip_ready, n - 1)
                    nc.scalar.activation(sc[:, j % 2, :], sc[:, j % 2, :], ACT.Exp, bias=nb[:, j % 2:j % 2 + 1],
                                         accum_out=rs[:, j % 2:j % 2 + 1]).then_inc(exp_done, 1)
                if "O" in parts and not (first and j < 2):
                    act.wait_ge(recip_ready, n - 1)
                    if not (first and j < 4):
                        act.wait_ge(o_norm, n - 3)
                    act.wait_ge(pv_done, n - 1)
                    nc.scalar.activation(o2[:, j % 2, :], o_bank[:, D:2 * D], ACT.Copy,
                                         scale=rr[:, j % 2:j % 2 + 1]).then_inc(o2_done, 1)
                if "O" in parts or "X" in parts:
                    if not (first and j < 3):
                        if first and j == 3:
                            act.wait_ge(oT_zero, 1)
                        if j == 3 and not first:
                            act.wait_ge(proj_done, i)
                        act.wait_ge(o_trans, n - 2)
                        m = (j - 3) % PAIR
                        nc.scalar.copy(oT[:, m // QT, P * (m % QT):P * (m % QT + 1)], misc[:, 0:P]).then_inc(oT_copied, 1)

            for u in range(NB):
                front_wait(act, "cT", u)
            nc.scalar.sem_inc(cT_copied, NB)
            for j in range(PAIR):
                tile_step(0, j, first=True)
            with act.Fori(1, NT) as i:
                for j in range(PAIR):
                    tile_step(i, j)
            tile_step(NT, 0, parts="HO")
            tile_step(NT, 1, parts="O")
            tile_step(NT, 2, parts="X")
            std(2)

            def take2(name, i=0):
                f = mid.at(name, i)
                act.wait_ge(filled2, f + 1)
                return ps[:, f % 8, :]

            nc.scalar.copy(x1T[:, 1, :], take2("x2T", 1)).then_inc(emptied2_a, 1)
            nc.scalar.activation(r1[:].rearrange("p a b -> p (a b)"), take2("logit")[:, 0:NT * E],
                                 ACT.Sigmoid).then_inc(emptied2_a, 1)
            for j in range(NT):
                if j >= 2:
                    act.wait_ge(sh_done, j - 1)
                nc.scalar.activation(sh_g[:, j % 2, :], take2("shgu", j)[:, 0:F], ACT.Silu).then_inc(emptied2_a, 1)

            gu_bank, xs_bank, dn_bank = ps[:, 3:5], ps[:, 2], ps[:, 6]

            def move_rows(g, par):
                act.wait_ge(xs_filled, 2 * g + 1)
                nc.scalar.copy(xs[:, par, 0, :, 0:CAP],
                               xs_bank[:, 0:GE * CAP].rearrange("p (e s) -> p e s", s=CAP)).then_inc(xs_a, 1)

            def pair_step(i, q, first=False, parts="GND"):
                n = 2 * GP * i + q
                if "G" in parts:
                    act.wait_ge(gu_filled, n + 1)
                    if not (first and q < 2):
                        act.wait_ge(h_ready, n - 1)
                    nc.scalar.activation(act_g[:, q % 2, :], gu_bank[:, q % 2, 0:F],
                                         ACT.Silu).then_inc(silu_done, 1)
                if "N" in parts and not (first and q < 1):
                    g1, dq = 2 * i + (q - 1) // GP, (q - 1) % GP
                    act.wait_ge(dn_filled, n)
                    act.wait_ge(w_copied, g1 + 1)
                    if not (first and q < 3):
                        act.wait_ge(comb_done, n - 2)
                    nc.scalar.activation(o_hl[:, (q - 1) % 2, 0, :], dn_bank[:, 0:C], ACT.Copy,
                                         scale=ws_slot[:, g1_par(q), dq:dq + 1]).then_inc(o_high, 1)
                if "D" in parts and q % GP == 1:
                    move_rows(2 * i + q // GP + 1, (q // GP + 1) % 2)

            def g1_par(q):
                return ((q - 1) // GP) % 2

            act.wait_ge(routed, 2)
            move_rows(0, 0)
            for q in range(2 * GP):
                pair_step(0, q, first=True)
            with act.Fori(1, NG // 2) as i:
                for q in range(2 * GP):
                    pair_step(i, q)
            pair_step(NG // 2, 0, parts="N")
            act.wait_ge(y_filled, 2)
            nc.scalar.copy(yT_sb[:, 0, :], ps[:, 0, :]).then_inc(y_copied_a, 1)
            std(3)

        @block.vector
        def _(dve):
            steps = [0]

            def chained(ins):
                steps[0] += 1
                ins.then_inc(dve_step, 1)
                dve.wait_ge(dve_step, steps[0])

            def take(name, i=0):
                f = front.at(name, i)
                dve.wait_ge(filled, f + 1)
                return ps[:, f % 8, :]

            def mine(name):
                return [i for i in range(dict((p[0], p[1]) for p in FRONT)[name]) if front.takes("v", front.at(name, i))]

            def norm(src, dst, k):
                for j in range(NT):
                    last = nc.vector.bn_stats(st[:, j, :], src[:, j, :])
                chained(last)
                for j in range(NT):
                    last = nc.vector.bn_aggr(mv[:, j, :], st[:, j, :])
                chained(last)
                nc.vector.tensor_scalar(ve[:], mv[:, :, 1], LN_EPS, None, ALU.add).then_inc(ln_var, 1)
                dve.wait_ge(ln_std, k)
                chained(nc.vector.reciprocal(rstd[:], sd[:]))
                for j in range(NT):
                    nc.vector.tensor_scalar(dst[:, j, :], src[:, j, :], mv[:, j, 0:1], rstd[:, j:j + 1],
                                            ALU.subtract, ALU.mult).then_inc(ln_out, 1)

            chained(nc.vector.memset(x_sb[32:64, :, :], 0.0))
            nc.vector.memset(x_sb[96:128, :, :], 0.0).then_inc(pads_zero, 1)
            nc.vector.memset(v_aug[:, :, :, HD:VW], 1.0).then_inc(dve_const, 1)

            for c in mine("xT"):
                nc.vector.tensor_copy(xT[:, c, :], take("xT", c)).then_inc(emptied_v, 1)
            for i in mine("wqkvT"):
                nc.vector.tensor_copy(wqkvT[:, i // 2, 384 * (i % 2):384 * (i % 2 + 1)],
                                      take("wqkvT", i)[:, 0:384]).then_inc(emptied_v, 1)
            for c in mine("qT"):
                nc.vector.tensor_scalar(qT[:, c, :], take("qT", c), 0.0, None, ALU.max).then_inc(emptied_v, 1)
            dve.wait_ge(dve_const, 1)
            for j in mine("kv"):
                o = take("kv", j)
                dve.wait_ge(emptied_a, front.emptied("a", front.at("kv", j)))
                nc.vector.tensor_scalar(k_sb[:, j, :], o[:, 0:C], 0.0, None, ALU.max).then_inc(emptied_v, 1)
            for i in mine("WkT"):
                nc.vector.tensor_copy(wkT[:, 4 * i:4 * i + 4, :].rearrange("p a b -> p (a b)"),
                                      take("WkT", i)).then_inc(emptied_v, 1)
            for i in mine("WqT"):
                nc.vector.tensor_copy(wqT[:, 2 * i:2 * i + 2].rearrange("p a b c -> p (a b c)"),
                                      take("WqT", i)).then_inc(emptied_v, 1)
            dve.wait_ge(consts_set, 8)
            for b in range(B):
                w = HC * VW
                nc.vector.tensor_tensor(kvm[:, b, :].rearrange("p (c w) -> p c w", w=w),
                                        take("G", b)[:, 0:CC * w].rearrange("p (c w) -> p c w", w=w),
                                        headmask[:].rearrange("p h v -> p (h v)").unsqueeze(1).to_broadcast([P, CC, w]),
                                        ALU.mult).then_inc(emptied_v, 1)
            for i in mine("M"):
                nc.vector.tensor_scalar(M[:, 2 * i:2 * i + 2].rearrange("p a b c -> p (a b c)"), take("M", i),
                                        D ** -0.5, None, ALU.mult).then_inc(emptied_v, 1)
            dve.wait_ge(bproj_dma, 16)
            chained(nc.vector.tensor_tensor(x_sb[:], x_sb[:], bproj[:].unsqueeze(1).to_broadcast([P, NT, C]), ALU.add))
            for j in range(NT):
                o = take("lin", j)[:, 0:LH * VW].rearrange("p (h v) -> p h v", v=VW)
                chained(nc.vector.tensor_scalar(den[:, j, :], o[:, :, HD], DEN_EPS, None, ALU.add))
                chained(nc.vector.reciprocal(den[:, NT + j, :], den[:, j, :]))
                last = nc.vector.tensor_tensor(ao[:, j, :].rearrange("p (h d) -> p h d", d=HD), o[:, :, 0:HD],
                                               den[:, NT + j, :].unsqueeze(2).to_broadcast([P, LH, HD]), ALU.mult)
                last.then_inc(emptied_v, 1)
            dve.wait_ge(emptied_v, front.emptied("v", front.at("lin", NT - 1)))
            nc.vector.sem_inc(ao_ready, 1)
            for c in mine("aoT"):
                nc.vector.tensor_copy(aoT[:, c, :], take("aoT", c)).then_inc(emptied_v, 1)
            for j in range(NT):
                last = nc.vector.tensor_tensor(x_sb[:, j, :], x_sb[:, j, :], take("proj", j)[:, 0:C], ALU.add)
                last.then_inc(emptied_v, 1)
            dve.wait_ge(emptied_v, front.emptied("v", front.at("proj", NT - 1)))
            norm(x_sb, x1, 1)
            for i in mine("W2"):
                nc.vector.tensor_copy(W2[:, 2 * i:2 * i + 2, :].rearrange("p a b -> p (a b)"),
                                      take("W2", i)).then_inc(emptied_v, 1)
            for c in mine("x1T"):
                nc.vector.tensor_copy(x1T[:, c, :], take("x1T", c)).then_inc(emptied_v, 1)
            for h in range(QH):
                o = take("Qt", h)[:, 0:B * N].rearrange("p (b t) -> p b t", t=N)
                dve.wait_ge(emptied_a, front.emptied("a", front.at("Qt", h)))
                hi, lo = (Qt[:, s].rearrange("p b (t h) -> p b t h", h=QH)[:, :, :, h] for s in range(2))
                nc.vector.tensor_tensor(lo, o, hi, ALU.subtract).then_inc(emptied_v, 1)
            for u in mine("cT"):
                nc.vector.tensor_copy(
                    cT[:, 0, :, KB * u:KB * (u + 1)].rearrange("p s (t k) -> p s t k", k=KP),
                    take("cT", u).bitcast(F16).rearrange("p (s t k) -> p s t k", s=2, k=P)[:, :, :, 0:KP]
                ).then_inc(emptied_v, 1)

            score, prob_t, o_bank = ps[:, 0:NB], ps[:, NB:2 * NB], ps[:, 6]

            def tile_step(i, j, first=False, parts="SRLO"):
                n = PAIR * i + j
                b, par, tp = 2 * i + j // QT, (j // QT) % 2, j % 2
                if "S" in parts:
                    if j % QT == 0:
                        wait_alone(dve, mask_bias, b + 1)
                    if not (first and j < 2):
                        wait_alone(dve, p_trans, NB * (n - 1))
                    for k in range(NB):
                        keys = slice(KB * k, KB * (k + 1))
                        wait_alone(dve, scored, NB * n + k + 1)
                        nc.vector.tensor_tensor_reduce(out=sc[:, tp, keys], in0=score[:, k, 0:KB], in1=mb[:, par, keys],
                                                       scale=1.0, scalar=-3e38, op0=ALU.add, op1=ALU.max,
                                                       accum_out=mx3[:, tp, k:k + 1]).then_inc(masked, 1)
                    dve.wait_ge(masked, NB * (n + 1))
                    nc.vector.tensor_reduce(mxa[:, tp:tp + 1], mx3[:, tp, :], AX.X, ALU.max).then_inc(row_max, 1)
                    dve.wait_ge(row_max, n + 1)
                    nc.vector.tensor_scalar(nb[:, tp:tp + 1], mxa[:, tp:tp + 1], -1.0, LOG_P,
                                            ALU.mult, ALU.add).then_inc(bias_ready, 1)
                if "R" in parts and not (first and j < 1):
                    op = (j - 1) % 2
                    dve.wait_ge(exp_done, n)
                    nc.vector.reciprocal(rinv[:, op:op + 1], rs[:, op:op + 1]).then_inc(recip1, 1)
                    dve.wait_ge(recip1, n)
                    nc.vector.scalar_tensor_tensor(rr[:, op:op + 1], mxa[:, op:op + 1], -0.5 * BIG, rinv[:, op:op + 1],
                                                   ALU.is_gt, ALU.mult).then_inc(recip_ready, 1)
                if "L" in parts and not (first and j < 1):
                    if not (first and j < 3):
                        dve.wait_ge(pv_done, n - 2)
                    for k in range(NB):
                        part = slice(512 * k, 512 * (k + 1))
                        dve.wait_ge(p_high, NB * (n - 1) + k + 1)
                        nc.vector.tensor_tensor(pT[0:KP, (j - 1) % 2, 1, part], prob_t[0:KP, k, :],
                                                pT[0:KP, (j - 1) % 2, 0, part], ALU.subtract).then_inc(p_low, 1)
                if "O" in parts and not (first and j < 2):
                    dve.wait_ge(o2_done, n - 1)
                    if not (first and j < 4):
                        dve.wait_ge(o_trans, n - 3)
                    nc.vector.scalar_tensor_tensor(on[:, tp, :], o_bank[:, 0:D], rr[:, tp:tp + 1], o2[:, tp, :],
                                                   ALU.mult, ALU.add).then_inc(o_norm, 1)
                if j == 3 and not first and "S" in parts:
                    add_pair(i - 1)

            def add_pair(i):
                dve.wait_ge(proj_done, i + 1)
                nc.vector.tensor_tensor(x_sb[:, bass.ds(i, 1), :].rearrange("p a c -> p (a c)"), o_bank[:, C:2 * C],
                                        x1[:, bass.ds(i, 1), :].rearrange("p a c -> p (a c)"), ALU.add).then_inc(pair_sum, 1)

            for j in range(PAIR):
                tile_step(0, j, first=True)
            with dve.Fori(1, NT) as i:
                for j in range(PAIR):
                    tile_step(i, j)
            tile_step(NT, 0, parts="RLO")
            tile_step(NT, 1, parts="O")
            add_pair(NT - 1)
            dve.wait_ge(pair_sum, NT)
            norm(x_sb, x1, 2)
            dve.wait_ge(ln_out, 2 * NT)

            def take2(name, i=0):
                f = mid.at(name, i)
                dve.wait_ge(filled2, f + 1)
                return ps[:, f % 8, :]

            nc.vector.tensor_copy(x1T[:, 0, :], take2("x2T", 0)).then_inc(emptied2_v, 1)
            x2v = x1[:].rearrange("p j (m k) -> p j k m", k=CC)
            for j in range(NT):
                last = nc.vector.tensor_copy(x2h[:, 0, j], x2v[:, j])
            chained(last)
            for j in range(NT):
                nc.vector.tensor_tensor(x2h[:, 1, j], x2v[:, j], x2h[:, 0, j], ALU.subtract).then_inc(x2_split, 1)

            mid_wait(dve, "logit")
            dve.wait_ge(small_dma, 16 * 5)
            chained(nc.vector.tensor_tensor(r2[:], r1[:], gbias[:].unsqueeze(1).to_broadcast([P, NT, E]), ALU.add))
            for j in range(NT):
                for g in range(G):
                    last = nc.vector.max(m8[:, G * j + g, :], r2[:, j, EG * g:EG * (g + 1)])
            nc.vector.memset(gs[:, :, G:G + KG], -2 * BIG)
            nc.vector.memset(t8[:], -2 * BIG)
            nc.vector.memset(t6[:], -2 * BIG)
            chained(nc.vector.memset(r3[:, :, E:E + 2], -2 * BIG))
            chained(nc.vector.tensor_tensor(gs[:, :, 0:G], m8[:, :, 0].rearrange("p (j g) -> p j g", g=G),
                                            m8[:, :, 1].rearrange("p (j g) -> p j g", g=G), ALU.add))
            for j in range(NT):
                last = nc.vector.max(m8[:, j, :], gs[:, j, 0:G])
            chained(last)
            chained(nc.vector.tensor_copy(t8[:, :, 0:KG], m8[:, 0:NT, 0:KG]))
            for j in range(NT):
                last = nc.vector.match_replace(gsr[:, j, :], t8[:, j, :], gs[:, j, :], -3 * BIG)
            chained(last)
            chained(nc.vector.tensor_tensor(gsel[:], gs[:, :, 0:G], gsr[:, :, 0:G], ALU.not_equal))
            chained(nc.vector.tensor_scalar(gpen[:], gsel[:], BIG, -BIG, ALU.mult, ALU.add))
            for j in range(NT):
                last = nc.vector.tensor_tensor(r3[:, j, 0:E].rearrange("p (g e) -> p g e", e=EG),
                                               r2[:, j, :].rearrange("p (g e) -> p g e", e=EG),
                                               gsel[:, j, :].unsqueeze(2).to_broadcast([P, G, EG]), ALU.mult)
            chained(last)
            for j in range(NT):
                last = nc.vector.tensor_tensor(r3[:, j, 0:E].rearrange("p (g e) -> p g e", e=EG),
                                               r3[:, j, 0:E].rearrange("p (g e) -> p g e", e=EG),
                                               gpen[:, j, :].unsqueeze(2).to_broadcast([P, G, EG]), ALU.add)
            chained(last)
            for j in range(NT):
                last = nc.vector.max(m8[:, NT + j, :], r3[:, j, 0:E])
            chained(last)
            chained(nc.vector.tensor_copy(t6[:, :, 0:TOPK], m8[:, NT:2 * NT, 0:TOPK]))
            for j in range(NT):
                last = nc.vector.match_replace(r4[:, j, :], t6[:, j, :], r3[:, j, :], -3 * BIG)
            chained(last)
            chained(nc.vector.tensor_tensor(r2[:], r3[:, :, 0:E], r4[:, :, 0:E], ALU.not_equal))
            chained(nc.vector.tensor_tensor(r1[:], r1[:], r2[:], ALU.mult))
            nc.vector.memset(w16[:, :, E:, :], 0.0)
            nc.vector.memset(posm[:, :, E:], 1000.0)
            nc.vector.tensor_scalar(sel16[:], r2[:], valid[:, 0:1], None, ALU.mult).then_inc(routed, 1)
            chained(nc.vector.tensor_reduce(wsum[:], r1[:], AX.X, ALU.add))
            chained(nc.vector.reciprocal(wrec[:], wsum[:]))
            chained(nc.vector.tensor_tensor(r1[:], r1[:], wrec[:].unsqueeze(2).to_broadcast([P, NT, E]), ALU.mult))
            chained(nc.vector.tensor_scalar(r1[:], r1[:], SCALE, None, ALU.mult))
            chained(nc.vector.tensor_copy(w16[:, :, 0:E, 0], r1[:]))
            chained(nc.vector.tensor_tensor(w16[:, :, 0:E, 1], r1[:], w16[:, :, 0:E, 0], ALU.subtract))
            chained(nc.vector.tensor_scalar(r2[:], sel16[:], -1000.0, 1000.0, ALU.mult, ALU.add))

            for j in range(NT):
                o = take2("shgu", j)
                mid_wait(dve, "shgu", j) if False else dve.wait_ge(emptied2_a, mid.emptied("a", mid.at("shgu", j)))
                nc.vector.tensor_tensor(sh_h[:, j, :], sh_g[:, j % 2, :], o[:, F:2 * F], ALU.mult).then_inc(emptied2_v, 1)
                dve.wait_ge(emptied2_v, mid.emptied("v", mid.at("shgu", j)))
                nc.vector.sem_inc(sh_done, 1)
            nc.vector.tensor_copy(sh_hT[:], take2("shT")[0:F, :]).then_inc(emptied2_v, 1)
            for j in range(NT):
                nc.vector.tensor_tensor(x_sb[:, j, :], x1[:, j, :], take2("shy", j)[:, 0:C], ALU.add).then_inc(emptied2_v, 1)
            nc.vector.tensor_tensor(posm[:, :, 0:E], take2("pos")[:, 0:NT * E].rearrange("p (j e) -> p j e", e=E),
                                    r2[:], ALU.add).then_inc(emptied2_v, 1)
            nc.vector.memset(xs[:].rearrange("p a b c d -> p (a b c d)"), 0.0)
            chained(nc.vector.memset(disp[:].rearrange("p a b c d -> p (a b c d)"), 0.0))
            dve.wait_ge(emptied2_v, mid.emptied("v", mid.at("pos")))
            nc.vector.sem_inc(routed, 1)

            xs_bank, gu_bank, misc2, dn_bank, dT_bank = ps[:, 2], ps[:, 3:5], ps[:, 5], ps[:, 6], ps[:, 7]

            def build(g, par):
                for j in range(NT):
                    nc.vector.tensor_tensor(disp[:, par, j, :, 0:CAP],
                                            posm[:, j, bass.ds(GE * g, GE)].unsqueeze(2).to_broadcast([P, GE, CAP]),
                                            slots[:].unsqueeze(1).to_broadcast([P, GE, CAP]), ALU.is_equal)
                nc.vector.tensor_copy(w_grp[:, par], w16[:, :, bass.ds(GE * g, GE), :]).then_inc(disp_built, 1)

            def move_rows(g, par):
                dve.wait_ge(xs_filled, 2 * g + 2)
                nc.vector.tensor_copy(xs[:, par, 1, :, 0:CAP],
                                      xs_bank[:, 0:GE * CAP].rearrange("p (e s) -> p e s", s=CAP)).then_inc(xs_v, 1)
                dve.wait_ge(w_filled, g + 1)
                wv4 = misc2[:, C:C + 4 * GP].rearrange("p (q e s) -> p q e s", e=2, s=2)
                for s in range(2):
                    last = nc.vector.tensor_reduce(ws_slot[SLOT * s:SLOT * (s + 1), par, :],
                                                   wv4[SLOT * s:SLOT * (s + 1), :, s, :], AX.X, ALU.add)
                last.then_inc(w_copied, 1)

            def pair_step(i, q, first=False, parts="BGTND"):
                n = 2 * GP * i + q
                if "B" in parts and q % GP == 0:
                    build(2 * i + q // GP + 1, (q // GP + 1) % 2)
                if "G" in parts:
                    dve.wait_ge(dT_filled, n + 1)
                    if not (first and q < GP):
                        dve.wait_ge(comb_done, n - GP + 1)
                    nc.vector.tensor_copy(dispT[:, q % GP, :],
                                          dT_bank.bitcast(F16)[:, 512 * (q % 2):512 * (q % 2 + 1)]).then_inc(dT_copied, 1)
                    dve.wait_ge(silu_done, n + 1)
                    if not (first and q < 2):
                        dve.wait_ge(hT_filled, n - 1)
                    nc.vector.tensor_tensor(h_sb[:, q % 2, :], act_g[:, q % 2, :],
                                            gu_bank[:, q % 2, F:2 * F], ALU.mult).then_inc(h_ready, 1)
                if "T" in parts and not (first and q < 1):
                    dve.wait_ge(hT_filled, n)
                    if not (first and q < 3):
                        dve.wait_ge(dn_filled, n - 2)
                    nc.vector.tensor_copy(hT[:, (q - 1) % 2, :], misc2[0:F, 0:P]).then_inc(hT_copied, 1)
                if "N" in parts and not (first and q < 1):
                    g1p, dq = ((q - 1) // GP) % 2, (q - 1) % GP
                    dve.wait_ge(o_high, n)
                    nc.vector.scalar_tensor_tensor(o_hl[:, (q - 1) % 2, 1, :], dn_bank[:, 0:C],
                                                   ws_slot[:, g1p, dq:dq + 1], o_hl[:, (q - 1) % 2, 0, :],
                                                   ALU.mult, ALU.subtract).then_inc(o_low, 1)
                if "D" in parts and q % GP == 2:
                    move_rows(2 * i + q // GP + 1, (q // GP + 1) % 2)

            build(0, 0)
            move_rows(0, 0)
            for q in range(2 * GP):
                pair_step(0, q, first=True)
            with dve.Fori(1, NG // 2) as i:
                for q in range(2 * GP):
                    pair_step(i, q)
            pair_step(NG // 2, 0, parts="TN")
            dve.wait_ge(y_filled, 2)
            nc.vector.tensor_copy(yT_sb[:, 1, :], ps[:, 1, :]).then_inc(y_copied, 1)
            dve.wait_ge(yb_filled, 1)
            for j in range(NT):
                last = nc.vector.tensor_tensor(x_sb[:, j, :], x_sb[:, j, :],
                                               ps[:, 2 + j // 2, C * (j % 2):C * (j % 2 + 1)], ALU.add)
            chained(last)
            norm(x_sb, x1, 3)


_INS = ["x", "ctx_1024", "mask_BxS2_bf1", "L0_attn_w_qkv", "L0_attn_w_proj", "L0_attn_b_proj", "L0_xattn_Wq",
        "L0_xattn_Wk", "L0_xattn_Wv", "L0_xattn_Wo", "L0_ffn_gate_w", "L0_ffn_bias", "L0_ffn_w_gate", "L0_ffn_w_up",
        "L0_ffn_w_down", "L0_ffn_ws_gate", "L0_ffn_ws_up", "L0_ffn_ws_down"]


def kernel(**inputs):
    import numpy as np
    import concourse.bacc as bacc
    from concourse.bass_utils import run_bass_kernel_spmd

    nc = bacc.Bacc("TRN2", target_bir_lowering=False, num_devices=1)
    arrays, args = {}, []
    for name in _INS:
        a = np.ascontiguousarray(inputs[name])
        if a.dtype == np.bool_:
            a = a.view(np.uint8)
        arrays[f"in_{name}"] = a
        args.append(nc.dram_tensor(f"in_{name}", a.shape, mybir.dt.from_np(a.dtype), kind="ExternalInput").ap())
    y = nc.dram_tensor("y", (B, N, C), F32, kind="ExternalOutput").ap()
    decoder_kernel(nc, *args, y)
    r = run_bass_kernel_spmd(nc, [arrays], core_ids=[0])
    return r.results[0]["y"]
```

```python
from contextlib import ExitStack

import concourse.bass as bass
from concourse import mybir

F32 = mybir.dt.float32
F16 = mybir.dt.float16
BF16 = mybir.dt.bfloat16
U8 = mybir.dt.uint8
I32 = mybir.dt.int32
ALU = mybir.AluOpType
ACT = mybir.ActivationFunctionType
AX = mybir.AxisListType

P = 128
B, N, C = 8, 56, 256
NT = B // 2
HALF = 64
CC = C // P
HD = 32
LH = C // HD
HC = P // HD
VW = HD + 1
SK, D = 1500, 128
KT, KP = 12, 125
QH, GH = 16, 8
NQ = N * QH
QT = NQ // P
NB = 3
KB = SK // NB
TB = KT // NB
PAIR = 2 * QT
TILES = B * QT
E, TOPK, G, KG, F = 64, 6, 8, 4, 96
EG = E // G
CAP = 48
SLOT = 64
GE = 8
NG = E // GE
GP = GE // 2
PAIRS = E // 2
SCALE = 2.5
LN_EPS, DEN_EPS = 1e-5, 1e-15
BIG = 1e30
LOG_P = 6.931471805599453
M_UP, W_UP = 64.0, 256.0

FRONT = [("wqkvT", 4, "va"), ("xT", 2, "va"), ("qT", 2, "va"), ("kv", 4, "b"), ("wpT", 1, "a"),
         ("WkT", 2, "va"), ("G", 8, "v"), ("WqT", 8, "av"), ("lin", 4, "v"), ("M", 8, "b"),
         ("aoT", 2, "va"), ("WvT", 2, "a"), ("proj", 4, "v"), ("W2", 6, "b"), ("x1T", 2, "b"),
         ("cT", NB, "av"), ("W2", 2, "b"), ("Qt", 16, "b")]
MID = [("x2T", 2, "va"), ("logit", 1, "a"), ("shgu", 4, "a"), ("shT", 1, "a"), ("shy", 2, "a"), ("pos", 1, "v"),
       ("shy", 2, "a")]
EARLY_W2 = range(6)
LATE_W2 = range(6, 8)


class Fills:

    def __init__(self, plan):
        self.where, self.by = {}, []
        for name, n, engines in plan:
            self.where.setdefault(name, []).extend(range(len(self.by), len(self.by) + n))
            self.by += [engines[i % len(engines)] for i in range(n)]

    def at(self, name, i=0):
        return self.where[name][i]

    def emptied(self, engine, f):
        return sum(e in (engine, "b") for e in self.by[:f + 1])

    def takes(self, engine, f):
        return self.by[f] in (engine, "b")


def decoder_kernel(nc, x, ctx, mask, w_qkv, w_proj, b_proj, Wq, Wk, Wv, Wo, gate_w, bias,
                   w_gate, w_up, w_down, ws_gate, ws_up, ws_down, out):
    with ExitStack() as stack:
        def sb(name, shape, dt):
            return stack.enter_context(nc.sbuf_tensor(name, shape, dt))

        def sem(name):
            return stack.enter_context(nc.semaphore(name))

        def carver(region):
            at = [0]

            def carve(shape, dt, size):
                n = 1
                for s in shape:
                    n *= s
                words = (n * size + 3) // 4
                v = region[:, at[0]:at[0] + words]
                at[0] += words
                if dt != F32:
                    v = v.bitcast(dt)
                names = "abcde"[:len(shape)]
                if len(shape) > 1:
                    v = v.rearrange(f"p ({' '.join(names)}) -> p {' '.join(names)}",
                                    **{c: s for c, s in zip(names, shape)})
                return v
            return carve

        ra = sb("ra", [P, 76 * 256], F32)
        cut = carver(ra)
        wq_in = cut([CC, QH * D], F32, 4)
        wqT = cut([QH, CC, P], F32, 4)
        wo_in = cut([QH, C], F32, 4)
        wqkv_in = cut([6, C], F32, 4)
        wqkvT = cut([CC, 3 * C], F32, 4)
        wk_in = cut([GH, D], F32, 4)
        wv_in = cut([GH, D], F32, 4)
        wkT = cut([GH, D], F32, 4)
        wvT = cut([GH, D], F32, 4)
        M = wq_in.bitcast(F16).rearrange("p s (h b c) -> p s h b c", b=CC, c=D)
        cut = carver(ra)
        sc = cut([2, SK], F32, 4)
        pT = cut([2, 2, KT * P], F16, 2)
        w_gu = cut([2, 2, GE, CC * F], F32, 4)
        w_dn = cut([2, GE, C], F32, 4)
        rb = sb("rb", [P, 29 * 256], F32)
        cut = carver(rb)
        qT = cut([CC, NT * P], F32, 4)
        k_sb = cut([NT, C], F32, 4)
        v_aug = cut([NT, LH, VW], F32, 4)
        kvm = cut([B, CC * HC * VW], F32, 4)
        ao = cut([NT, C], F32, 4)
        aoT = cut([CC, NT * P], F32, 4)
        cut = carver(rb)
        cT = cut([2, 2, SK], F16, 2)
        oT = cut([2, 2, HALF * QH], F16, 2)
        q_st = cut([2, 2, NQ], F16, 2)
        rc = sb("rc", [P, 30 * 256], F32)
        cut = carver(rc)
        Qt = cut([2, B, NQ], F16, 2)
        cut = carver(rc)
        x2h = cut([2, NT, CC, P], F16, 2)
        disp = cut([2, NT, GE, SLOT], F16, 2)
        xs = cut([2, CC, GE, SLOT], F32, 4)
        dispT = cut([GP, NT * P], F16, 2)
        w_grp = cut([2, NT, GE, 2], F16, 2)
        ws_slot = cut([2, GP], F32, 4)
        yT_sb = cut([CC, NT * P], F32, 4)
        c_in = sb("c_in", [KP, KT, D], F32)
        c16 = sb("c16", [KP, 2, KT, 2, D], F16)
        m_in = sb("m_in", [P, SK], U8)
        mb = sb("mb", [P, 2, SK], BF16)
        W2 = sb("W2", [P, 2, QH, C], F16)
        x_sb = sb("x_sb", [P, NT, C], F32)
        xT = sb("xT", [P, CC, NT * P], F32)
        x1 = sb("x1", [P, NT, C], F32)
        x1T = sb("x1T", [P, CC, NT * P], F32)
        x1T16 = x1T[:].bitcast(F16).rearrange("p s (a t) -> p s a t", a=CC)
        wp_in = sb("wp_in", [P, CC, C], F32)
        wpT = sb("wpT", [P, CC, C], F32)
        bproj = sb("bproj", [P, C], F32)
        ident = sb("ident", [P, P], F32)
        ident16 = sb("ident16", [P, P], F16)
        ones16 = sb("ones16", [P, P], F16)
        before = sb("before", [P, P], F16)
        zero16 = sb("zero16", [P, NT * P], F16)
        headmask = sb("headmask", [P, HC, VW], F32)
        slots_i = sb("slots_i", [P, CAP], I32)
        slots = sb("slots", [P, CAP], F16)
        in_batch = sb("in_batch", [P, 2], F32)
        valid = sb("valid", [P, 1], F32)
        mx3 = sb("mx3", [P, 2, NB], F32)
        mxa = sb("mxa", [P, 2], F32)
        nb = sb("nb", [P, 2], F32)
        rs = sb("rs", [P, 2], F32)
        rinv = sb("rinv", [P, 2], F32)
        rr = sb("rr", [P, 2], F32)
        o2 = sb("o2", [P, 2, D], F32)
        warm = sb("warm", [P, 1], F32)
        on = sb("on", [P, 2, D], F32)
        den = sb("den", [P, 2 * NT, LH], F32)
        st = sb("st", [P, NT, 6], F32)
        mv = sb("mv", [P, NT, 2], F32)
        ve = sb("ve", [P, NT], F32)
        sd = sb("sd", [P, NT], F32)
        rstd = sb("rstd", [P, NT], F32)
        gw = sb("gw", [P, CC, E], F32)
        gbias = sb("gbias", [P, E], F32)
        wsgu = sb("wsgu", [P, CC, 2, F], F32)
        wsd = sb("wsd", [F, C], F32)
        cut = carver(rb)
        r1 = cut([NT, E], F32, 4)
        r2 = cut([NT, E], F32, 4)
        r3 = cut([NT, E + 2], F32, 4)
        r4 = cut([NT, E + 2], F32, 4)
        m8 = cut([NT * G, 8], F32, 4)
        gs = cut([NT, G + KG], F32, 4)
        gsr = cut([NT, G + KG], F32, 4)
        t8 = cut([NT, 8], F32, 4)
        t6 = cut([NT, 8], F32, 4)
        gsel = cut([NT, G], F32, 4)
        gpen = cut([NT, G], F32, 4)
        sel16 = cut([NT, E], F16, 2)
        w16 = cut([NT, E + GE, 2], F16, 2)
        posm = cut([NT, E + 2 * GE], F16, 2)
        wsum = cut([NT], F32, 4)
        wrec = cut([NT], F32, 4)
        sh_g = cut([NT, F], F32, 4)
        sh_u = cut([NT, F], F32, 4)
        sh_h = cut([NT, F], F32, 4)
        sh_hT = cut([NT * P], F32, 4)[0:F]
        act_g = cut([2, F], F32, 4)
        h_sb = cut([2, F], F32, 4)
        hT = cut([2, P], F32, 4)[0:F]
        o_hl = cut([2, 2, C], F16, 2)

        ps = stack.enter_context(nc.psum_tensor("ps", [P, 8, 512], F32))

        x_in, wp_dma, wk_dma, wq_dma, wv_dma, wo_dma, small_dma = (
            sem(n) for n in ("x_in", "wp_dma", "wk_dma", "wq_dma", "wv_dma", "wo_dma", "small_dma"))
        wqkv_dma = [sem("wqkv_dma0"), sem("wqkv_dma1")]
        bproj_dma = sem("bproj_dma")
        tiles_set = sem("tiles_set")
        oT_low = sem("oT_low")
        ctx_dma, mask_dma = sem("ctx_dma"), sem("mask_dma")
        ew_dma = [sem("ew_dma0"), sem("ew_dma1")]
        out_dma = sem("out_dma")
        pads_zero = sem("pads_zero")
        const_step = sem("const_step")
        consts_set = sem("consts_set")
        dve_const = sem("dve_const")
        filled, emptied_v, emptied_a = sem("filled"), sem("emptied_v"), sem("emptied_a")
        filled2, emptied2_v, emptied2_a = sem("filled2"), sem("emptied2_v"), sem("emptied2_a")
        dve_step = sem("dve_step")
        act_step = sem("act_step")
        ln_var, ln_std, ln_out = sem("ln_var"), sem("ln_std"), sem("ln_out")
        ao_ready = sem("ao_ready")
        ctx_high = sem("ctx_high")
        ctx_split, mask_bias, q_staged, oT_zero = sem("ctx_split"), sem("mask_bias"), sem("q_staged"), sem("oT_zero")
        scored, p_trans, pv_done, o_trans, cT_trans, proj_done = (
            sem(n) for n in ("scored", "p_trans", "pv_done", "o_trans", "cT_trans", "proj_done"))
        masked, row_max, bias_ready, p_low, recip1, recip_ready, o_norm, pair_sum = (
            sem(n) for n in ("masked", "row_max", "bias_ready", "p_low", "recip1", "recip_ready", "o_norm", "pair_sum"))
        exp_done, p_high, o2_done, oT_copied, cT_copied = (
            sem(n) for n in ("exp_done", "p_high", "o2_done", "oT_copied", "cT_copied"))
        x2_split, routed, sh_done, x2_summed = sem("x2_split"), sem("routed"), sem("sh_done"), sem("x2_summed")
        disp_built, w_built, xs_filled, xs_copied, w_filled, w_copied = (
            sem(n) for n in ("disp_built", "w_built", "xs_filled", "xs_copied", "w_filled", "w_copied"))
        dT_filled, dT_copied, gu_filled, silu_done, h_ready, hT_filled, hT_copied, dn_filled, o_high, o_low, comb_done = (
            sem(n) for n in ("dT_filled", "dT_copied", "gu_filled", "silu_done", "h_ready", "hT_filled", "hT_copied",
                             "dn_filled", "o_high", "o_low", "comb_done"))
        y_filled, y_copied, y_copied_a, yb_filled = sem("y_filled"), sem("y_copied"), sem("y_copied_a"), sem("yb_filled")

        front, mid = Fills(FRONT), Fills(MID)

        def front_wait(eng, name, i=0):
            f = front.at(name, i)
            if front.takes("v", f):
                eng.wait_ge(emptied_v, front.emptied("v", f))
            if front.takes("a", f):
                eng.wait_ge(emptied_a, front.emptied("a", f))

        def mid_wait(eng, name, i=0):
            f = mid.at(name, i)
            if mid.takes("v", f):
                eng.wait_ge(emptied2_v, mid.emptied("v", f))
            if mid.takes("a", f):
                eng.wait_ge(emptied2_a, mid.emptied("a", f))

        def wait_alone(eng, semaphore, value):
            value = value if isinstance(value, int) else eng.to_reg(value)
            eng.wait_ge(consts_set, 8)
            eng.wait_ge(semaphore, value)

        block = stack.enter_context(nc.Block())

        @block.sync
        def _(sp):
            for half in range(2):
                sp.dma_start(wqkv_in[:, 3 * half:3 * half + 3, :],
                             w_qkv.rearrange("(g p) c -> p g c", p=P)[:, 3 * half:3 * half + 3, :]).then_inc(wqkv_dma[half], 16)
            sp.wait_ge(pads_zero, 1)
            for k in range(2):
                sp.dma_start(x_sb[HALF * k:HALF * k + N, :, :],
                             x.rearrange("(j k) n c -> k n j c", k=2)[k]).then_inc(x_in, 16)
            sp.dma_start(wp_in[:], w_proj.rearrange("(g p) c -> p g c", p=P)).then_inc(wp_dma, 16)
            sp.dma_start(wk_in, Wk.rearrange("e (g d) -> e g d", d=D)).then_inc(wk_dma, 16)
            sp.dma_start(wq_in, Wq.rearrange("(k p) n -> p k n", p=P)).then_inc(wq_dma, 16)
            sp.dma_start(bproj[:], b_proj.rearrange("(a c) -> a c", a=1).to_broadcast([P, C])).then_inc(bproj_dma, 16)
            sp.dma_start(wv_in, Wv.rearrange("e (g d) -> e g d", d=D)).then_inc(wv_dma, 16)
            sp.dma_start(wo_in, Wo.rearrange("(h v) n -> v h n", v=D)).then_inc(wo_dma, 16)

            def load_batch(b):
                if b >= 1:
                    sp.wait_ge(ctx_split, b)
                    sp.wait_ge(mask_bias, b)
                s = b % B
                sp.dma_start(c_in[:], ctx[s].rearrange("(c p) d -> p c d", p=KP)).then_inc(ctx_dma, 16)
                sp.dma_start(m_in[:], mask[s:s + 1, :].to_broadcast([P, SK])).then_inc(mask_dma, 16)

            load_batch(0)
            sp.dma_start(gw[:], gate_w.rearrange("(k p) e -> p k e", p=P)).then_inc(small_dma, 16)
            sp.dma_start(gbias[:], bias.rearrange("(a e) -> a e", a=1).to_broadcast([P, E])).then_inc(small_dma, 16)
            sp.dma_start(wsgu[:, :, 0, :], ws_gate.rearrange("(k p) f -> p k f", p=P)).then_inc(small_dma, 16)
            sp.dma_start(wsgu[:, :, 1, :], ws_up.rearrange("(k p) f -> p k f", p=P)).then_inc(small_dma, 16)
            sp.dma_start(wsd[:], ws_down).then_inc(small_dma, 16)
            load_batch(1)

            def load_experts(g):
                e = slice(GE * g, GE * (g + 1))
                s = ew_dma[g % 2]
                sp.dma_start(w_gu[:, g % 2, 0], w_gate[e].rearrange("e (p k) f -> p e (k f)", k=CC)).then_inc(s, 16)
                sp.dma_start(w_gu[:, g % 2, 1], w_up[e].rearrange("e (p k) f -> p e (k f)", k=CC)).then_inc(s, 16)
                sp.dma_start(w_dn[0:F, g % 2], w_down[e].rearrange("e f h -> f e h")).then_inc(s, 16)

            sp.wait_ge(scored, 1)
            load_experts(0)
            load_experts(1)
            for b in range(2, B + 1):
                load_batch(b)
            for g in range(2, NG):
                sp.wait_ge(dn_filled, GP * (g - 1))
                load_experts(g)
            sp.wait_ge(ln_out, 3 * NT)
            for k in range(2):
                sp.dma_start(out.rearrange("(j k) n c -> k n j c", k=2)[k],
                             x1[HALF * k:HALF * k + N, :, :]).then_inc(out_dma, 16)
            sp.wait_ge(out_dma, 32)

        @block.gpsimd
        def _(pool):
            steps = [0]

            def chained(ins):
                steps[0] += 1
                ins.then_inc(const_step, 1)
                pool.wait_ge(const_step, steps[0])

            nc.gpsimd.memset(ident[:], 0.0).then_inc(const_step, 1)
            nc.gpsimd.memset(ident16[:], 0.0).then_inc(const_step, 1)
            nc.gpsimd.memset(before[:], 1.0).then_inc(const_step, 1)
            nc.gpsimd.memset(headmask[:], 1.0).then_inc(const_step, 1)
            nc.gpsimd.memset(in_batch[:], 1.0).then_inc(const_step, 1)
            steps[0] = 5
            chained(nc.gpsimd.iota(slots_i[:], pattern=[[1, CAP]], base=0, channel_multiplier=0))
            nc.gpsimd.memset(ones16[:], 1.0).then_inc(consts_set, 1)
            nc.gpsimd.memset(zero16[:], 0.0).then_inc(consts_set, 1)
            for m in (ident, ident16):
                nc.gpsimd.affine_select(out=m[:], in_=m[:], compare_op=ALU.not_equal, fill=1.0, base=0,
                                        pattern=[[-1, P]], channel_multiplier=1).then_inc(consts_set, 1)
            nc.gpsimd.affine_select(out=before[:], in_=before[:], compare_op=ALU.is_gt, fill=0.0, base=0,
                                    pattern=[[1, P]], channel_multiplier=-1).then_inc(consts_set, 1)
            nc.gpsimd.tensor_copy(slots[:], slots_i[:]).then_inc(consts_set, 1)
            chained(nc.gpsimd.affine_select(out=in_batch[:], in_=in_batch[:], compare_op=ALU.is_ge, fill=0.0, base=N - 1,
                                            pattern=[[HALF, 2]], channel_multiplier=-1))
            chained(nc.gpsimd.affine_select(out=in_batch[:], in_=in_batch[:], compare_op=ALU.is_ge, fill=0.0, base=0,
                                            pattern=[[-HALF, 2]], channel_multiplier=1))
            nc.gpsimd.tensor_tensor(valid[:], in_batch[:, 0:1], in_batch[:, 1:2], ALU.add).then_inc(consts_set, 1)
            chained(nc.gpsimd.affine_select(out=headmask[:], in_=headmask[:], compare_op=ALU.is_ge, fill=0.0, base=0,
                                            pattern=[[-HD, HC], [0, VW]], channel_multiplier=1))
            nc.gpsimd.affine_select(out=headmask[:], in_=headmask[:], compare_op=ALU.is_ge, fill=0.0, base=HD - 1,
                                    pattern=[[HD, HC], [0, VW]], channel_multiplier=-1).then_inc(consts_set, 1)

            def split_ctx(b, parity):
                wait_alone(pool, ctx_dma, 16 * (b + 1))
                nc.gpsimd.tensor_copy(c16[:, parity, :, 0, :], c_in[:]).then_inc(ctx_high, 1)
                wait_alone(pool, ctx_high, b + 1)
                nc.gpsimd.tensor_tensor(c16[:, parity, :, 1, :], c_in[:], c16[:, parity, :, 0, :],
                                        ALU.subtract).then_inc(ctx_split, 1)
                wait_alone(pool, mask_dma, 16 * (b + 1))
                nc.gpsimd.tensor_scalar(mb[:, parity, :], m_in[:], BIG, -BIG, ALU.mult, ALU.add).then_inc(mask_bias, 1)

            def stage_q(b, parity):
                for hl in range(2):
                    nc.gpsimd.tensor_copy(q_st[:, parity, hl, :],
                                          Qt[:, hl, bass.ds(b, 1), :].rearrange("p a q -> p (a q)")).then_inc(q_staged, 1)

            split_ctx(0, 0)
            front_wait(pool, "x1T", 1)
            nc.gpsimd.memset(oT, 0.0).then_inc(oT_zero, 1)
            split_ctx(1, 1)

            def pair_body(i):
                for k in range(2):
                    wait_alone(pool, pv_done, PAIR * i + QT * (k + 1))
                    split_ctx(2 * i + 2 + k, k)
                    stage_q(2 * i + 2 + k, k)
            with pool.Fori(0, NT - 1) as i:
                pair_body(i)
            pool.wait_ge(pv_done, PAIR * (NT - 1) + QT)
            split_ctx(B, 0)
            pool.wait_ge(pair_sum, NT)
            for m, v in ((gs[:, :, G:G + KG], -2 * BIG), (t8, -2 * BIG), (t6, -2 * BIG), (r3[:, :, E:E + 2], -2 * BIG),
                         (w16[:, :, E:, :], 0.0), (posm[:, :, E:], 1000.0), (disp, 0.0), (xs, 0.0)):
                nc.gpsimd.memset(m, v).then_inc(tiles_set, 1)

            pool.wait_ge(emptied2_a, mid.emptied("a", mid.at("shgu", NT - 1)))
            nc.gpsimd.tensor_tensor(sh_h[:], sh_g[:], sh_u[:], ALU.mult).then_inc(sh_done, 1)

            pool.wait_ge(emptied2_a, mid.emptied("a", mid.at("shy", NT - 1)))
            nc.gpsimd.tensor_tensor(x_sb[:], x_sb[:], x1[:], ALU.add).then_inc(x2_summed, 1)

        @block.tensor
        def _(pe):
            pe.wait_ge(consts_set, 8)

            def fill(name, i=0):
                f = front.at(name, i)
                if f >= 8:
                    g = f - 8
                    if front.takes("v", g):
                        pe.wait_ge(emptied_v, front.emptied("v", g))
                    if front.takes("a", g):
                        pe.wait_ge(emptied_a, front.emptied("a", g))
                return ps[:, f % 8, :]

            for i in range(4):
                c, half = i % 2, i // 2
                if c == 0:
                    pe.wait_ge(wqkv_dma[half], 16)
                o = fill("wqkvT", i)
                for g in range(3):
                    last = nc.tensor.transpose(o[:, P * g:P * (g + 1)],
                                               wqkv_in[:, 3 * half + g, P * c:P * (c + 1)], ident[:])
                last.then_inc(filled, 1)
            pe.wait_ge(x_in, 32)
            for c in range(CC):
                o = fill("xT", c)
                for j in range(NT):
                    last = nc.tensor.transpose(o[:, P * j:P * (j + 1)], x_sb[:, j, P * c:P * (c + 1)], ident[:])
                last.then_inc(filled, 1)
            for c in range(CC):
                front_wait(pe, "xT", c)
            for i in range(4):
                front_wait(pe, "wqkvT", i)
            for o_c in range(CC):
                o = fill("qT", o_c)
                for c in range(CC):
                    last = nc.tensor.matmul(o, wqkvT[:, c, P * o_c:P * (o_c + 1)], xT[:, c, :],
                                            start=(c == 0), stop=(c == CC - 1))
                last.then_inc(filled, 1)
            for j in range(NT):
                o = fill("kv", j)
                for c in range(CC):
                    last = nc.tensor.matmul(o, xT[:, c, P * j:P * (j + 1)], wqkvT[:, c, C:3 * C],
                                            start=(c == 0), stop=(c == CC - 1))
                last.then_inc(filled, 1)
            pe.wait_ge(wp_dma, 16)
            o = fill("wpT")
            for c in range(CC):
                for g in range(CC):
                    last = nc.tensor.transpose(o[:, C * c + P * g:C * c + P * (g + 1)],
                                               wp_in[:, g, P * c:P * (c + 1)], ident[:])
            last.then_inc(filled, 1)
            pe.wait_ge(wk_dma, 16)
            for i in range(2):
                o = fill("WkT", i)
                for g in range(4):
                    last = nc.tensor.transpose(o[:, D * g:D * (g + 1)], wk_in[:, 4 * i + g, :], ident[:])
                last.then_inc(filled, 1)
            for b in range(B):
                front_wait(pe, "kv", b // 2)
                o = fill("G", b)
                r = HALF * (b % 2)
                for c in range(CC):
                    last = nc.tensor.matmul(o[:, HC * VW * c:HC * VW * (c + 1)],
                                            k_sb[r:r + N, b // 2, P * c:P * (c + 1)],
                                            v_aug[r:r + N, b // 2, HC * c:HC * (c + 1), :], start=True, stop=True)
                last.then_inc(filled, 1)
            pe.wait_ge(wq_dma, 16)
            for i in range(8):
                o = fill("WqT", i)
                for n in range(4):
                    h, c = 2 * i + n // 2, n % 2
                    last = nc.tensor.transpose(o[:, P * n:P * (n + 1)], wq_in[:, c, D * h:D * (h + 1)], ident[:])
                last.then_inc(filled, 1)
            front_wait(pe, "qT", 0)
            front_wait(pe, "qT", 1)
            for j in range(NT):
                o = fill("lin", j)
                for k in range(2):
                    b = 2 * j + k
                    front_wait(pe, "G", b)
                    for c in range(CC):
                        last = nc.tensor.matmul(o[HALF * k:HALF * (k + 1), HC * VW * c:HC * VW * (c + 1)],
                                                qT[:, c, HALF * b:HALF * (b + 1)],
                                                kvm[:, b, HC * VW * c:HC * VW * (c + 1)], start=True, stop=True)
                last.then_inc(filled, 1)
            front_wait(pe, "WkT", 0)
            front_wait(pe, "WkT", 1)
            front_wait(pe, "WqT", 6)
            front_wait(pe, "WqT", 7)
            for i in range(8):
                o = fill("M", i)
                for n in range(4):
                    h, c = 2 * i + n // 2, n % 2
                    last = nc.tensor.matmul(o[:, D * n:D * (n + 1)], wqT[:, h, c, :], wkT[:, h // 2, :],
                                            start=True, stop=True)
                last.then_inc(filled, 1)
            pe.wait_ge(ao_ready, 1)
            for c in range(CC):
                o = fill("aoT", c)
                for j in range(NT):
                    last = nc.tensor.transpose(o[:, P * j:P * (j + 1)], ao[:, j, P * c:P * (c + 1)], ident[:])
                last.then_inc(filled, 1)
            pe.wait_ge(wv_dma, 16)
            for i in range(2):
                o = fill("WvT", i)
                for g in range(4):
                    last = nc.tensor.transpose(o[:, D * g:D * (g + 1)], wv_in[:, 4 * i + g, :], ident[:])
                last.then_inc(filled, 1)
            front_wait(pe, "wpT")
            front_wait(pe, "aoT", 0)
            front_wait(pe, "aoT", 1)
            for j in range(NT):
                o = fill("proj", j)
                for c in range(CC):
                    last = nc.tensor.matmul(o[:, 0:C], aoT[:, c, P * j:P * (j + 1)], wpT[:, c, :],
                                            start=(c == 0), stop=(c == CC - 1))
                last.then_inc(filled, 1)
            front_wait(pe, "WvT", 0)
            front_wait(pe, "WvT", 1)
            pe.wait_ge(wo_dma, 16)

            def multiply_W2(i):
                o = fill("W2", i)
                for n in range(2):
                    h = 2 * i + n
                    last = nc.tensor.matmul(o[:, C * n:C * (n + 1)], wvT[:, h // 2, :], wo_in[:, h, :],
                                            start=True, stop=True)
                last.then_inc(filled, 1)

            for i in EARLY_W2:
                multiply_W2(i)
            pe.wait_ge(ln_out, NT)
            for c in range(CC):
                o = fill("x1T", c)
                for j in range(NT):
                    last = nc.tensor.transpose(o[:, P * j:P * (j + 1)], x1[:, j, P * c:P * (c + 1)], ident[:])
                last.then_inc(filled, 1)
            pe.wait_ge(ctx_split, 1)
            def transpose_ctx(o, parity, u):
                for hl in range(2):
                    for t in range(TB):
                        at = 512 * hl + P * t
                        last = nc.tensor.transpose(o[:, at:at + KP], c16[:, parity, TB * u + t, hl, :],
                                                   ident16[0:KP, 0:KP])
                return last

            for u in range(NB):
                transpose_ctx(fill("cT", u).bitcast(F16), 0, u).then_inc(filled, 1)
            for i in LATE_W2:
                multiply_W2(i)
            front_wait(pe, "M", 6)
            front_wait(pe, "M", 7)
            front_wait(pe, "x1T", 0)
            front_wait(pe, "x1T", 1)
            for h in range(QH):
                o = fill("Qt", h)
                for n, (c, mh, xh) in enumerate([(c, mh, xh) for c in range(CC) for mh, xh in ((0, 0), (0, 1), (1, 0))]):
                    last = nc.tensor.matmul(o[:, 0:B * N], M[:, mh, h, c, :],
                                            x1T16[:, xh, c, :].rearrange("p (b t) -> p b t", t=HALF)[:, :, 0:N],
                                            start=(n == 0), stop=(n == 3 * CC - 1))
                last.then_inc(filled, 1)
            score, prob_t, o_bank, misc = ps[:, 0:NB], ps[:, NB:2 * NB], ps[:, 6], ps[:, 7]

            def project(i, o_read):
                pe.wait_ge(oT_low, PAIR * (i + 1))
                pe.wait_ge(o_norm, o_read)
                if not (isinstance(i, int) and i == 0):
                    pe.wait_ge(pair_sum, i)
                for h in range(QH):
                    for n, (oh, wh) in enumerate(((0, 0), (0, 1), (1, 0))):
                        last = nc.tensor.matmul(o_bank[:, C:2 * C],
                                                oT[:, oh].rearrange("p b (t h) -> p (b t) h", h=QH)[:, :, h],
                                                W2[:, wh, h, :], start=(h == 0 and n == 0),
                                                stop=(h == QH - 1 and n == 2))
                last.then_inc(proj_done, 1)

            def tile_step(i, j, first=False, parts="STPOC"):
                n = PAIR * i + j
                b, par = 2 * i + j // QT, (j // QT) % 2
                cols = slice(P * (j % QT), P * (j % QT + 1))
                if "S" in parts:
                    if j % QT == 0:
                        if not first:
                            pe.wait_ge(q_staged, 2 * (b - 1))
                        pe.wait_ge(cT_copied, NB * (b + 1))
                    q = Qt[:, :, j // QT, cols] if first else q_st[:, par, :, cols]
                    for k in range(NB):
                        if not (first and j == 0):
                            pe.wait_ge(masked, NB * (n - 1) + k + 1)
                        keys = slice(KB * k, KB * (k + 1))
                        o = score[:, k, 0:KB]
                        nc.tensor.matmul(o, q[:, 0], cT[:, par, 0, keys], start=True, stop=False)
                        nc.tensor.matmul(o, q[:, 0], cT[:, par, 1, keys], start=False, stop=False)
                        nc.tensor.matmul(o, q[:, 1], cT[:, par, 0, keys],
                                         start=False, stop=True).then_inc(scored, 1)
                if j == 3 and not first:
                    project(i - 1, n - 2)
                u = j % QT - (QT - NB)
                if "C" in parts and u >= 0:
                    if u == 0:
                        pe.wait_ge(ctx_split, b + 2)
                    if not (first and j < 4):
                        pe.wait_ge(oT_low, n - 3)
                    transpose_ctx(misc.bitcast(F16), 1 - par, u).then_inc(cT_trans, 1)
                if "T" in parts and not (first and j < 1):
                    pe.wait_ge(exp_done, n)
                    for k in range(NB):
                        if not (first and j < 2):
                            pe.wait_ge(p_high, NB * (n - 2) + k + 1)
                            pe.wait_ge(p_low, NB * (n - 2) + k + 1)
                        for t in range(TB):
                            kt = TB * k + t
                            last = nc.tensor.transpose(prob_t[0:KP, k, P * t:P * (t + 1)],
                                                       sc[:, (j - 1) % 2, KP * kt:KP * (kt + 1)], ident[:])
                        last.then_inc(p_trans, 1)
                if "P" in parts and not (first and j < 2):
                    if not (first and j < 3):
                        pe.wait_ge(o_norm, n - 2)
                        if j == 3 and not first:
                            pe.wait_ge(pair_sum, i)
                    pe.wait_ge(p_high, NB * (n - 1))
                    pe.wait_ge(p_low, NB * (n - 1))
                    cp = ((j - 2) // QT) % 2
                    for kt in range(KT):
                        for hl in range(2):
                            last = nc.tensor.matmul(
                                o_bank[:, 0:(2 - hl) * D], pT[0:KP, j % 2, hl, P * kt:P * (kt + 1)],
                                c16[:, cp, kt, 0:2 - hl, :], start=(kt == 0 and hl == 0),
                                stop=(kt == KT - 1 and hl == 1))
                    last.then_inc(pv_done, 1)
                if "O" in parts and not (first and j < 3):
                    pe.wait_ge(o_norm, n - 2)
                    if not (first and j < 4):
                        pe.wait_ge(oT_low, n - 3)
                    if "C" in parts and u >= 0:
                        pe.wait_ge(cT_copied, NB * (b + 1) + u + 1)
                    nc.tensor.transpose(misc[:, 0:P], on[:, (j - 3) % 2, :], ident[:]).then_inc(o_trans, 1)

            for u in range(NB):
                front_wait(pe, "cT", u)
            front_wait(pe, "Qt", QH - 1)
            for j in range(PAIR):
                tile_step(0, j, first=True)
            with pe.Fori(1, NT) as i:
                for j in range(PAIR):
                    tile_step(i, j)
            for j, parts in ((0, "TPO"), (1, "PO"), (2, "O")):
                tile_step(NT, j, parts=parts)
            project(NT - 1, TILES)

            def fill2(name, i=0):
                f = mid.at(name, i)
                if f >= 8:
                    g = f - 8
                    if mid.takes("v", g):
                        pe.wait_ge(emptied2_v, mid.emptied("v", g))
                    if mid.takes("a", g):
                        pe.wait_ge(emptied2_a, mid.emptied("a", g))
                return ps[:, f % 8, :]

            pe.wait_ge(ln_out, 2 * NT)
            for c in range(CC):
                o = fill2("x2T", c)
                for j in range(NT):
                    last = nc.tensor.transpose(o[:, P * j:P * (j + 1)], x1[:, j, P * c:P * (c + 1)], ident[:])
                last.then_inc(filled2, 1)
            pe.wait_ge(small_dma, 16 * 5)
            mid_wait(pe, "x2T", 0)
            mid_wait(pe, "x2T", 1)
            o = fill2("logit")
            for j in range(NT):
                for c in range(CC):
                    last = nc.tensor.matmul(o[:, E * j:E * (j + 1)], x1T[:, c, P * j:P * (j + 1)], gw[:, c, :],
                                            start=(c == 0), stop=(c == CC - 1))
            last.then_inc(filled2, 1)
            for j in range(NT):
                o = fill2("shgu", j)
                for c in range(CC):
                    last = nc.tensor.matmul(o[:, 0:2 * F], x1T[:, c, P * j:P * (j + 1)], wsgu[:, c, :, :],
                                            start=(c == 0), stop=(c == CC - 1))
                last.then_inc(filled2, 1)
            o = fill2("shT")
            pe.wait_ge(sh_done, 1)
            for j in range(NT):
                last = nc.tensor.transpose(o[0:F, P * j:P * (j + 1)], sh_h[:, j, :], ident[:])
            last.then_inc(filled2, 1)
            mid_wait(pe, "shT")

            def shared_down(j):
                o = fill2("shy", j)
                nc.tensor.matmul(o[:, 0:C], sh_hT[:, P * j:P * (j + 1)], wsd[:], start=True, stop=True).then_inc(filled2, 1)

            shared_down(0)
            shared_down(1)
            pe.wait_ge(routed, 1)
            o = fill2("pos")
            for j in range(NT):
                for k in range(j + 1):
                    last = nc.tensor.matmul(o[:, E * j:E * (j + 1)], (before if k == j else ones16)[:],
                                            sel16[:, k, :], start=(k == 0), stop=(k == j))
            last.then_inc(filled2, 1)
            shared_down(2)
            shared_down(3)

            mid_wait(pe, "pos")
            mid_wait(pe, "shy", NT - 1)
            y_acc, xs_bank, gu_bank, misc2, dn_bank, dT_bank = ps[:, 0:2], ps[:, 2], ps[:, 3:5], ps[:, 5], ps[:, 6], ps[:, 7]
            for c in range(CC):
                nc.tensor.matmul(y_acc[:, c, :], zero16[:, 0:P], zero16[:], start=True, stop=False,
                                 skip_group_check=True)

            def dispatch(g, par, piece, first=False):
                c, half = piece // 2, piece % 2
                if c == 0:
                    pe.wait_ge(disp_built, 2 * g + half + 1)
                if piece == 0:
                    if not first:
                        pe.wait_ge(xs_copied, CC * g)
                if piece == 2:
                    pe.wait_ge(xs_copied, CC * g + 1)
                for j in (2 * half, 2 * half + 1):
                    for hl in range(2):
                        last = nc.tensor.matmul(xs_bank[:, 0:GE * CAP], x2h[:, hl, j, c, :],
                                                disp[:, par, j, :, 0:CAP], start=(j == 0 and hl == 0),
                                                stop=(j == NT - 1 and hl == 1))
                if half == 1:
                    last.then_inc(xs_filled, 1)

            def slot_weights(g, par, first, n):
                pe.wait_ge(w_built, g + 1)
                if not first:
                    pe.wait_ge(hT_copied, n)
                for q in range(GP):
                    for j in range(NT):
                        last = nc.tensor.matmul(misc2[:, C + 4 * q:C + 4 * (q + 1)],
                                                disp[:, par, j, 2 * q:2 * q + 2, :].rearrange("p e s -> p (e s)"),
                                                w_grp[:, par, j, 2 * q:2 * q + 2, :].rearrange("p e s -> p (e s)"),
                                                start=(j == 0), stop=(j == NT - 1))
                last.then_inc(w_filled, 1)

            def pair_step(i, q, first=False, parts="GTCN"):
                n = 2 * GP * i + q
                g, par, gq = 2 * i + q // GP, (q // GP) % 2, q % GP
                if "T" in parts and not (first and q < 1):
                    pe.wait_ge(h_ready, n)
                    if not (first and q < 2):
                        pe.wait_ge(hT_copied, n - 1)
                    if gq == 0:
                        pe.wait_ge(w_copied, g + 1)
                    nc.tensor.transpose(misc2[0:F, 0:P], h_sb[:, (q - 1) % 2, :], ident[:]).then_inc(hT_filled, 1)
                if "G" in parts:
                    if not (first and q < 1):
                        pe.wait_ge(dT_copied, n)
                    o = dT_bank.bitcast(F16)[:, 512 * (q % 2):512 * (q % 2 + 1)]
                    for j in range(NT):
                        last = nc.tensor.transpose(o[:, P * j:P * (j + 1)],
                                                   disp[:, par, j, 2 * gq:2 * gq + 2, :].rearrange("p e s -> p (e s)"),
                                                   ident16[:])
                    last.then_inc(dT_filled, 1)
                    if gq == 0:
                        pe.wait_ge(xs_copied, CC * (g + 1))
                        pe.wait_ge(ew_dma[par], 48 * (i + 1))
                    if not (first and q < 2):
                        pe.wait_ge(h_ready, n - 1)
                    for c in range(CC):
                        for s in range(2):
                            e = 2 * gq + s
                            last = nc.tensor.matmul(gu_bank[SLOT * s:SLOT * (s + 1), q % 2, 0:2 * F],
                                                    xs[:, par, c, e, :], w_gu[:, par, :, e, F * c:F * (c + 1)],
                                                    start=(c == 0), stop=(c == CC - 1))
                    last.then_inc(gu_filled, 1)
                    dispatch(g + 1, 1 - par, gq)
                    if gq == GP - 1:
                        slot_weights(g + 1, 1 - par, False, n)
                if "C" in parts and not (first and q < 2):
                    pe.wait_ge(o_high, n - 1)
                    pe.wait_ge(o_low, n - 1)
                    pe.wait_ge(dT_copied, n - 1)
                    for c in range(CC):
                        for hl in range(2):
                            last = nc.tensor.matmul(batches(y_acc[:, c, :]), o_hl[:, q % 2, hl, P * c:P * (c + 1)],
                                                    batches(dispT[:, (q - 2) % GP, :]), start=False, stop=False,
                                                    skip_group_check=True)
                    last.then_inc(comb_done, 1)
                if "N" in parts and not (first and q < 1):
                    pe.wait_ge(hT_copied, n)
                    if not (first and q < 2):
                        pe.wait_ge(o_high, n - 1)
                        pe.wait_ge(o_low, n - 1)
                    dq, dp = (q - 1) % GP, ((q - 1) // GP) % 2
                    for s in range(2):
                        last = nc.tensor.matmul(dn_bank[SLOT * s:SLOT * (s + 1), 0:C],
                                                hT[:, (q - 1) % 2, SLOT * s:SLOT * (s + 1)],
                                                w_dn[0:F, dp, 2 * dq + s, :], start=True, stop=True)
                    last.then_inc(dn_filled, 1)

            def batches(cols):
                return cols.rearrange("p (b t) -> p b t", t=HALF)[:, :, 0:N]

            for piece in range(2 * CC):
                dispatch(0, 0, piece, first=True)
            slot_weights(0, 0, True, 0)
            pe.wait_ge(w_copied, 1)
            for q in range(2 * GP):
                pair_step(0, q, first=True)
            with pe.Fori(1, NG // 2) as i:
                for q in range(2 * GP):
                    pair_step(i, q)
            pair_step(NG // 2, 0, parts="TCN")
            pair_step(NG // 2, 1, parts="C")
            for c in range(CC):
                nc.tensor.matmul(y_acc[:, c, :], zero16[:, 0:P], zero16[:], start=False, stop=True,
                                 skip_group_check=True).then_inc(y_filled, 1)
            pe.wait_ge(y_copied, 1)
            pe.wait_ge(y_copied_a, 1)
            for j in range(NT):
                for c in range(CC):
                    last = nc.tensor.transpose(ps[:, 2 + j // 2, C * (j % 2) + P * c:C * (j % 2) + P * (c + 1)],
                                               yT_sb[:, c, P * j:P * (j + 1)], ident[:])
            last.then_inc(yb_filled, 1)

        @block.scalar
        def _(act):
            def take(name, i=0):
                f = front.at(name, i)
                act.wait_ge(filled, f + 1)
                return ps[:, f % 8, :]

            def mine(name):
                return [i for i, f in enumerate(front.where[name]) if front.takes("a", f)]

            def std(k, tiles=slice(0, NT)):
                act.wait_ge(ln_var, k)
                nc.scalar.activation(sd[:, tiles], ve[:, tiles], ACT.Sqrt).then_inc(ln_std, 1)

            for i in mine("wqkvT"):
                nc.scalar.copy(wqkvT[:, i % 2, 384 * (i // 2):384 * (i // 2 + 1)],
                               take("wqkvT", i)[:, 0:384]).then_inc(emptied_a, 1)
            for c in mine("xT"):
                nc.scalar.copy(xT[:, c, :], take("xT", c)).then_inc(emptied_a, 1)
            for c in mine("qT"):
                nc.scalar.activation(qT[:, c, :], take("qT", c), ACT.Relu).then_inc(emptied_a, 1)
            for j in mine("kv"):
                nc.scalar.copy(v_aug[:, j, :, 0:HD],
                               take("kv", j)[:, C:2 * C].rearrange("p (h d) -> p h d", d=HD)).then_inc(emptied_a, 1)
            nc.scalar.copy(wpT[:].rearrange("p a b -> p (a b)"), take("wpT")).then_inc(emptied_a, 1)
            for i in mine("WkT"):
                nc.scalar.copy(wkT[:, 4 * i:4 * i + 4, :].rearrange("p a b -> p (a b)"),
                               take("WkT", i)).then_inc(emptied_a, 1)
            for i in mine("WqT"):
                nc.scalar.copy(wqT[:, 2 * i:2 * i + 2].rearrange("p a b c -> p (a b c)"),
                               take("WqT", i)).then_inc(emptied_a, 1)
            for i in mine("M"):
                nc.scalar.mul(M[:, 0, 2 * i:2 * i + 2].rearrange("p a b c -> p (a b c)"), take("M", i),
                              M_UP * D ** -0.5).then_inc(emptied_a, 1)
            for c in mine("aoT"):
                nc.scalar.copy(aoT[:, c, :], take("aoT", c)).then_inc(emptied_a, 1)
            for i in mine("WvT"):
                nc.scalar.copy(wvT[:, 4 * i:4 * i + 4, :].rearrange("p a b -> p (a b)"),
                               take("WvT", i)).then_inc(emptied_a, 1)

            def high_W2(i):
                nc.scalar.mul(W2[:, 0, 2 * i:2 * i + 2, :].rearrange("p a b -> p (a b)"),
                              take("W2", i), W_UP).then_inc(emptied_a, 1)

            def copy_cT(dst_par, u, bank16):
                return nc.scalar.copy(
                    cT[:, dst_par, :, KB * u:KB * (u + 1)].rearrange("p s (t k) -> p s t k", k=KP),
                    bank16.rearrange("p (s t k) -> p s t k", s=2, k=P)[:, :, :, 0:KP])

            for i in EARLY_W2:
                high_W2(i)
                if i == 0:
                    std(1)
            for c in mine("x1T"):
                nc.scalar.copy(x1T16[:, 0, c, :], take("x1T", c)).then_inc(emptied_a, 1)
            for u in mine("cT"):
                copy_cT(0, u, take("cT", u).bitcast(F16)).then_inc(emptied_a, 1)
            for i in LATE_W2:
                high_W2(i)
            for h in range(QH):
                nc.scalar.copy(Qt[:, 0].rearrange("p b (t h) -> p b t h", h=QH)[:, :, :, h],
                               take("Qt", h)[:, 0:B * N].rearrange("p (b t) -> p b t", t=N)).then_inc(emptied_a, 1)
                if h == 0:
                    nc.scalar.activation(warm[:], ident[:, 0:1], ACT.Exp)

            prob_t, o_bank, misc = ps[:, NB:2 * NB], ps[:, 6], ps[:, 7]

            def tile_step(i, j, first=False, parts="HEOC"):
                n = PAIR * i + j
                b = 2 * i + j // QT
                u = j % QT - (QT - NB)
                if "C" in parts and u >= 0:
                    act.wait_ge(cT_trans, NB * b + u + 1)
                    copy_cT((j // QT + 1) % 2, u, misc.bitcast(F16)).then_inc(cT_copied, 1)
                if "H" in parts and not (first and j < 1):
                    if not (first and j < 3):
                        act.wait_ge(pv_done, n - 2)
                    for k in range(NB):
                        act.wait_ge(p_trans, NB * (n - 1) + k + 1)
                        nc.scalar.copy(pT[0:KP, (j - 1) % 2, 0, 512 * k:512 * (k + 1)],
                                       prob_t[0:KP, k, :]).then_inc(p_high, 1)
                if "E" in parts:
                    act.wait_ge(bias_ready, n + 1)
                    if not (first and j < 2):
                        act.wait_ge(recip_ready, n - 1)
                    nc.scalar.activation(sc[:, j % 2, :], sc[:, j % 2, :], ACT.Exp, bias=nb[:, j % 2:j % 2 + 1],
                                         scale=1.0 / M_UP, accum_out=rs[:, j % 2:j % 2 + 1]).then_inc(exp_done, 1)
                if "O" in parts and not (first and j < 2):
                    act.wait_ge(recip_ready, n - 1)
                    if not (first and j < 4):
                        act.wait_ge(o_norm, n - 3)
                    act.wait_ge(pv_done, n - 1)
                    nc.scalar.activation(o2[:, j % 2, :], o_bank[:, D:2 * D], ACT.Copy,
                                         scale=rr[:, j % 2:j % 2 + 1]).then_inc(o2_done, 1)
                if "O" in parts or "X" in parts:
                    if not (first and j < 3):
                        if first and j == 3:
                            act.wait_ge(oT_zero, 1)
                        if j == 3 and not first:
                            act.wait_ge(proj_done, i)
                        act.wait_ge(o_trans, n - 2)
                        m = (j - 3) % PAIR
                        nc.scalar.copy(oT[:, 0, m // QT, P * (m % QT):P * (m % QT + 1)], misc[:, 0:P]).then_inc(oT_copied, 1)

            for u in range(NB):
                front_wait(act, "cT", u)
            nc.scalar.sem_inc(cT_copied, NB)
            for j in range(PAIR):
                tile_step(0, j, first=True)
            with act.Fori(1, NT) as i:
                for j in range(PAIR):
                    tile_step(i, j)
            tile_step(NT, 0, parts="HO")
            tile_step(NT, 1, parts="O")
            tile_step(NT, 2, parts="X")
            std(2, slice(0, NT - 1))
            std(3, slice(NT - 1, NT))

            def take2(name, i=0):
                f = mid.at(name, i)
                act.wait_ge(filled2, f + 1)
                return ps[:, f % 8, :]

            nc.scalar.copy(x1T[:, 1, :], take2("x2T", 1)).then_inc(emptied2_a, 1)
            nc.scalar.activation(r1[:].rearrange("p a b -> p (a b)"), take2("logit")[:, 0:NT * E],
                                 ACT.Sigmoid).then_inc(emptied2_a, 1)
            for j in range(NT):
                o = take2("shgu", j)
                nc.scalar.activation(sh_g[:, j, :], o[:, 0:F], ACT.Silu)
                nc.scalar.copy(sh_u[:, j, :], o[:, F:2 * F]).then_inc(emptied2_a, 1)
            nc.scalar.copy(sh_hT[:], take2("shT")[0:F, :]).then_inc(emptied2_a, 1)
            for j in range(NT):
                nc.scalar.copy(x_sb[:, j, :], take2("shy", j)[:, 0:C]).then_inc(emptied2_a, 1)

            gu_bank, xs_bank, dn_bank = ps[:, 3:5], ps[:, 2], ps[:, 6]

            def move_rows(g, par, c):
                act.wait_ge(xs_filled, CC * g + c + 1)
                nc.scalar.copy(xs[:, par, c, :, 0:CAP],
                               xs_bank[:, 0:GE * CAP].rearrange("p (e s) -> p e s", s=CAP)).then_inc(xs_copied, 1)

            def pair_step(i, q, first=False, parts="GN"):
                n = 2 * GP * i + q
                if "G" in parts:
                    act.wait_ge(gu_filled, n + 1)
                    if not (first and q < 2):
                        act.wait_ge(h_ready, n - 1)
                    nc.scalar.activation(act_g[:, q % 2, :], gu_bank[:, q % 2, 0:F],
                                         ACT.Silu).then_inc(silu_done, 1)
                    if q % 2 == 1:
                        move_rows(2 * i + q // GP + 1, (q // GP + 1) % 2, q % GP // 2)
                if "N" in parts and not (first and q < 1):
                    g1, dq = 2 * i + (q - 1) // GP, (q - 1) % GP
                    act.wait_ge(dn_filled, n)
                    act.wait_ge(w_copied, g1 + 1)
                    if not (first and q < 3):
                        act.wait_ge(comb_done, n - 2)
                    nc.scalar.activation(o_hl[:, (q - 1) % 2, 0, :], dn_bank[:, 0:C], ACT.Copy,
                                         scale=ws_slot[:, g1_par(q), dq:dq + 1]).then_inc(o_high, 1)
            def g1_par(q):
                return ((q - 1) // GP) % 2

            for c in range(CC):
                move_rows(0, 0, c)
            for q in range(2 * GP):
                pair_step(0, q, first=True)
            with act.Fori(1, NG // 2) as i:
                for q in range(2 * GP):
                    pair_step(i, q)
            pair_step(NG // 2, 0, parts="N")
            act.wait_ge(y_filled, 2)
            nc.scalar.copy(yT_sb[:, 0, :], ps[:, 0, :]).then_inc(y_copied_a, 1)
            std(4)

        @block.vector
        def _(dve):
            steps = [0]

            def chained(ins):
                steps[0] += 1
                ins.then_inc(dve_step, 1)
                dve.wait_ge(dve_step, steps[0])

            def take(name, i=0):
                f = front.at(name, i)
                dve.wait_ge(filled, f + 1)
                return ps[:, f % 8, :]

            def mine(name):
                return [i for i, f in enumerate(front.where[name]) if front.takes("v", f)]

            def norm(src, dst, k, tiles=range(NT)):
                w = slice(tiles[0], tiles[-1] + 1)
                for j in tiles:
                    last = nc.vector.bn_stats(st[:, j, :], src[:, j, :])
                chained(last)
                for j in tiles:
                    last = nc.vector.bn_aggr(mv[:, j, :], st[:, j, :])
                chained(last)
                nc.vector.tensor_scalar(ve[:, w], mv[:, w, 1], LN_EPS, None, ALU.add).then_inc(ln_var, 1)
                dve.wait_ge(ln_std, k)
                chained(nc.vector.reciprocal(rstd[:, w], sd[:, w]))
                for j in tiles:
                    nc.vector.tensor_scalar(dst[:, j, :], src[:, j, :], mv[:, j, 0:1], rstd[:, j:j + 1],
                                            ALU.subtract, ALU.mult).then_inc(ln_out, 1)

            chained(nc.vector.memset(x_sb[32:64, :, :], 0.0))
            nc.vector.memset(x_sb[96:128, :, :], 0.0).then_inc(pads_zero, 1)
            nc.vector.memset(v_aug[:, :, :, HD:VW], 1.0).then_inc(dve_const, 1)

            for i in mine("wqkvT"):
                nc.vector.tensor_copy(wqkvT[:, i % 2, 384 * (i // 2):384 * (i // 2 + 1)],
                                      take("wqkvT", i)[:, 0:384]).then_inc(emptied_v, 1)
            for c in mine("xT"):
                nc.vector.tensor_copy(xT[:, c, :], take("xT", c)).then_inc(emptied_v, 1)
            for c in mine("qT"):
                nc.vector.tensor_scalar(qT[:, c, :], take("qT", c), 0.0, None, ALU.max).then_inc(emptied_v, 1)
            dve.wait_ge(dve_const, 1)
            for j in mine("kv"):
                o = take("kv", j)
                dve.wait_ge(emptied_a, front.emptied("a", front.at("kv", j)))
                nc.vector.tensor_scalar(k_sb[:, j, :], o[:, 0:C], 0.0, None, ALU.max).then_inc(emptied_v, 1)
            for i in mine("WkT"):
                nc.vector.tensor_copy(wkT[:, 4 * i:4 * i + 4, :].rearrange("p a b -> p (a b)"),
                                      take("WkT", i)).then_inc(emptied_v, 1)
            dve.wait_ge(consts_set, 8)
            for b in range(B):
                w = HC * VW
                nc.vector.tensor_tensor(kvm[:, b, :].rearrange("p (c w) -> p c w", w=w),
                                        take("G", b)[:, 0:CC * w].rearrange("p (c w) -> p c w", w=w),
                                        headmask[:].rearrange("p h v -> p (h v)").unsqueeze(1).to_broadcast([P, CC, w]),
                                        ALU.mult).then_inc(emptied_v, 1)
            for i in mine("WqT"):
                nc.vector.tensor_copy(wqT[:, 2 * i:2 * i + 2].rearrange("p a b c -> p (a b c)"),
                                      take("WqT", i)).then_inc(emptied_v, 1)
            dve.wait_ge(bproj_dma, 16)
            chained(nc.vector.tensor_tensor(x_sb[:], x_sb[:], bproj[:].unsqueeze(1).to_broadcast([P, NT, C]), ALU.add))
            for j in range(NT):
                o = take("lin", j)[:, 0:LH * VW].rearrange("p (h v) -> p h v", v=VW)
                chained(nc.vector.tensor_scalar(den[:, j, :], o[:, :, HD], DEN_EPS, None, ALU.add))
                chained(nc.vector.reciprocal(den[:, NT + j, :], den[:, j, :]))
                last = nc.vector.tensor_tensor(ao[:, j, :].rearrange("p (h d) -> p h d", d=HD), o[:, :, 0:HD],
                                               den[:, NT + j, :].unsqueeze(2).to_broadcast([P, LH, HD]), ALU.mult)
                last.then_inc(emptied_v, 1)
            dve.wait_ge(emptied_v, front.emptied("v", front.at("lin", NT - 1)))
            nc.vector.sem_inc(ao_ready, 1)
            for i in mine("M"):
                o = take("M", i)
                dve.wait_ge(emptied_a, front.emptied("a", front.at("M", i)))
                nc.vector.scalar_tensor_tensor(M[:, 1, 2 * i:2 * i + 2].rearrange("p a b c -> p (a b c)"), o,
                                               M_UP * D ** -0.5, M[:, 0, 2 * i:2 * i + 2].rearrange("p a b c -> p (a b c)"),
                                               ALU.mult, ALU.subtract).then_inc(emptied_v, 1)
            for c in mine("aoT"):
                nc.vector.tensor_copy(aoT[:, c, :], take("aoT", c)).then_inc(emptied_v, 1)
            for j in range(NT):
                last = nc.vector.tensor_tensor(x_sb[:, j, :], x_sb[:, j, :], take("proj", j)[:, 0:C], ALU.add)
                last.then_inc(emptied_v, 1)
            dve.wait_ge(emptied_v, front.emptied("v", front.at("proj", NT - 1)))
            norm(x_sb, x1, 1)

            def low_W2(i):
                o = take("W2", i)
                dve.wait_ge(emptied_a, front.emptied("a", front.at("W2", i)))
                hi, lo = (W2[:, s, 2 * i:2 * i + 2, :].rearrange("p a b -> p (a b)") for s in range(2))
                nc.vector.scalar_tensor_tensor(lo, o, W_UP, hi, ALU.mult, ALU.subtract).then_inc(emptied_v, 1)

            for i in EARLY_W2:
                low_W2(i)
            for c in mine("x1T"):
                o = take("x1T", c)
                dve.wait_ge(emptied_a, front.emptied("a", front.at("x1T", c)))
                nc.vector.tensor_tensor(x1T16[:, 1, c, :], o, x1T16[:, 0, c, :], ALU.subtract).then_inc(emptied_v, 1)
            for u in mine("cT"):
                nc.vector.tensor_copy(
                    cT[:, 0, :, KB * u:KB * (u + 1)].rearrange("p s (t k) -> p s t k", k=KP),
                    take("cT", u).bitcast(F16).rearrange("p (s t k) -> p s t k", s=2, k=P)[:, :, :, 0:KP]
                ).then_inc(emptied_v, 1)
            for i in LATE_W2:
                low_W2(i)
            for h in range(QH):
                o = take("Qt", h)[:, 0:B * N].rearrange("p (b t) -> p b t", t=N)
                dve.wait_ge(emptied_a, front.emptied("a", front.at("Qt", h)))
                hi, lo = (Qt[:, s].rearrange("p b (t h) -> p b t h", h=QH)[:, :, :, h] for s in range(2))
                nc.vector.tensor_tensor(lo, o, hi, ALU.subtract).then_inc(emptied_v, 1)

            score, prob_t, o_bank, misc = ps[:, 0:NB], ps[:, NB:2 * NB], ps[:, 6], ps[:, 7]

            def tile_step(i, j, first=False, parts="SRLO"):
                n = PAIR * i + j
                b, par, tp = 2 * i + j // QT, (j // QT) % 2, j % 2
                if "S" in parts:
                    if j % QT == 0:
                        wait_alone(dve, mask_bias, b + 1)
                    if not (first and j < 2):
                        wait_alone(dve, p_trans, NB * (n - 1))
                    for k in range(NB):
                        keys = slice(KB * k, KB * (k + 1))
                        wait_alone(dve, scored, NB * n + k + 1)
                        nc.vector.tensor_tensor_reduce(out=sc[:, tp, keys], in0=score[:, k, 0:KB], in1=mb[:, par, keys],
                                                       scale=1.0, scalar=-3e38, op0=ALU.add, op1=ALU.max,
                                                       accum_out=mx3[:, tp, k:k + 1]).then_inc(masked, 1)
                    dve.wait_ge(masked, NB * (n + 1))
                    nc.vector.tensor_reduce(mxa[:, tp:tp + 1], mx3[:, tp, :], AX.X, ALU.max).then_inc(row_max, 1)
                    dve.wait_ge(row_max, n + 1)
                    nc.vector.tensor_scalar(nb[:, tp:tp + 1], mxa[:, tp:tp + 1], -1.0 / M_UP, LOG_P,
                                            ALU.mult, ALU.add).then_inc(bias_ready, 1)
                if "R" in parts and not (first and j < 1):
                    op = (j - 1) % 2
                    dve.wait_ge(exp_done, n)
                    nc.vector.reciprocal(rinv[:, op:op + 1], rs[:, op:op + 1]).then_inc(recip1, 1)
                    dve.wait_ge(recip1, n)
                    nc.vector.scalar_tensor_tensor(rr[:, op:op + 1], mxa[:, op:op + 1], -0.5 * BIG, rinv[:, op:op + 1],
                                                   ALU.is_gt, ALU.mult).then_inc(recip_ready, 1)
                if j == 3 and not first:
                    add_pair(i - 1)
                if "L" in parts and not (first and j < 1):
                    if not (first and j < 3):
                        dve.wait_ge(pv_done, n - 2)
                    for k in range(NB):
                        part = slice(512 * k, 512 * (k + 1))
                        dve.wait_ge(p_high, NB * (n - 1) + k + 1)
                        nc.vector.tensor_tensor(pT[0:KP, (j - 1) % 2, 1, part], prob_t[0:KP, k, :],
                                                pT[0:KP, (j - 1) % 2, 0, part], ALU.subtract).then_inc(p_low, 1)
                if "O" in parts and not (first and j < 2):
                    dve.wait_ge(o2_done, n - 1)
                    if not (first and j < 4):
                        dve.wait_ge(o_trans, n - 3)
                    nc.vector.scalar_tensor_tensor(on[:, tp, :], o_bank[:, 0:D], rr[:, tp:tp + 1], o2[:, tp, :],
                                                   ALU.mult, ALU.add).then_inc(o_norm, 1)
                if ("O" in parts or "X" in parts) and not (first and j < 3):
                    m = (j - 3) % PAIR
                    at = slice(P * (m % QT), P * (m % QT + 1))
                    dve.wait_ge(oT_copied, n - 2)
                    nc.vector.tensor_tensor(oT[:, 1, m // QT, at], misc[:, 0:P], oT[:, 0, m // QT, at],
                                            ALU.subtract).then_inc(oT_low, 1)

            def add_pair(i):
                dve.wait_ge(proj_done, i + 1)
                nc.vector.scalar_tensor_tensor(x_sb[:, bass.ds(i, 1), :].rearrange("p a c -> p (a c)"), o_bank[:, C:2 * C],
                                               1.0 / W_UP, x1[:, bass.ds(i, 1), :].rearrange("p a c -> p (a c)"),
                                               ALU.mult, ALU.add).then_inc(pair_sum, 1)

            for j in range(PAIR):
                tile_step(0, j, first=True)
            with dve.Fori(1, NT) as i:
                for j in range(PAIR):
                    tile_step(i, j)
            tile_step(NT, 0, parts="RLO")
            tile_step(NT, 1, parts="O")
            tile_step(NT, 2, parts="X")
            norm(x_sb, x1, 2, range(NT - 1))
            add_pair(NT - 1)
            dve.wait_ge(pair_sum, NT)
            norm(x_sb, x1, 3, range(NT - 1, NT))
            dve.wait_ge(ln_out, 2 * NT)

            def take2(name, i=0):
                f = mid.at(name, i)
                dve.wait_ge(filled2, f + 1)
                return ps[:, f % 8, :]

            nc.vector.tensor_copy(x1T[:, 0, :], take2("x2T", 0)).then_inc(emptied2_v, 1)
            x2v = x1[:].rearrange("p j (m k) -> p j k m", k=CC)
            for j in range(NT):
                last = nc.vector.tensor_copy(x2h[:, 0, j], x2v[:, j])
            chained(last)
            for j in range(NT):
                nc.vector.tensor_tensor(x2h[:, 1, j], x2v[:, j], x2h[:, 0, j], ALU.subtract).then_inc(x2_split, 1)

            mid_wait(dve, "logit")
            dve.wait_ge(small_dma, 16 * 5)
            chained(nc.vector.tensor_tensor(r2[:], r1[:], gbias[:].unsqueeze(1).to_broadcast([P, NT, E]), ALU.add))
            for j in range(NT):
                for g in range(G):
                    last = nc.vector.max(m8[:, G * j + g, :], r2[:, j, EG * g:EG * (g + 1)])
            chained(last)
            dve.wait_ge(tiles_set, 8)
            chained(nc.vector.tensor_tensor(gs[:, :, 0:G], m8[:, :, 0].rearrange("p (j g) -> p j g", g=G),
                                            m8[:, :, 1].rearrange("p (j g) -> p j g", g=G), ALU.add))
            for j in range(NT):
                last = nc.vector.max(m8[:, j, :], gs[:, j, 0:G])
            chained(last)
            chained(nc.vector.tensor_copy(t8[:, :, 0:KG], m8[:, 0:NT, 0:KG]))
            for j in range(NT):
                last = nc.vector.match_replace(gsr[:, j, :], t8[:, j, :], gs[:, j, :], -3 * BIG)
            chained(last)
            chained(nc.vector.tensor_tensor(gsel[:], gs[:, :, 0:G], gsr[:, :, 0:G], ALU.not_equal))
            chained(nc.vector.tensor_scalar(gpen[:], gsel[:], BIG, -BIG, ALU.mult, ALU.add))
            for j in range(NT):
                last = nc.vector.tensor_tensor(r3[:, j, 0:E].rearrange("p (g e) -> p g e", e=EG),
                                               r2[:, j, :].rearrange("p (g e) -> p g e", e=EG),
                                               gsel[:, j, :].unsqueeze(2).to_broadcast([P, G, EG]), ALU.mult)
            chained(last)
            for j in range(NT):
                last = nc.vector.tensor_tensor(r3[:, j, 0:E].rearrange("p (g e) -> p g e", e=EG),
                                               r3[:, j, 0:E].rearrange("p (g e) -> p g e", e=EG),
                                               gpen[:, j, :].unsqueeze(2).to_broadcast([P, G, EG]), ALU.add)
            chained(last)
            for j in range(NT):
                last = nc.vector.max(m8[:, NT + j, :], r3[:, j, 0:E])
            chained(last)
            chained(nc.vector.tensor_copy(t6[:, :, 0:TOPK], m8[:, NT:2 * NT, 0:TOPK]))
            for j in range(NT):
                last = nc.vector.match_replace(r4[:, j, :], t6[:, j, :], r3[:, j, :], -3 * BIG)
            chained(last)
            chained(nc.vector.tensor_tensor(r2[:], r3[:, :, 0:E], r4[:, :, 0:E], ALU.not_equal))
            chained(nc.vector.tensor_tensor(r1[:], r1[:], r2[:], ALU.mult))
            chained(nc.vector.tensor_scalar(sel16[:], r2[:], valid[:, 0:1], None, ALU.mult))
            nc.vector.sem_inc(routed, 1)
            nc.vector.tensor_scalar(r2[:], sel16[:], -1000.0, 1000.0, ALU.mult, ALU.add)
            chained(nc.vector.tensor_reduce(wsum[:], r1[:], AX.X, ALU.add))
            chained(nc.vector.reciprocal(wrec[:], wsum[:]))
            nc.vector.tensor_tensor(posm[:, :, 0:E], take2("pos")[:, 0:NT * E].rearrange("p (j e) -> p j e", e=E),
                                    r2[:], ALU.add).then_inc(emptied2_v, 1)
            mid_wait(dve, "pos")

            def build(g, par, half):
                for j in (2 * half, 2 * half + 1):
                    last = nc.vector.tensor_tensor(disp[:, par, j, :, 0:CAP],
                                                   posm[:, j, bass.ds(GE * g, GE)].unsqueeze(2).to_broadcast([P, GE, CAP]),
                                                   slots[:].unsqueeze(1).to_broadcast([P, GE, CAP]), ALU.is_equal)
                last.then_inc(disp_built, 1)

            def group_weights(g, par):
                nc.vector.tensor_copy(w_grp[:, par], w16[:, :, bass.ds(GE * g, GE), :]).then_inc(w_built, 1)

            build(0, 0, 0)
            build(0, 0, 1)
            chained(nc.vector.tensor_tensor(r1[:], r1[:], wrec[:].unsqueeze(2).to_broadcast([P, NT, E]), ALU.mult))
            chained(nc.vector.tensor_scalar(r1[:], r1[:], SCALE, None, ALU.mult))
            chained(nc.vector.tensor_copy(w16[:, :, 0:E, 0], r1[:]))
            chained(nc.vector.tensor_tensor(w16[:, :, 0:E, 1], r1[:], w16[:, :, 0:E, 0], ALU.subtract))
            group_weights(0, 0)
            build(1, 1, 0)

            gu_bank, misc2, dn_bank, dT_bank = ps[:, 3:5], ps[:, 5], ps[:, 6], ps[:, 7]

            def move_weights(g, par):
                dve.wait_ge(w_filled, g + 1)
                wv4 = misc2[:, C:C + 4 * GP].rearrange("p (q e s) -> p q e s", e=2, s=2)
                for s in range(2):
                    last = nc.vector.tensor_reduce(ws_slot[SLOT * s:SLOT * (s + 1), par, :],
                                                   wv4[SLOT * s:SLOT * (s + 1), :, s, :], AX.X, ALU.add)
                last.then_inc(w_copied, 1)

            def pair_step(i, q, first=False, parts="GTN"):
                n = 2 * GP * i + q
                if "T" in parts and not (first and q < 1):
                    dve.wait_ge(hT_filled, n)
                    if not (first and q < 3):
                        dve.wait_ge(dn_filled, n - 2)
                    nc.vector.tensor_copy(hT[:, (q - 1) % 2, :], misc2[0:F, 0:P]).then_inc(hT_copied, 1)
                if "G" in parts:
                    dve.wait_ge(dT_filled, n + 1)
                    if not (first and q < GP):
                        dve.wait_ge(comb_done, n - GP + 1)
                    nc.vector.tensor_copy(dispT[:, q % GP, :],
                                          dT_bank.bitcast(F16)[:, 512 * (q % 2):512 * (q % 2 + 1)]).then_inc(dT_copied, 1)
                    dve.wait_ge(silu_done, n + 1)
                    if not (first and q < 2):
                        dve.wait_ge(hT_filled, n - 1)
                    nc.vector.tensor_tensor(h_sb[:, q % 2, :], act_g[:, q % 2, :],
                                            gu_bank[:, q % 2, F:2 * F], ALU.mult).then_inc(h_ready, 1)
                    if q % GP == 0:
                        group_weights(2 * i + q // GP + 1, (q // GP + 1) % 2)
                        build(2 * i + q // GP + 1, (q // GP + 1) % 2, 1)
                    if q % GP == GP - 1:
                        move_weights(2 * i + q // GP + 1, (q // GP + 1) % 2)
                        build(2 * i + q // GP + 2, (q // GP) % 2, 0)
                if "N" in parts and not (first and q < 1):
                    g1p, dq = ((q - 1) // GP) % 2, (q - 1) % GP
                    dve.wait_ge(o_high, n)
                    nc.vector.scalar_tensor_tensor(o_hl[:, (q - 1) % 2, 1, :], dn_bank[:, 0:C],
                                                   ws_slot[:, g1p, dq:dq + 1], o_hl[:, (q - 1) % 2, 0, :],
                                                   ALU.mult, ALU.subtract).then_inc(o_low, 1)

            move_weights(0, 0)
            for q in range(2 * GP):
                pair_step(0, q, first=True)
            with dve.Fori(1, NG // 2) as i:
                for q in range(2 * GP):
                    pair_step(i, q)
            pair_step(NG // 2, 0, parts="TN")
            dve.wait_ge(y_filled, 2)
            nc.vector.tensor_copy(yT_sb[:, 1, :], ps[:, 1, :]).then_inc(y_copied, 1)
            dve.wait_ge(x2_summed, 1)
            dve.wait_ge(yb_filled, 1)
            for j in range(NT):
                last = nc.vector.tensor_tensor(x_sb[:, j, :], x_sb[:, j, :],
                                               ps[:, 2 + j // 2, C * (j % 2):C * (j % 2 + 1)], ALU.add)
            chained(last)
            norm(x_sb, x1, 4)


_INS = ["x", "ctx_1024", "mask_BxS2_bf1", "L0_attn_w_qkv", "L0_attn_w_proj", "L0_attn_b_proj", "L0_xattn_Wq",
        "L0_xattn_Wk", "L0_xattn_Wv", "L0_xattn_Wo", "L0_ffn_gate_w", "L0_ffn_bias", "L0_ffn_w_gate", "L0_ffn_w_up",
        "L0_ffn_w_down", "L0_ffn_ws_gate", "L0_ffn_ws_up", "L0_ffn_ws_down"]


def kernel(**inputs):
    import numpy as np
    import concourse.bacc as bacc
    from concourse.bass_utils import run_bass_kernel_spmd

    nc = bacc.Bacc("TRN2", target_bir_lowering=False, num_devices=1)
    arrays, args = {}, []
    for name in _INS:
        a = np.ascontiguousarray(inputs[name])
        if a.dtype == np.bool_:
            a = a.view(np.uint8)
        arrays[f"in_{name}"] = a
        args.append(nc.dram_tensor(f"in_{name}", a.shape, mybir.dt.from_np(a.dtype), kind="ExternalInput").ap())
    y = nc.dram_tensor("y", (B, N, C), F32, kind="ExternalOutput").ap()
    decoder_kernel(nc, *args, y)
    r = run_bass_kernel_spmd(nc, [arrays], core_ids=[0])
    return r.results[0]["y"]
```

```python
from contextlib import ExitStack

import concourse.bass as bass
from concourse import mybir

F32 = mybir.dt.float32
F16 = mybir.dt.float16
BF16 = mybir.dt.bfloat16
U8 = mybir.dt.uint8
I32 = mybir.dt.int32
ALU = mybir.AluOpType
ACT = mybir.ActivationFunctionType
AX = mybir.AxisListType

P = 128
B, N, C = 8, 56, 256
NT = B // 2
HALF = 64
CC = C // P
HD = 32
LH = C // HD
HC = P // HD
VW = HD + 1
SK, D = 1500, 128
KT, KP = 12, 125
QH, GH = 16, 8
NQ = N * QH
QT = NQ // P
NB = 3
KB = SK // NB
TB = KT // NB
PAIR = 2 * QT
TILES = B * QT
E, TOPK, G, KG, F = 64, 6, 8, 4, 96
EG = E // G
CAP = 2 * (2 * 128 * TOPK // E)
SLOT = 64
GE = 8
NG = E // GE
GP = GE // 2
SCALE = 2.5
CHOSEN = 1000
LN_EPS, DEN_EPS = 1e-5, 1e-15
BIG = 1e30
LOG_P = 6.931471805599453
IN_UP = 16.0
M_UP, W_UP = 64.0, 256.0

M_SCALE = M_UP * D ** -0.5 / IN_UP ** 2
HALVES = ((0, 0), (0, 1), (1, 0))
PASSES = [(c, a, b) for c in range(CC) for a, b in HALVES]

FRONT = [("wqkvT", 4, "b"), ("xT", 2, "b"), ("wpT", 1, "a"), ("WkT", 2, "b"), ("qT", 2, "va"), ("kv", 4, "b"),
         ("WqT", 8, "b"), ("G", 8, "v"), ("M", 4, "b"), ("lin", 4, "v"), ("M", 4, "b"),
         ("aoT", 2, "a"), ("WvT", 2, "a"), ("proj", 4, "v"), ("W2", 4, "b"), ("x1T", 2, "b"),
         ("cT", NB, "av"), ("W2", 2, "b"), ("Qt", 16, "b"), ("W2", 2, "b")]
MID = [("x2T", 2, "av"), ("logit", 1, "a"), ("shgu", 2, "a"), ("x2T", 1, "v"), ("logit", 1, "a"), ("shgu", 2, "a"),
       ("pos", 1, "v"), ("shT", 1, "a"), ("shy", 2, "a")]
BEFORE, LAST = slice(0, NT - 1), slice(NT - 1, NT)
EARLY_W2, MIDDLE_W2, LATE_W2 = range(4), range(4, 6), range(6, 8)


class Fills:

    def __init__(self, plan):
        self.where, self.by = {}, []
        for name, n, engines in plan:
            self.where.setdefault(name, []).extend(range(len(self.by), len(self.by) + n))
            self.by += [engines[i % len(engines)] for i in range(n)]

    def at(self, name, i=0):
        return self.where[name][i]

    def emptied(self, engine, f):
        return sum(e in (engine, "b") for e in self.by[:f + 1])

    def takes(self, engine, f):
        return self.by[f] in (engine, "b")


def decoder_kernel(nc, x, ctx, mask, w_qkv, w_proj, b_proj, Wq, Wk, Wv, Wo, gate_w, bias,
                   w_gate, w_up, w_down, ws_gate, ws_up, ws_down, out):
    with ExitStack() as stack:
        def sb(name, shape, dt):
            return stack.enter_context(nc.sbuf_tensor(name, shape, dt))

        def sem(name):
            return stack.enter_context(nc.semaphore(name))

        def carver(region):
            at = [0]

            def carve(shape, dt, size):
                n = 1
                for s in shape:
                    n *= s
                words = (n * size + 3) // 4
                v = region[:, at[0]:at[0] + words]
                at[0] += words
                if dt != F32:
                    v = v.bitcast(dt)
                names = "abcde"[:len(shape)]
                if len(shape) > 1:
                    v = v.rearrange(f"p ({' '.join(names)}) -> p {' '.join(names)}",
                                    **{c: s for c, s in zip(names, shape)})
                return v
            return carve

        ra = sb("ra", [P, 76 * 256], F32)
        cut = carver(ra)
        wq_in = cut([CC, QH * D], F32, 4)
        wqT = cut([2, QH, CC, P], F16, 2)
        wo_in = cut([QH, C], F32, 4)
        wqkv_in = cut([6, C], F32, 4)
        wqkvT = cut([CC, 2, 3 * C], F16, 2)
        wk_in = cut([GH, D], F32, 4)
        wv_in = cut([GH, D], F32, 4)
        wkT = cut([2, GH, D], F16, 2)
        wvT = cut([GH, D], F32, 4)
        M = wq_in.bitcast(F16).rearrange("p s (h b c) -> p s h b c", b=CC, c=D)
        cut = carver(ra)
        sc = cut([2, SK], F32, 4)
        pT = cut([2, 2, KT * P], F16, 2)
        w_gu = cut([2, 2, GE, CC * F], F32, 4)
        w_dn = cut([2, GE, C], F32, 4)
        rb = sb("rb", [P, 29 * 256], F32)
        cut = carver(rb)
        qT = cut([CC, NT * P], F32, 4)
        k_sb = cut([NT, C], F32, 4)
        v_aug = cut([NT, LH, VW], F32, 4)
        kvm = cut([B, CC * HC * VW], F32, 4)
        ao = cut([NT, C], F32, 4)
        aoT = cut([CC, NT * P], F32, 4)
        cut = carver(rb)
        cT = cut([2, 2, SK], F16, 2)
        oT = cut([2, 2, HALF * QH], F16, 2)
        q_st = cut([2, 2, NQ], F16, 2)
        rc = sb("rc", [P, 30 * 256], F32)
        cut = carver(rc)
        Qt = cut([2, B, NQ], F16, 2)
        cut = carver(rc)
        x2h = cut([2, NT, CC, P], F16, 2)
        disp = cut([2, NT, GE, SLOT], F16, 2)
        xs = cut([2, CC, GE, SLOT], F32, 4)
        dispT = cut([GP, NT * P], F16, 2)
        w_grp = cut([2, NT, GE, 2], F16, 2)
        ws_slot = cut([2, GP], F32, 4)
        yT_sb = cut([CC, NT * P], F32, 4)
        c_in = sb("c_in", [KP, KT, D], F32)
        c16 = sb("c16", [KP, 2, KT, 2, D], F16)
        m_in = sb("m_in", [P, SK], U8)
        mb = sb("mb", [P, 2, SK], BF16)
        W2 = sb("W2", [P, 2, QH, C], F16)
        x_sb = sb("x_sb", [P, NT, C], F32)
        xT = sb("xT", [P, CC, 2, NT * P], F16)
        x1 = sb("x1", [P, NT, C], F32)
        x1T = sb("x1T", [P, CC, NT * P], F32)
        x1T16 = x1T[:].bitcast(F16).rearrange("p s (a t) -> p s a t", a=CC)
        wp_in = sb("wp_in", [P, CC, C], F32)
        wpT = sb("wpT", [P, CC, C], F32)
        bproj = sb("bproj", [P, C], F32)
        ident = sb("ident", [P, P], F32)
        ident16 = sb("ident16", [P, P], F16)
        ones16 = sb("ones16", [P, P], F16)
        before = sb("before", [P, P], F16)
        zero16 = sb("zero16", [P, NT * P], F16)
        headmask = sb("headmask", [P, HC, VW], F32)
        slots_i = sb("slots_i", [P, CAP], I32)
        slots = sb("slots", [P, CAP], F16)
        in_batch = sb("in_batch", [P, 2], F32)
        valid = sb("valid", [P, 1], F32)
        mx3 = sb("mx3", [P, 2, NB], F32)
        mxa = sb("mxa", [P, 2], F32)
        nb = sb("nb", [P, 2], F32)
        rs = sb("rs", [P, 2], F32)
        rinv = sb("rinv", [P, 2], F32)
        rr = sb("rr", [P, 2], F32)
        o2 = sb("o2", [P, 2, D], F32)
        warm = sb("warm", [P, 5], F32)
        on = sb("on", [P, 2, D], F32)
        den = sb("den", [P, 2 * NT, LH], F32)
        st = sb("st", [P, NT, 6], F32)
        mv = sb("mv", [P, NT, 2], F32)
        ve = sb("ve", [P, NT], F32)
        sd = sb("sd", [P, NT], F32)
        rstd = sb("rstd", [P, NT], F32)
        gw = sb("gw", [P, CC, E], F32)
        gbias = sb("gbias", [P, E], F32)
        wsgu = sb("wsgu", [P, CC, 2, F], F32)
        wsd = sb("wsd", [F, C], F32)
        cut = carver(rb)
        r1 = cut([NT, E], F32, 4)
        r2 = cut([NT, E], F32, 4)
        r3 = cut([NT, E + 2], F32, 4)
        r4 = cut([NT, E + 2], F32, 4)
        m8 = cut([NT * G, 8], F32, 4)
        gs = cut([NT, G + KG], F32, 4)
        gsr = cut([NT, G + KG], F32, 4)
        t8 = cut([NT, 8], F32, 4)
        t6 = cut([NT, 8], F32, 4)
        gsel = cut([NT, G], F32, 4)
        gpen = cut([NT, G], F32, 4)
        sel16 = cut([NT, E], F16, 2)
        w16 = cut([NT, E, 2], F16, 2)
        posm = cut([NT, E], F16, 2)
        wsum = cut([NT], F32, 4)
        wrec = cut([NT], F32, 4)
        sh_s = cut([NT, F], F32, 4)
        sh_gu = cut([NT, 2 * F], F32, 4)
        sh_h = cut([NT, F], F32, 4)
        sh_hT = cut([NT * P], F32, 4)[0:F]
        act_g = cut([2, F], F32, 4)
        h_sb = cut([2, F], F32, 4)
        hT = cut([2, P], F32, 4)[0:F]
        o_hl = cut([2, 2, C], F16, 2)

        ps = stack.enter_context(nc.psum_tensor("ps", [P, 8, 512], F32))

        x_in, wp_dma, wk_dma, wq_dma, wv_dma, wo_dma, small_dma = (
            sem(n) for n in ("x_in", "wp_dma", "wk_dma", "wq_dma", "wv_dma", "wo_dma", "small_dma"))
        wqkv_dma = [sem("wqkv_dma0"), sem("wqkv_dma1")]
        bproj_dma, x_biased = sem("bproj_dma"), sem("x_biased")
        tiles_set = sem("tiles_set")
        oT_low = sem("oT_low")
        ctx_dma, mask_dma = sem("ctx_dma"), sem("mask_dma")
        ew_dma = [sem("ew_dma0"), sem("ew_dma1")]
        out_dma = [sem("out_dma0"), sem("out_dma1")]
        pads_zero = sem("pads_zero")
        const_step = sem("const_step")
        consts_set = sem("consts_set")
        zero_set = sem("zero_set")
        dve_const = sem("dve_const")
        filled, emptied_v, emptied_a = sem("filled"), sem("emptied_v"), sem("emptied_a")
        filled2, emptied2_v, emptied2_a = sem("filled2"), sem("emptied2_v"), sem("emptied2_a")
        dve_step = sem("dve_step")
        act_step = sem("act_step")
        ln_var, ln_std, ln_out = sem("ln_var"), sem("ln_std"), sem("ln_out")
        ao_ready = sem("ao_ready")
        ctx_high = sem("ctx_high")
        ctx_split, mask_bias, q_staged, oT_zero = sem("ctx_split"), sem("mask_bias"), sem("q_staged"), sem("oT_zero")
        scored, p_trans, pv_done, o_trans, cT_trans, proj_done = (
            sem(n) for n in ("scored", "p_trans", "pv_done", "o_trans", "cT_trans", "proj_done"))
        masked, row_max, bias_ready, p_low, recip1, recip_ready, o_norm, pair_sum = (
            sem(n) for n in ("masked", "row_max", "bias_ready", "p_low", "recip1", "recip_ready", "o_norm", "pair_sum"))
        exp_done, p_high, o2_done, oT_copied, cT_copied = (
            sem(n) for n in ("exp_done", "p_high", "o2_done", "oT_copied", "cT_copied"))
        x2_high, sh_silu = sem("x2_high"), sem("sh_silu")
        x2_split, routed, sh_done, x2_summed = sem("x2_split"), sem("routed"), sem("sh_done"), sem("x2_summed")
        disp_built, w_built, xs_filled, xs_copied, w_filled, w_copied = (
            sem(n) for n in ("disp_built", "w_built", "xs_filled", "xs_copied", "w_filled", "w_copied"))
        dT_filled, dT_copied, gu_filled, silu_done, h_ready, hT_filled, hT_copied, dn_filled, o_high, o_low, comb_done = (
            sem(n) for n in ("dT_filled", "dT_copied", "gu_filled", "silu_done", "h_ready", "hT_filled", "hT_copied",
                             "dn_filled", "o_high", "o_low", "comb_done"))
        y_filled, y_copied, y_copied_a, yb_filled = sem("y_filled"), sem("y_copied"), sem("y_copied_a"), sem("yb_filled")

        front, mid = Fills(FRONT), Fills(MID)

        def front_wait(eng, name, i=0):
            f = front.at(name, i)
            if front.takes("v", f):
                eng.wait_ge(emptied_v, front.emptied("v", f))
            if front.takes("a", f):
                eng.wait_ge(emptied_a, front.emptied("a", f))

        def mid_wait(eng, name, i=0):
            f = mid.at(name, i)
            if mid.takes("v", f):
                eng.wait_ge(emptied2_v, mid.emptied("v", f))
            if mid.takes("a", f):
                eng.wait_ge(emptied2_a, mid.emptied("a", f))

        def wait_alone(eng, semaphore, value):
            value = value if isinstance(value, int) else eng.to_reg(value)
            eng.wait_ge(consts_set, 7)
            eng.wait_ge(semaphore, value)

        block = stack.enter_context(nc.Block())

        def store(eng, k):
            eng.dma_start(out.rearrange("(j k) n c -> k n j c", k=2)[k],
                          x1[HALF * k:HALF * k + N, :, :]).then_inc(out_dma[k], 16)

        @block.sync
        def _(sp):
            for half in range(2):
                sp.dma_start(wqkv_in[:, 3 * half:3 * half + 3, :],
                             w_qkv.rearrange("(g p) c -> p g c", p=P)[:, 3 * half:3 * half + 3, :]).then_inc(wqkv_dma[half], 16)
            sp.wait_ge(pads_zero, 1)
            for k in range(2):
                sp.dma_start(x_sb[HALF * k:HALF * k + N, :, :],
                             x.rearrange("(j k) n c -> k n j c", k=2)[k]).then_inc(x_in, 16)
            sp.dma_start(wp_in[:], w_proj.rearrange("(g p) c -> p g c", p=P)).then_inc(wp_dma, 16)
            sp.dma_start(wk_in, Wk.rearrange("e (g d) -> e g d", d=D)).then_inc(wk_dma, 16)
            sp.dma_start(bproj[:], b_proj.rearrange("(a c) -> a c", a=1).to_broadcast([P, C])).then_inc(bproj_dma, 16)
            sp.dma_start(wq_in, Wq.rearrange("(k p) n -> p k n", p=P)).then_inc(wq_dma, 16)
            sp.dma_start(wv_in, Wv.rearrange("e (g d) -> e g d", d=D)).then_inc(wv_dma, 16)
            sp.dma_start(wo_in, Wo.rearrange("(h v) n -> v h n", v=D)).then_inc(wo_dma, 16)

            def load_batch(b):
                if b >= 1:
                    sp.wait_ge(ctx_split, b)
                    sp.wait_ge(mask_bias, b)
                s = b % B
                sp.dma_start(c_in[:], ctx[s].rearrange("(c p) d -> p c d", p=KP)).then_inc(ctx_dma, 16)
                sp.dma_start(m_in[:], mask[s:s + 1, :].to_broadcast([P, SK])).then_inc(mask_dma, 16)

            load_batch(0)
            sp.dma_start(gw[:], gate_w.rearrange("(k p) e -> p k e", p=P)).then_inc(small_dma, 16)
            sp.dma_start(gbias[:], bias.rearrange("(a e) -> a e", a=1).to_broadcast([P, E])).then_inc(small_dma, 16)
            sp.dma_start(wsgu[:, :, 0, :], ws_gate.rearrange("(k p) f -> p k f", p=P)).then_inc(small_dma, 16)
            sp.dma_start(wsgu[:, :, 1, :], ws_up.rearrange("(k p) f -> p k f", p=P)).then_inc(small_dma, 16)
            sp.dma_start(wsd[:], ws_down).then_inc(small_dma, 16)
            load_batch(1)

            def load_experts(g):
                e = slice(GE * g, GE * (g + 1))
                s = ew_dma[g % 2]
                sp.dma_start(w_gu[:, g % 2, 0], w_gate[e].rearrange("e (p k) f -> p e (k f)", k=CC)).then_inc(s, 16)
                sp.dma_start(w_gu[:, g % 2, 1], w_up[e].rearrange("e (p k) f -> p e (k f)", k=CC)).then_inc(s, 16)
                sp.dma_start(w_dn[0:F, g % 2], w_down[e].rearrange("e f h -> f e h")).then_inc(s, 16)

            sp.wait_ge(scored, 1)
            load_experts(0)
            load_experts(1)
            for b in range(2, B + 1):
                load_batch(b)
            for g in range(2, NG):
                sp.wait_ge(dn_filled, GP * (g - 1))
                load_experts(g)
            sp.wait_ge(ln_out, 3 * NT)
            store(sp, 0)
            sp.wait_ge(out_dma[0], 16)

        @block.gpsimd
        def _(pool):
            steps = [0]

            def chained(ins):
                steps[0] += 1
                ins.then_inc(const_step, 1)
                pool.wait_ge(const_step, steps[0])

            nc.gpsimd.memset(zero16[:], 0.0).then_inc(zero_set, 1)
            nc.gpsimd.memset(ident[:], 0.0).then_inc(const_step, 1)
            nc.gpsimd.memset(ident16[:], 0.0).then_inc(const_step, 1)
            nc.gpsimd.memset(before[:], 1.0).then_inc(const_step, 1)
            nc.gpsimd.memset(headmask[:], 1.0).then_inc(const_step, 1)
            nc.gpsimd.memset(in_batch[:], 1.0).then_inc(const_step, 1)
            steps[0] = 5
            chained(nc.gpsimd.iota(slots_i[:], pattern=[[1, CAP]], base=-CHOSEN, channel_multiplier=0))
            nc.gpsimd.memset(ones16[:], 1.0).then_inc(consts_set, 1)
            for m in (ident, ident16):
                nc.gpsimd.affine_select(out=m[:], in_=m[:], compare_op=ALU.not_equal, fill=1.0, base=0,
                                        pattern=[[-1, P]], channel_multiplier=1).then_inc(consts_set, 1)
            nc.gpsimd.affine_select(out=before[:], in_=before[:], compare_op=ALU.is_gt, fill=0.0, base=0,
                                    pattern=[[1, P]], channel_multiplier=-1).then_inc(consts_set, 1)
            nc.gpsimd.tensor_copy(slots[:], slots_i[:]).then_inc(consts_set, 1)
            chained(nc.gpsimd.affine_select(out=in_batch[:], in_=in_batch[:], compare_op=ALU.is_ge, fill=0.0, base=N - 1,
                                            pattern=[[HALF, 2]], channel_multiplier=-1))
            chained(nc.gpsimd.affine_select(out=in_batch[:], in_=in_batch[:], compare_op=ALU.is_ge, fill=0.0, base=0,
                                            pattern=[[-HALF, 2]], channel_multiplier=1))
            nc.gpsimd.tensor_tensor(valid[:], in_batch[:, 0:1], in_batch[:, 1:2], ALU.add).then_inc(consts_set, 1)
            chained(nc.gpsimd.affine_select(out=headmask[:], in_=headmask[:], compare_op=ALU.is_ge, fill=0.0, base=0,
                                            pattern=[[-HD, HC], [0, VW]], channel_multiplier=1))
            nc.gpsimd.affine_select(out=headmask[:], in_=headmask[:], compare_op=ALU.is_ge, fill=0.0, base=HD - 1,
                                    pattern=[[HD, HC], [0, VW]], channel_multiplier=-1).then_inc(consts_set, 1)

            def split_ctx(b, parity):
                wait_alone(pool, ctx_dma, 16 * (b + 1))
                nc.gpsimd.tensor_copy(c16[:, parity, :, 0, :], c_in[:]).then_inc(ctx_high, 1)
                wait_alone(pool, ctx_high, b + 1)
                nc.gpsimd.tensor_tensor(c16[:, parity, :, 1, :], c_in[:], c16[:, parity, :, 0, :],
                                        ALU.subtract).then_inc(ctx_split, 1)
                wait_alone(pool, mask_dma, 16 * (b + 1))
                nc.gpsimd.tensor_scalar(mb[:, parity, :], m_in[:], BIG, -BIG, ALU.mult, ALU.add).then_inc(mask_bias, 1)

            def stage_q(b, parity):
                for hl in range(2):
                    nc.gpsimd.tensor_copy(q_st[:, parity, hl, :],
                                          Qt[:, hl, bass.ds(b, 1), :].rearrange("p a q -> p (a q)")).then_inc(q_staged, 1)

            pool.wait_ge(filled, front.at("xT", CC - 1) + 1)
            pool.wait_ge(bproj_dma, 16)
            nc.gpsimd.tensor_tensor(x_sb[:], x_sb[:], bproj[:].unsqueeze(1).to_broadcast([P, NT, C]), ALU.add).then_inc(x_biased, 1)
            split_ctx(0, 0)
            front_wait(pool, "x1T", 1)
            nc.gpsimd.memset(oT, 0.0).then_inc(oT_zero, 1)
            split_ctx(1, 1)

            def pair_body(i):
                for k in range(2):
                    wait_alone(pool, pv_done, PAIR * i + QT * (k + 1))
                    split_ctx(2 * i + 2 + k, k)
                    stage_q(2 * i + 2 + k, k)
            with pool.Fori(0, NT - 1) as i:
                pair_body(i)
            pool.wait_ge(pv_done, PAIR * (NT - 1) + QT)
            split_ctx(B, 0)
            pool.wait_ge(scored, NB * TILES)
            pool.wait_ge(cT_copied, NB * (B + 1))
            for m, v in ((gs[:, :, G:G + KG], -2 * BIG), (t8, -2 * BIG), (t6, -2 * BIG), (r3[:, :, E:E + 2], -2 * BIG),
                         (disp, 0.0), (xs, 0.0)):
                nc.gpsimd.memset(m, v).then_inc(tiles_set, 1)
            x2v = x1[:].rearrange("p j (m k) -> p j k m", k=CC)
            pool.wait_ge(ln_out, 2 * NT - 1)
            nc.gpsimd.tensor_copy(x2h[:, 0, BEFORE], x2v[:, BEFORE]).then_inc(x2_high, 1)
            pool.wait_ge(x2_high, 1)
            nc.gpsimd.tensor_tensor(x2h[:, 1, BEFORE], x2v[:, BEFORE], x2h[:, 0, BEFORE], ALU.subtract).then_inc(x2_split, 1)
            pool.wait_ge(ln_out, 2 * NT)
            nc.gpsimd.tensor_copy(x2h[:, 0, LAST], x2v[:, LAST]).then_inc(x2_high, 1)
            pool.wait_ge(x2_high, 2)
            nc.gpsimd.tensor_tensor(x2h[:, 1, LAST], x2v[:, LAST], x2h[:, 0, LAST], ALU.subtract).then_inc(x2_split, 1)
            pool.wait_ge(emptied2_a, mid.emptied("a", mid.at("shgu", NT - 1)))
            nc.gpsimd.tensor_tensor(sh_h[:], sh_gu[:, :, 0:F], sh_s[:], ALU.mult).then_inc(sh_silu, 1)
            pool.wait_ge(sh_silu, 1)
            nc.gpsimd.tensor_tensor(sh_h[:], sh_h[:], sh_gu[:, :, F:2 * F], ALU.mult).then_inc(sh_done, 1)

            pool.wait_ge(emptied2_a, mid.emptied("a", mid.at("shy", 1)))
            nc.gpsimd.tensor_tensor(x_sb[:], x_sb[:], x1[:], ALU.add).then_inc(x2_summed, 1)

        @block.tensor
        def _(pe):
            def stay_warm(bank, n):
                for k in range(n):
                    nc.tensor.matmul(ps[:, bank, :], zero16[:, 0:P], zero16[:], start=True, stop=True)

            pe.wait_ge(zero_set, 1)
            stay_warm(7, 8)
            pe.wait_ge(consts_set, 7)

            def fill(name, i=0):
                f = front.at(name, i)
                if f >= 8:
                    g = f - 8
                    if front.takes("v", g):
                        pe.wait_ge(emptied_v, front.emptied("v", g))
                    if front.takes("a", g):
                        pe.wait_ge(emptied_a, front.emptied("a", g))
                return ps[:, f % 8, :]

            for i in range(4):
                c, half = i % 2, i // 2
                if c == 0:
                    pe.wait_ge(wqkv_dma[half], 16)
                o = fill("wqkvT", i)
                for g in range(3):
                    last = nc.tensor.transpose(o[:, P * g:P * (g + 1)],
                                               wqkv_in[:, 3 * half + g, P * c:P * (c + 1)], ident[:])
                last.then_inc(filled, 1)
            pe.wait_ge(x_in, 32)
            for c in range(CC):
                o = fill("xT", c)
                for j in range(NT):
                    last = nc.tensor.transpose(o[:, P * j:P * (j + 1)], x_sb[:, j, P * c:P * (c + 1)], ident[:])
                last.then_inc(filled, 1)
            pe.wait_ge(wp_dma, 16)
            o = fill("wpT")
            for c in range(CC):
                for g in range(CC):
                    last = nc.tensor.transpose(o[:, C * c + P * g:C * c + P * (g + 1)],
                                               wp_in[:, g, P * c:P * (c + 1)], ident[:])
            last.then_inc(filled, 1)
            pe.wait_ge(wk_dma, 16)
            for i in range(2):
                o = fill("WkT", i)
                for g in range(4):
                    last = nc.tensor.transpose(o[:, D * g:D * (g + 1)], wk_in[:, 4 * i + g, :], ident[:])
                last.then_inc(filled, 1)
            for c in range(CC):
                front_wait(pe, "xT", c)
            for i in range(4):
                front_wait(pe, "wqkvT", i)
            for o_c in range(CC):
                o = fill("qT", o_c)
                for n, (c, wh, xh) in enumerate(PASSES):
                    last = nc.tensor.matmul(o, wqkvT[:, c, wh, P * o_c:P * (o_c + 1)], xT[:, c, xh, :],
                                            start=(n == 0), stop=(n == len(PASSES) - 1))
                last.then_inc(filled, 1)
            for j in range(NT):
                o = fill("kv", j)
                for n, (c, xh, wh) in enumerate(PASSES):
                    last = nc.tensor.matmul(o, xT[:, c, xh, P * j:P * (j + 1)], wqkvT[:, c, wh, C:3 * C],
                                            start=(n == 0), stop=(n == len(PASSES) - 1))
                last.then_inc(filled, 1)
            pe.wait_ge(wq_dma, 16)
            for i in range(8):
                o = fill("WqT", i)
                for n in range(4):
                    h, c = 2 * i + n // 2, n % 2
                    last = nc.tensor.transpose(o[:, P * n:P * (n + 1)], wq_in[:, c, D * h:D * (h + 1)], ident[:])
                last.then_inc(filled, 1)
            for b in range(B):
                front_wait(pe, "kv", b // 2)
                o = fill("G", b)
                r = HALF * (b % 2)
                for c in range(CC):
                    last = nc.tensor.matmul(o[:, HC * VW * c:HC * VW * (c + 1)],
                                            k_sb[r:r + N, b // 2, P * c:P * (c + 1)],
                                            v_aug[r:r + N, b // 2, HC * c:HC * (c + 1), :], start=True, stop=True)
                last.then_inc(filled, 1)
            front_wait(pe, "WkT", 0)
            front_wait(pe, "WkT", 1)
            front_wait(pe, "WqT", 6)
            front_wait(pe, "WqT", 7)

            def multiply_M(i):
                o = fill("M", i)
                for n in range(4):
                    h, c = 2 * i + n // 2, n % 2
                    for k, (a, b) in enumerate(HALVES):
                        last = nc.tensor.matmul(o[:, D * n:D * (n + 1)], wqT[:, a, h, c, :], wkT[:, b, h // 2, :],
                                                start=(k == 0), stop=(k == len(HALVES) - 1))
                last.then_inc(filled, 1)

            for i in range(4):
                multiply_M(i)
            front_wait(pe, "qT", 0)
            front_wait(pe, "qT", 1)
            for j in range(NT):
                o = fill("lin", j)
                for k in range(2):
                    b = 2 * j + k
                    front_wait(pe, "G", b)
                    for c in range(CC):
                        last = nc.tensor.matmul(o[HALF * k:HALF * (k + 1), HC * VW * c:HC * VW * (c + 1)],
                                                qT[:, c, HALF * b:HALF * (b + 1)],
                                                kvm[:, b, HC * VW * c:HC * VW * (c + 1)], start=True, stop=True)
                last.then_inc(filled, 1)
            for i in range(4, 8):
                multiply_M(i)
            pe.wait_ge(ao_ready, 1)
            for c in range(CC):
                o = fill("aoT", c)
                for j in range(NT):
                    last = nc.tensor.transpose(o[:, P * j:P * (j + 1)], ao[:, j, P * c:P * (c + 1)], ident[:])
                last.then_inc(filled, 1)
            pe.wait_ge(wv_dma, 16)
            for i in range(2):
                o = fill("WvT", i)
                for g in range(4):
                    last = nc.tensor.transpose(o[:, D * g:D * (g + 1)], wv_in[:, 4 * i + g, :], ident[:])
                last.then_inc(filled, 1)
            front_wait(pe, "wpT")
            front_wait(pe, "aoT", 0)
            front_wait(pe, "aoT", 1)
            for j in range(NT):
                o = fill("proj", j)
                for c in range(CC):
                    last = nc.tensor.matmul(o[:, 0:C], aoT[:, c, P * j:P * (j + 1)], wpT[:, c, :],
                                            start=(c == 0), stop=(c == CC - 1))
                last.then_inc(filled, 1)
            front_wait(pe, "WvT", 0)
            front_wait(pe, "WvT", 1)
            pe.wait_ge(wo_dma, 16)

            def multiply_W2(i):
                o = fill("W2", i)
                for n in range(2):
                    h = 2 * i + n
                    last = nc.tensor.matmul(o[:, C * n:C * (n + 1)], wvT[:, h // 2, :], wo_in[:, h, :],
                                            start=True, stop=True)
                last.then_inc(filled, 1)

            for i in EARLY_W2:
                multiply_W2(i)
            pe.wait_ge(ln_out, NT)
            for c in range(CC):
                o = fill("x1T", c)
                for j in range(NT):
                    last = nc.tensor.transpose(o[:, P * j:P * (j + 1)], x1[:, j, P * c:P * (c + 1)], ident[:])
                last.then_inc(filled, 1)
            pe.wait_ge(ctx_split, 1)
            def transpose_ctx(o, parity, u):
                for hl in range(2):
                    for t in range(TB):
                        at = 512 * hl + P * t
                        last = nc.tensor.transpose(o[:, at:at + KP], c16[:, parity, TB * u + t, hl, :],
                                                   ident16[0:KP, 0:KP])
                return last

            for u in range(NB):
                transpose_ctx(fill("cT", u).bitcast(F16), 0, u).then_inc(filled, 1)
            for i in MIDDLE_W2:
                multiply_W2(i)
            front_wait(pe, "M", 6)
            front_wait(pe, "M", 7)
            front_wait(pe, "x1T", 0)
            front_wait(pe, "x1T", 1)
            for h in range(QH):
                o = fill("Qt", h)
                for n, (c, mh, xh) in enumerate(PASSES):
                    last = nc.tensor.matmul(o[:, 0:B * N], M[:, mh, h, c, :],
                                            x1T16[:, xh, c, :].rearrange("p (b t) -> p b t", t=HALF)[:, :, 0:N],
                                            start=(n == 0), stop=(n == len(PASSES) - 1))
                last.then_inc(filled, 1)
            for i in LATE_W2:
                multiply_W2(i)
            score, prob_t, o_bank, misc = ps[:, 0:NB], ps[:, NB:2 * NB], ps[:, 6], ps[:, 7]

            def project(i, o_read):
                pe.wait_ge(oT_low, PAIR * (i + 1))
                pe.wait_ge(o_norm, o_read)
                if not (isinstance(i, int) and i == 0):
                    pe.wait_ge(pair_sum, i)
                for h in range(QH):
                    for n, (oh, wh) in enumerate(((0, 0), (0, 1), (1, 0))):
                        last = nc.tensor.matmul(o_bank[:, C:2 * C],
                                                oT[:, oh].rearrange("p b (t h) -> p (b t) h", h=QH)[:, :, h],
                                                W2[:, wh, h, :], start=(h == 0 and n == 0),
                                                stop=(h == QH - 1 and n == 2))
                last.then_inc(proj_done, 1)

            def tile_step(i, j, first=False, parts="STPOC"):
                n = PAIR * i + j
                b, par = 2 * i + j // QT, (j // QT) % 2
                cols = slice(P * (j % QT), P * (j % QT + 1))
                if "S" in parts:
                    if j % QT == 0:
                        if not first:
                            pe.wait_ge(q_staged, 2 * (b - 1))
                        pe.wait_ge(cT_copied, NB * (b + 1))
                    q = Qt[:, :, j // QT, cols] if first else q_st[:, par, :, cols]
                    for k in range(NB):
                        if not (first and j == 0):
                            pe.wait_ge(masked, NB * (n - 1) + k + 1)
                        keys = slice(KB * k, KB * (k + 1))
                        o = score[:, k, 0:KB]
                        nc.tensor.matmul(o, q[:, 0], cT[:, par, 0, keys], start=True, stop=False)
                        nc.tensor.matmul(o, q[:, 0], cT[:, par, 1, keys], start=False, stop=False)
                        nc.tensor.matmul(o, q[:, 1], cT[:, par, 0, keys],
                                         start=False, stop=True).then_inc(scored, 1)
                if j == 3 and not first:
                    project(i - 1, n - 2)
                u = j % QT - (QT - NB)
                if "C" in parts and u >= 0:
                    if u == 0:
                        pe.wait_ge(ctx_split, b + 2)
                    if not (first and j < 4):
                        pe.wait_ge(oT_low, n - 3)
                    transpose_ctx(misc.bitcast(F16), 1 - par, u).then_inc(cT_trans, 1)
                if first and j == 1:
                    front_wait(pe, "W2", LATE_W2[-1])
                if "T" in parts and not (first and j < 1):
                    pe.wait_ge(exp_done, n)
                    for k in range(NB):
                        if not (first and j < 2):
                            pe.wait_ge(p_high, NB * (n - 2) + k + 1)
                            pe.wait_ge(p_low, NB * (n - 2) + k + 1)
                        for t in range(TB):
                            kt = TB * k + t
                            last = nc.tensor.transpose(prob_t[0:KP, k, P * t:P * (t + 1)],
                                                       sc[:, (j - 1) % 2, KP * kt:KP * (kt + 1)], ident[:])
                        last.then_inc(p_trans, 1)
                if "P" in parts and not (first and j < 2):
                    if not (first and j < 3):
                        pe.wait_ge(o_norm, n - 2)
                        if j == 3 and not first:
                            pe.wait_ge(pair_sum, i)
                    pe.wait_ge(p_high, NB * (n - 1))
                    pe.wait_ge(p_low, NB * (n - 1))
                    cp = ((j - 2) // QT) % 2
                    for kt in range(KT):
                        for hl in range(2):
                            last = nc.tensor.matmul(
                                o_bank[:, 0:(2 - hl) * D], pT[0:KP, j % 2, hl, P * kt:P * (kt + 1)],
                                c16[:, cp, kt, 0:2 - hl, :], start=(kt == 0 and hl == 0),
                                stop=(kt == KT - 1 and hl == 1))
                    last.then_inc(pv_done, 1)
                if "O" in parts and not (first and j < 3):
                    pe.wait_ge(o_norm, n - 2)
                    if not (first and j < 4):
                        pe.wait_ge(oT_low, n - 3)
                    if "C" in parts and u >= 0:
                        pe.wait_ge(cT_copied, NB * (b + 1) + u + 1)
                    nc.tensor.transpose(misc[:, 0:P], on[:, (j - 3) % 2, :], ident[:]).then_inc(o_trans, 1)

            for u in range(NB):
                front_wait(pe, "cT", u)
            front_wait(pe, "Qt", QH - 1)
            for j in range(PAIR):
                tile_step(0, j, first=True)
            with pe.Fori(1, NT) as i:
                for j in range(PAIR):
                    tile_step(i, j)

            def fill2(name, i=0):
                f = mid.at(name, i)
                if f >= 8:
                    g = f - 8
                    if mid.takes("v", g):
                        pe.wait_ge(emptied2_v, mid.emptied("v", g))
                    if mid.takes("a", g):
                        pe.wait_ge(emptied2_a, mid.emptied("a", g))
                return ps[:, f % 8, :]

            def transpose_x2(o, c, tiles):
                for j in tiles:
                    last = nc.tensor.transpose(o[:, P * (j - tiles[0]):P * (j - tiles[0] + 1)], x1[:, j, P * c:P * (c + 1)],
                                               ident[:])
                return last

            def router(i, tiles):
                o = fill2("logit", i)
                for j in tiles:
                    for c in range(CC):
                        last = nc.tensor.matmul(o[:, E * j:E * (j + 1)], x1T[:, c, P * j:P * (j + 1)], gw[:, c, :],
                                                start=(c == 0), stop=(c == CC - 1))
                last.then_inc(filled2, 1)

            tile_step(NT, 0, parts="TPO")
            pe.wait_ge(masked, NB * TILES)
            stay_warm(2, 6)
            tile_step(NT, 1, parts="PO")
            pe.wait_ge(ln_out, 2 * NT - 1)
            for c in range(CC):
                transpose_x2(fill2("x2T", c), c, range(NT - 1)).then_inc(filled2, 1)
            tile_step(NT, 2, parts="O")
            pe.wait_ge(small_dma, 16 * 5)
            stay_warm(2, 5)
            mid_wait(pe, "x2T", 0)
            mid_wait(pe, "x2T", 1)
            router(0, range(NT - 1))
            project(NT - 1, TILES)

            def shared_gate_up(j):
                o = fill2("shgu", j)
                for c in range(CC):
                    last = nc.tensor.matmul(o[:, 0:2 * F], x1T[:, c, P * j:P * (j + 1)], wsgu[:, c, :, :],
                                            start=(c == 0), stop=(c == CC - 1))
                last.then_inc(filled2, 1)

            shared_gate_up(0)
            shared_gate_up(1)
            mid_wait(pe, "logit", 0)
            stay_warm(2, 5)
            pe.wait_ge(ln_out, 2 * NT)
            o = fill2("x2T", 2)
            for c in range(CC):
                last = transpose_x2(o[:, P * c:P * (c + 1)], c, [NT - 1])
            last.then_inc(filled2, 1)
            mid_wait(pe, "x2T", 2)
            router(1, [NT - 1])
            shared_gate_up(2)
            shared_gate_up(3)
            y_acc = ps[:, 5:7]
            mid_wait(pe, "logit", 1)
            for c in range(CC):
                nc.tensor.matmul(y_acc[:, c, :], zero16[:, 0:P], zero16[:], start=True, stop=False,
                                 skip_group_check=True)

            stay_warm(2, 7)
            pe.wait_ge(routed, 1)
            o = fill2("pos")
            for j in range(NT):
                for k in range(j + 1):
                    last = nc.tensor.matmul(o[:, E * j:E * (j + 1)], (before if k == j else ones16)[:],
                                            sel16[:, k, :], start=(k == 0), stop=(k == j))
            last.then_inc(filled2, 1)
            pe.wait_ge(sh_done, 1)
            o = fill2("shT")
            for j in range(NT):
                last = nc.tensor.transpose(o[0:F, P * j:P * (j + 1)], sh_h[:, j, :], ident[:])
            last.then_inc(filled2, 1)
            mid_wait(pe, "shgu", 2)
            stay_warm(7, 2)
            mid_wait(pe, "shT")

            def shared_down(i):
                o = fill2("shy", i)
                for k in range(2):
                    last = nc.tensor.matmul(o[:, C * k:C * (k + 1)], sh_hT[:, P * (2 * i + k):P * (2 * i + k + 1)], wsd[:],
                                            start=True, stop=True)
                last.then_inc(filled2, 1)

            shared_down(0)

            mid_wait(pe, "pos")
            gu_bank, xs_bank, misc2, dn_bank, dT_bank = ps[:, 0:2], ps[:, 2], ps[:, 3], ps[:, 4], ps[:, 7]

            def dispatch(g, par, piece, first=False):
                c, half = piece // 2, piece % 2
                if c == 0:
                    pe.wait_ge(disp_built, 2 * g + half + 1)
                if piece == 0:
                    if first:
                        pe.wait_ge(x2_split, 2)
                    else:
                        pe.wait_ge(xs_copied, CC * g)
                if piece == 2:
                    pe.wait_ge(xs_copied, CC * g + 1)
                for j in (2 * half, 2 * half + 1):
                    for hl in range(2):
                        last = nc.tensor.matmul(xs_bank[:, 0:GE * CAP], x2h[:, hl, j, c, :],
                                                disp[:, par, j, :, 0:CAP], start=(j == 0 and hl == 0),
                                                stop=(j == NT - 1 and hl == 1))
                if half == 1:
                    last.then_inc(xs_filled, 1)

            def slot_weights(g, par, first, n):
                pe.wait_ge(w_built, g + 1)
                if not first:
                    pe.wait_ge(hT_copied, n)
                for q in range(GP):
                    for j in range(NT):
                        last = nc.tensor.matmul(misc2[:, C + 4 * q:C + 4 * (q + 1)],
                                                disp[:, par, j, 2 * q:2 * q + 2, :].rearrange("p e s -> p (e s)"),
                                                w_grp[:, par, j, 2 * q:2 * q + 2, :].rearrange("p e s -> p (e s)"),
                                                start=(j == 0), stop=(j == NT - 1))
                last.then_inc(w_filled, 1)

            def pair_step(i, q, first=False, parts="GTDCN"):
                n = 2 * GP * i + q
                g, par, gq = 2 * i + q // GP, (q // GP) % 2, q % GP
                if "T" in parts and not (first and q < 1):
                    pe.wait_ge(h_ready, n)
                    if not (first and q < 2):
                        pe.wait_ge(hT_copied, n - 1)
                    if gq == 0 and "G" in parts:
                        pe.wait_ge(w_copied, g + 1)
                    nc.tensor.transpose(misc2[0:F, 0:P], h_sb[:, (q - 1) % 2, :], ident[:]).then_inc(hT_filled, 1)
                if "G" in parts:
                    if not (first and q < 1):
                        pe.wait_ge(dT_copied, n)
                    o = dT_bank.bitcast(F16)[:, 512 * (q % 2):512 * (q % 2 + 1)]
                    for j in range(NT):
                        last = nc.tensor.transpose(o[:, P * j:P * (j + 1)],
                                                   disp[:, par, j, 2 * gq:2 * gq + 2, :].rearrange("p e s -> p (e s)"),
                                                   ident16[:])
                    last.then_inc(dT_filled, 1)
                    if gq == 0:
                        pe.wait_ge(xs_copied, CC * (g + 1))
                        pe.wait_ge(ew_dma[par], 48 * (i + 1))
                    if not (first and q < 2):
                        pe.wait_ge(h_ready, n - 1)
                    for c in range(CC):
                        for s in range(2):
                            e = 2 * gq + s
                            last = nc.tensor.matmul(gu_bank[SLOT * s:SLOT * (s + 1), q % 2, 0:2 * F],
                                                    xs[:, par, c, e, :], w_gu[:, par, :, e, F * c:F * (c + 1)],
                                                    start=(c == 0), stop=(c == CC - 1))
                    last.then_inc(gu_filled, 1)
                if "D" in parts:
                    dispatch(g + 1, 1 - par, gq)
                    if gq == GP - 1:
                        slot_weights(g + 1, 1 - par, False, n)
                if "C" in parts and not (first and q < 2):
                    pe.wait_ge(o_high, n - 1)
                    pe.wait_ge(o_low, n - 1)
                    pe.wait_ge(dT_copied, n - 1)
                    for c in range(CC):
                        for hl in range(2):
                            last = nc.tensor.matmul(batches(y_acc[:, c, :]), o_hl[:, q % 2, hl, P * c:P * (c + 1)],
                                                    batches(dispT[:, (q - 2) % GP, :]), start=False, stop=False,
                                                    skip_group_check=True)
                    last.then_inc(comb_done, 1)
                if "N" in parts and not (first and q < 1):
                    pe.wait_ge(hT_copied, n)
                    if not (first and q < 2):
                        pe.wait_ge(o_high, n - 1)
                        pe.wait_ge(o_low, n - 1)
                    dq, dp = (q - 1) % GP, ((q - 1) // GP) % 2
                    for s in range(2):
                        last = nc.tensor.matmul(dn_bank[SLOT * s:SLOT * (s + 1), 0:C],
                                                hT[:, (q - 1) % 2, SLOT * s:SLOT * (s + 1)],
                                                w_dn[0:F, dp, 2 * dq + s, :], start=True, stop=True)
                    last.then_inc(dn_filled, 1)

            def batches(cols):
                return cols.rearrange("p (b t) -> p b t", t=HALF)[:, :, 0:N]

            dispatch(0, 0, 0, first=True)
            dispatch(0, 0, 1, first=True)
            shared_down(1)
            dispatch(0, 0, 2, first=True)
            dispatch(0, 0, 3, first=True)
            mid_wait(pe, "shy", 1)
            slot_weights(0, 0, True, 0)
            pe.wait_ge(w_copied, 1)
            for q in range(2 * GP):
                pair_step(0, q, first=True)
            with pe.Fori(1, NG // 2 - 1) as i:
                for q in range(2 * GP):
                    pair_step(i, q)
            for q in range(2 * GP):
                pair_step(NG // 2 - 1, q, parts="GTDCN" if q < GP else "GTCN")
            pair_step(NG // 2, 0, parts="T")
            pe.wait_ge(xs_copied, CC * NG)
            stay_warm(2, 4)
            pair_step(NG // 2, 0, parts="CN")
            stay_warm(2, 5)
            pair_step(NG // 2, 1, parts="C")
            for c in range(CC):
                nc.tensor.matmul(y_acc[:, c, :], zero16[:, 0:P], zero16[:], start=False, stop=True,
                                 skip_group_check=True).then_inc(y_filled, 1)
            stay_warm(2, 3)
            pe.wait_ge(y_copied, 1)
            pe.wait_ge(y_copied_a, 1)
            for j in range(NT):
                for c in range(CC):
                    last = nc.tensor.transpose(ps[:, j // 2, C * (j % 2) + P * c:C * (j % 2) + P * (c + 1)],
                                               yT_sb[:, c, P * j:P * (j + 1)], ident[:])
            last.then_inc(yb_filled, 1)

        @block.scalar
        def _(act):
            def take(name, i=0):
                f = front.at(name, i)
                act.wait_ge(filled, f + 1)
                return ps[:, f % 8, :]

            def mine(name):
                return [i for i, f in enumerate(front.where[name]) if front.takes("a", f)]

            def std(k, tiles=slice(0, NT)):
                act.wait_ge(ln_var, k)
                nc.scalar.activation(sd[:, tiles], ve[:, tiles], ACT.Sqrt).then_inc(ln_std, 1)

            for i in mine("wqkvT"):
                nc.scalar.mul(wqkvT[:, i % 2, 0, 384 * (i // 2):384 * (i // 2 + 1)],
                              take("wqkvT", i)[:, 0:384], IN_UP).then_inc(emptied_a, 1)
            for c in mine("xT"):
                nc.scalar.copy(xT[:, c, 0, :], take("xT", c)).then_inc(emptied_a, 1)
            nc.scalar.copy(wpT[:].rearrange("p a b -> p (a b)"), take("wpT")).then_inc(emptied_a, 1)
            for i in mine("WkT"):
                nc.scalar.mul(wkT[:, 0, 4 * i:4 * i + 4, :].rearrange("p a b -> p (a b)"),
                              take("WkT", i), IN_UP).then_inc(emptied_a, 1)
            for c in mine("qT"):
                nc.scalar.activation(qT[:, c, :], take("qT", c), ACT.Relu, scale=1.0 / IN_UP).then_inc(emptied_a, 1)
            for j in mine("kv"):
                nc.scalar.mul(v_aug[:, j, :, 0:HD],
                              take("kv", j)[:, C:2 * C].rearrange("p (h d) -> p h d", d=HD), 1.0 / IN_UP).then_inc(emptied_a, 1)
            for i in mine("WqT"):
                nc.scalar.mul(wqT[:, 0, 2 * i:2 * i + 2].rearrange("p a b c -> p (a b c)"),
                              take("WqT", i), IN_UP).then_inc(emptied_a, 1)
            for i in range(8):
                nc.scalar.mul(M[:, 0, 2 * i:2 * i + 2].rearrange("p a b c -> p (a b c)"), take("M", i),
                              M_SCALE).then_inc(emptied_a, 1)
            for c in mine("aoT"):
                nc.scalar.copy(aoT[:, c, :], take("aoT", c)).then_inc(emptied_a, 1)
            for i in mine("WvT"):
                nc.scalar.copy(wvT[:, 4 * i:4 * i + 4, :].rearrange("p a b -> p (a b)"),
                               take("WvT", i)).then_inc(emptied_a, 1)

            def high_W2(i):
                nc.scalar.mul(W2[:, 0, 2 * i:2 * i + 2, :].rearrange("p a b -> p (a b)"),
                              take("W2", i), W_UP).then_inc(emptied_a, 1)

            def copy_cT(dst_par, u, bank16):
                return nc.scalar.copy(
                    cT[:, dst_par, :, KB * u:KB * (u + 1)].rearrange("p s (t k) -> p s t k", k=KP),
                    bank16.rearrange("p (s t k) -> p s t k", s=2, k=P)[:, :, :, 0:KP])

            for i in EARLY_W2:
                high_W2(i)
                if i == 0:
                    std(1)
            for c in mine("x1T"):
                nc.scalar.copy(x1T16[:, 0, c, :], take("x1T", c)).then_inc(emptied_a, 1)
            for u in mine("cT"):
                copy_cT(0, u, take("cT", u).bitcast(F16)).then_inc(emptied_a, 1)
            for i in MIDDLE_W2:
                high_W2(i)
            for h in range(QH):
                nc.scalar.copy(Qt[:, 0].rearrange("p b (t h) -> p b t h", h=QH)[:, :, :, h],
                               take("Qt", h)[:, 0:B * N].rearrange("p (b t) -> p b t", t=N)).then_inc(emptied_a, 1)
                if h == 0:
                    nc.scalar.activation(warm[:, 0:1], ident[:, 0:1], ACT.Exp)
            for i in LATE_W2:
                high_W2(i)

            prob_t, o_bank, misc = ps[:, NB:2 * NB], ps[:, 6], ps[:, 7]

            def tile_step(i, j, first=False, parts="HEOC"):
                n = PAIR * i + j
                b = 2 * i + j // QT
                u = j % QT - (QT - NB)
                if "C" in parts and u >= 0:
                    act.wait_ge(cT_trans, NB * b + u + 1)
                    copy_cT((j // QT + 1) % 2, u, misc.bitcast(F16)).then_inc(cT_copied, 1)
                if "H" in parts and not (first and j < 1):
                    if not (first and j < 3):
                        act.wait_ge(pv_done, n - 2)
                    for k in range(NB):
                        act.wait_ge(p_trans, NB * (n - 1) + k + 1)
                        nc.scalar.copy(pT[0:KP, (j - 1) % 2, 0, 512 * k:512 * (k + 1)],
                                       prob_t[0:KP, k, :]).then_inc(p_high, 1)
                if "E" in parts:
                    act.wait_ge(bias_ready, n + 1)
                    if not (first and j < 2):
                        act.wait_ge(recip_ready, n - 1)
                    nc.scalar.activation(sc[:, j % 2, :], sc[:, j % 2, :], ACT.Exp, bias=nb[:, j % 2:j % 2 + 1],
                                         scale=1.0 / M_UP, accum_out=rs[:, j % 2:j % 2 + 1]).then_inc(exp_done, 1)
                if "O" in parts and not (first and j < 2):
                    act.wait_ge(recip_ready, n - 1)
                    if not (first and j < 4):
                        act.wait_ge(o_norm, n - 3)
                    act.wait_ge(pv_done, n - 1)
                    nc.scalar.activation(o2[:, j % 2, :], o_bank[:, D:2 * D], ACT.Copy,
                                         scale=rr[:, j % 2:j % 2 + 1]).then_inc(o2_done, 1)
                if "O" in parts or "X" in parts:
                    if not (first and j < 3):
                        if first and j == 3:
                            act.wait_ge(oT_zero, 1)
                        if j == 3 and not first:
                            act.wait_ge(proj_done, i)
                        act.wait_ge(o_trans, n - 2)
                        m = (j - 3) % PAIR
                        nc.scalar.copy(oT[:, 0, m // QT, P * (m % QT):P * (m % QT + 1)], misc[:, 0:P]).then_inc(oT_copied, 1)

            for u in range(NB):
                front_wait(act, "cT", u)
            nc.scalar.sem_inc(cT_copied, NB)
            for j in range(PAIR):
                tile_step(0, j, first=True)
            with act.Fori(1, NT) as i:
                for j in range(PAIR):
                    tile_step(i, j)
            tile_step(NT, 0, parts="HO")
            std(2, BEFORE)
            tile_step(NT, 1, parts="O")
            tile_step(NT, 2, parts="X")

            def take2(name, i=0):
                f = mid.at(name, i)
                act.wait_ge(filled2, f + 1)
                return ps[:, f % 8, :]

            def scores(i, tiles):
                nc.scalar.activation(r1[:, tiles, :].rearrange("p a b -> p (a b)"),
                                     take2("logit", i)[:, E * tiles.start:E * tiles.stop],
                                     ACT.Sigmoid).then_inc(emptied2_a, 1)

            def load_table(k, function):
                nc.scalar.activation(warm[:, k:k + 1], ident[:, 0:1], function)

            nc.scalar.copy(x1T[:, 0, 0:P * (NT - 1)], take2("x2T", 0)[:, 0:P * (NT - 1)]).then_inc(emptied2_a, 1)
            load_table(1, ACT.Sigmoid)
            scores(0, BEFORE)
            load_table(2, ACT.Sqrt)
            std(3, LAST)
            load_table(3, ACT.Sigmoid)

            def shared_sigmoid(j):
                o = take2("shgu", j)
                nc.scalar.activation(sh_s[:, j, :], o[:, 0:F], ACT.Sigmoid)
                nc.scalar.copy(sh_gu[:, j, :], o[:, 0:2 * F]).then_inc(emptied2_a, 1)

            shared_sigmoid(0)
            shared_sigmoid(1)
            scores(1, LAST)
            shared_sigmoid(2)
            shared_sigmoid(3)
            nc.scalar.copy(sh_hT[:], take2("shT")[0:F, :]).then_inc(emptied2_a, 1)

            gu_bank, xs_bank, dn_bank = ps[:, 0:2], ps[:, 2], ps[:, 4]

            def move_rows(g, par, c):
                act.wait_ge(xs_filled, CC * g + c + 1)
                nc.scalar.copy(xs[:, par, c, :, 0:CAP],
                               xs_bank[:, 0:GE * CAP].rearrange("p (e s) -> p e s", s=CAP)).then_inc(xs_copied, 1)

            def pair_step(i, q, first=False, parts="GDN"):
                n = 2 * GP * i + q
                if "G" in parts:
                    act.wait_ge(gu_filled, n + 1)
                    if not (first and q < 2):
                        act.wait_ge(h_ready, n - 1)
                    nc.scalar.activation(act_g[:, q % 2, :], gu_bank[:, q % 2, 0:F],
                                         ACT.Silu).then_inc(silu_done, 1)
                if "D" in parts:
                    if q % 2 == 1:
                        move_rows(2 * i + q // GP + 1, (q // GP + 1) % 2, q % GP // 2)
                if "N" in parts and not (first and q < 1):
                    g1, dq = 2 * i + (q - 1) // GP, (q - 1) % GP
                    act.wait_ge(dn_filled, n)
                    act.wait_ge(w_copied, g1 + 1)
                    if not (first and q < 3):
                        act.wait_ge(comb_done, n - 2)
                    nc.scalar.activation(o_hl[:, (q - 1) % 2, 0, :], dn_bank[:, 0:C], ACT.Copy,
                                         scale=ws_slot[:, g1_par(q), dq:dq + 1]).then_inc(o_high, 1)
            def g1_par(q):
                return ((q - 1) // GP) % 2

            def move_shared(i):
                nc.scalar.copy(x_sb[:, 2 * i:2 * i + 2, :].rearrange("p a c -> p (a c)"), take2("shy", i)).then_inc(emptied2_a, 1)

            move_shared(0)
            move_rows(0, 0, 0)
            move_shared(1)
            move_rows(0, 0, 1)
            for q in range(2 * GP):
                pair_step(0, q, first=True)
            with act.Fori(1, NG // 2 - 1) as i:
                for q in range(2 * GP):
                    pair_step(i, q)
            for q in range(2 * GP):
                pair_step(NG // 2 - 1, q, parts="GDN" if q < GP else "GN")
            pair_step(NG // 2, 0, parts="N")
            load_table(4, ACT.Sqrt)
            act.wait_ge(y_filled, 2)
            nc.scalar.copy(yT_sb[:, 0, :], ps[:, 5, :]).then_inc(y_copied_a, 1)
            std(4)
            act.wait_ge(ln_out, 3 * NT)
            store(act, 1)
            act.wait_ge(out_dma[1], 16)

        @block.vector
        def _(dve):
            steps = [0]

            def chained(ins):
                steps[0] += 1
                ins.then_inc(dve_step, 1)
                dve.wait_ge(dve_step, steps[0])

            def take(name, i=0):
                f = front.at(name, i)
                dve.wait_ge(filled, f + 1)
                return ps[:, f % 8, :]

            def mine(name):
                return [i for i, f in enumerate(front.where[name]) if front.takes("v", f)]

            def norm_variance(src, tiles=slice(0, NT), stats=True):
                if stats:
                    for j in range(tiles.start, tiles.stop):
                        last = nc.vector.bn_stats(st[:, j, :], src[:, j, :])
                    chained(last)
                for j in range(tiles.start, tiles.stop):
                    last = nc.vector.bn_aggr(mv[:, j, :], st[:, j, :])
                chained(last)
                nc.vector.tensor_scalar(ve[:, tiles], mv[:, tiles, 1], LN_EPS, None, ALU.add).then_inc(ln_var, 1)

            def norm_output(src, dst, k, tiles=slice(0, NT)):
                dve.wait_ge(ln_std, k)
                chained(nc.vector.reciprocal(rstd[:, tiles], sd[:, tiles]))
                for j in range(tiles.start, tiles.stop):
                    nc.vector.tensor_scalar(dst[:, j, :], src[:, j, :], mv[:, j, 0:1], rstd[:, j:j + 1],
                                            ALU.subtract, ALU.mult).then_inc(ln_out, 1)

            chained(nc.vector.memset(x_sb[32:64, :, :], 0.0))
            nc.vector.memset(x_sb[96:128, :, :], 0.0).then_inc(pads_zero, 1)
            nc.vector.memset(v_aug[:, :, :, HD:VW], 1.0).then_inc(dve_const, 1)

            for i in mine("wqkvT"):
                part = slice(384 * (i // 2), 384 * (i // 2 + 1))
                o = take("wqkvT", i)[:, 0:384]
                dve.wait_ge(emptied_a, front.emptied("a", front.at("wqkvT", i)))
                nc.vector.scalar_tensor_tensor(wqkvT[:, i % 2, 1, part], o, IN_UP, wqkvT[:, i % 2, 0, part],
                                               ALU.mult, ALU.subtract).then_inc(emptied_v, 1)
            for c in mine("xT"):
                o = take("xT", c)
                dve.wait_ge(emptied_a, front.emptied("a", front.at("xT", c)))
                nc.vector.tensor_tensor(xT[:, c, 1, :], o, xT[:, c, 0, :], ALU.subtract).then_inc(emptied_v, 1)

            def low_half(o, name, i, high, low):
                dve.wait_ge(emptied_a, front.emptied("a", front.at(name, i)))
                nc.vector.scalar_tensor_tensor(low, o, IN_UP, high, ALU.mult, ALU.subtract).then_inc(emptied_v, 1)

            for i in mine("WkT"):
                low_half(take("WkT", i), "WkT", i, *(wkT[:, s, 4 * i:4 * i + 4, :].rearrange("p a b -> p (a b)") for s in range(2)))
            for c in mine("qT"):
                nc.vector.tensor_scalar(qT[:, c, :], take("qT", c), 0.0, 1.0 / IN_UP, ALU.max, ALU.mult).then_inc(emptied_v, 1)
            dve.wait_ge(dve_const, 1)
            for j in mine("kv"):
                o = take("kv", j)
                dve.wait_ge(emptied_a, front.emptied("a", front.at("kv", j)))
                nc.vector.tensor_scalar(k_sb[:, j, :], o[:, 0:C], 0.0, 1.0 / IN_UP, ALU.max, ALU.mult).then_inc(emptied_v, 1)
            for i in mine("WqT"):
                low_half(take("WqT", i), "WqT", i, *(wqT[:, s, 2 * i:2 * i + 2].rearrange("p a b c -> p (a b c)") for s in range(2)))
            dve.wait_ge(consts_set, 7)
            for b in range(B):
                w = HC * VW
                nc.vector.tensor_tensor(kvm[:, b, :].rearrange("p (c w) -> p c w", w=w),
                                        take("G", b)[:, 0:CC * w].rearrange("p (c w) -> p c w", w=w),
                                        headmask[:].rearrange("p h v -> p (h v)").unsqueeze(1).to_broadcast([P, CC, w]),
                                        ALU.mult).then_inc(emptied_v, 1)
            def low_M(i):
                o = take("M", i)
                dve.wait_ge(emptied_a, front.emptied("a", front.at("M", i)))
                nc.vector.scalar_tensor_tensor(M[:, 1, 2 * i:2 * i + 2].rearrange("p a b c -> p (a b c)"), o,
                                               M_SCALE, M[:, 0, 2 * i:2 * i + 2].rearrange("p a b c -> p (a b c)"),
                                               ALU.mult, ALU.subtract).then_inc(emptied_v, 1)

            for i in range(4):
                low_M(i)
            for j in range(NT):
                o = take("lin", j)[:, 0:LH * VW].rearrange("p (h v) -> p h v", v=VW)
                chained(nc.vector.tensor_scalar(den[:, j, :], o[:, :, HD], DEN_EPS, None, ALU.add))
                chained(nc.vector.reciprocal(den[:, NT + j, :], den[:, j, :]))
                last = nc.vector.tensor_tensor(ao[:, j, :].rearrange("p (h d) -> p h d", d=HD), o[:, :, 0:HD],
                                               den[:, NT + j, :].unsqueeze(2).to_broadcast([P, LH, HD]), ALU.mult)
                last.then_inc(emptied_v, 1)
            dve.wait_ge(emptied_v, front.emptied("v", front.at("lin", NT - 1)))
            nc.vector.sem_inc(ao_ready, 1)
            for i in range(4, 8):
                low_M(i)
            for c in mine("aoT"):
                nc.vector.tensor_copy(aoT[:, c, :], take("aoT", c)).then_inc(emptied_v, 1)
            dve.wait_ge(x_biased, 1)
            for j in range(NT):
                nc.vector.tensor_tensor(x_sb[:, j, :], x_sb[:, j, :], take("proj", j)[:, 0:C], ALU.add).then_inc(emptied_v, 1)
                dve.wait_ge(emptied_v, front.emptied("v", front.at("proj", j)))
                last = nc.vector.bn_stats(st[:, j, :], x_sb[:, j, :])
            chained(last)
            norm_variance(x_sb, stats=False)
            norm_output(x_sb, x1, 1)

            def low_W2(i):
                o = take("W2", i)
                dve.wait_ge(emptied_a, front.emptied("a", front.at("W2", i)))
                hi, lo = (W2[:, s, 2 * i:2 * i + 2, :].rearrange("p a b -> p (a b)") for s in range(2))
                nc.vector.scalar_tensor_tensor(lo, o, W_UP, hi, ALU.mult, ALU.subtract).then_inc(emptied_v, 1)

            for i in EARLY_W2:
                low_W2(i)
            for c in mine("x1T"):
                o = take("x1T", c)
                dve.wait_ge(emptied_a, front.emptied("a", front.at("x1T", c)))
                nc.vector.tensor_tensor(x1T16[:, 1, c, :], o, x1T16[:, 0, c, :], ALU.subtract).then_inc(emptied_v, 1)
            for u in mine("cT"):
                nc.vector.tensor_copy(
                    cT[:, 0, :, KB * u:KB * (u + 1)].rearrange("p s (t k) -> p s t k", k=KP),
                    take("cT", u).bitcast(F16).rearrange("p (s t k) -> p s t k", s=2, k=P)[:, :, :, 0:KP]
                ).then_inc(emptied_v, 1)
            for i in MIDDLE_W2:
                low_W2(i)
            for h in range(QH):
                o = take("Qt", h)[:, 0:B * N].rearrange("p (b t) -> p b t", t=N)
                dve.wait_ge(emptied_a, front.emptied("a", front.at("Qt", h)))
                hi, lo = (Qt[:, s].rearrange("p b (t h) -> p b t h", h=QH)[:, :, :, h] for s in range(2))
                nc.vector.tensor_tensor(lo, o, hi, ALU.subtract).then_inc(emptied_v, 1)
            for i in LATE_W2:
                low_W2(i)

            score, prob_t, o_bank, misc = ps[:, 0:NB], ps[:, NB:2 * NB], ps[:, 6], ps[:, 7]

            def tile_step(i, j, first=False, parts="SRLO"):
                n = PAIR * i + j
                b, par, tp = 2 * i + j // QT, (j // QT) % 2, j % 2
                if "S" in parts:
                    if j % QT == 0:
                        wait_alone(dve, mask_bias, b + 1)
                    if not (first and j < 2):
                        wait_alone(dve, p_trans, NB * (n - 1))
                    for k in range(NB):
                        keys = slice(KB * k, KB * (k + 1))
                        wait_alone(dve, scored, NB * n + k + 1)
                        nc.vector.tensor_tensor_reduce(out=sc[:, tp, keys], in0=score[:, k, 0:KB], in1=mb[:, par, keys],
                                                       scale=1.0, scalar=-3e38, op0=ALU.add, op1=ALU.max,
                                                       accum_out=mx3[:, tp, k:k + 1]).then_inc(masked, 1)
                    dve.wait_ge(masked, NB * (n + 1))
                    nc.vector.tensor_reduce(mxa[:, tp:tp + 1], mx3[:, tp, :], AX.X, ALU.max).then_inc(row_max, 1)
                    dve.wait_ge(row_max, n + 1)
                    nc.vector.tensor_scalar(nb[:, tp:tp + 1], mxa[:, tp:tp + 1], -1.0 / M_UP, LOG_P,
                                            ALU.mult, ALU.add).then_inc(bias_ready, 1)
                if "R" in parts and not (first and j < 1):
                    op = (j - 1) % 2
                    dve.wait_ge(exp_done, n)
                    nc.vector.reciprocal(rinv[:, op:op + 1], rs[:, op:op + 1]).then_inc(recip1, 1)
                    dve.wait_ge(recip1, n)
                    nc.vector.scalar_tensor_tensor(rr[:, op:op + 1], mxa[:, op:op + 1], -0.5 * BIG, rinv[:, op:op + 1],
                                                   ALU.is_gt, ALU.mult).then_inc(recip_ready, 1)
                if j == 3 and not first:
                    add_pair(i - 1)
                if "L" in parts and not (first and j < 1):
                    if not (first and j < 3):
                        dve.wait_ge(pv_done, n - 2)
                    for k in range(NB):
                        part = slice(512 * k, 512 * (k + 1))
                        dve.wait_ge(p_high, NB * (n - 1) + k + 1)
                        nc.vector.tensor_tensor(pT[0:KP, (j - 1) % 2, 1, part], prob_t[0:KP, k, :],
                                                pT[0:KP, (j - 1) % 2, 0, part], ALU.subtract).then_inc(p_low, 1)
                if "O" in parts and not (first and j < 2):
                    dve.wait_ge(o2_done, n - 1)
                    if not (first and j < 4):
                        dve.wait_ge(o_trans, n - 3)
                    nc.vector.scalar_tensor_tensor(on[:, tp, :], o_bank[:, 0:D], rr[:, tp:tp + 1], o2[:, tp, :],
                                                   ALU.mult, ALU.add).then_inc(o_norm, 1)
                if ("O" in parts or "X" in parts) and not (first and j < 3):
                    m = (j - 3) % PAIR
                    at = slice(P * (m % QT), P * (m % QT + 1))
                    dve.wait_ge(oT_copied, n - 2)
                    nc.vector.tensor_tensor(oT[:, 1, m // QT, at], misc[:, 0:P], oT[:, 0, m // QT, at],
                                            ALU.subtract).then_inc(oT_low, 1)

            def add_pair(i):
                dve.wait_ge(proj_done, i + 1)
                nc.vector.scalar_tensor_tensor(x_sb[:, bass.ds(i, 1), :].rearrange("p a c -> p (a c)"), o_bank[:, C:2 * C],
                                               1.0 / W_UP, x1[:, bass.ds(i, 1), :].rearrange("p a c -> p (a c)"),
                                               ALU.mult, ALU.add).then_inc(pair_sum, 1)

            for j in range(PAIR):
                tile_step(0, j, first=True)
            with dve.Fori(1, NT) as i:
                for j in range(PAIR):
                    tile_step(i, j)
            norm_variance(x_sb, BEFORE)
            tile_step(NT, 0, parts="RLO")
            norm_output(x_sb, x1, 2, BEFORE)
            tile_step(NT, 1, parts="O")
            tile_step(NT, 2, parts="X")

            def take2(name, i=0):
                f = mid.at(name, i)
                dve.wait_ge(filled2, f + 1)
                return ps[:, f % 8, :]

            def choose_groups(i, t):
                n, tiles = t.stop - t.start, range(t.start, t.stop)
                mid_wait(dve, "logit", i)
                chained(nc.vector.tensor_tensor(r2[:, t], r1[:, t], gbias[:].unsqueeze(1).to_broadcast([P, n, E]), ALU.add))
                for j in tiles:
                    for g in range(G):
                        last = nc.vector.max(m8[:, G * j + g, :], r2[:, j, EG * g:EG * (g + 1)])
                chained(last)
                best = m8[:, G * t.start:G * t.stop]
                chained(nc.vector.tensor_tensor(gs[:, t, 0:G], best[:, :, 0].rearrange("p (j g) -> p j g", g=G),
                                                best[:, :, 1].rearrange("p (j g) -> p j g", g=G), ALU.add))
                for j in tiles:
                    last = nc.vector.max(m8[:, j, :], gs[:, j, 0:G])
                chained(last)
                chained(nc.vector.tensor_copy(t8[:, t, 0:KG], m8[:, t, 0:KG]))
                for j in tiles:
                    last = nc.vector.match_replace(gsr[:, j, :], t8[:, j, :], gs[:, j, :], -3 * BIG)
                chained(last)
                chained(nc.vector.tensor_tensor(gsel[:, t], gs[:, t, 0:G], gsr[:, t, 0:G], ALU.not_equal))

            def leave_groups(t):
                tiles = range(t.start, t.stop)
                chained(nc.vector.tensor_scalar(gpen[:, t], gsel[:, t], BIG, -BIG, ALU.mult, ALU.add))
                for j in tiles:
                    last = nc.vector.tensor_tensor(r3[:, j, 0:E].rearrange("p (g e) -> p g e", e=EG),
                                                   r2[:, j, :].rearrange("p (g e) -> p g e", e=EG),
                                                   gsel[:, j, :].unsqueeze(2).to_broadcast([P, G, EG]), ALU.mult)
                chained(last)
                for j in tiles:
                    last = nc.vector.tensor_tensor(r3[:, j, 0:E].rearrange("p (g e) -> p g e", e=EG),
                                                   r3[:, j, 0:E].rearrange("p (g e) -> p g e", e=EG),
                                                   gpen[:, j, :].unsqueeze(2).to_broadcast([P, G, EG]), ALU.add)
                chained(last)

            def choose_experts(t):
                tiles = range(t.start, t.stop)
                for j in tiles:
                    last = nc.vector.max(m8[:, NT + j, :], r3[:, j, 0:E])
                chained(last)
                chained(nc.vector.tensor_copy(t6[:, t, 0:TOPK], m8[:, NT + t.start:NT + t.stop, 0:TOPK]))
                for j in tiles:
                    last = nc.vector.match_replace(r4[:, j, :], t6[:, j, :], r3[:, j, :], -3 * BIG)
                chained(last)
                chained(nc.vector.tensor_tensor(r2[:, t], r3[:, t, 0:E], r4[:, t, 0:E], ALU.not_equal))

            dve.wait_ge(small_dma, 16 * 5)
            dve.wait_ge(tiles_set, 6)
            nc.vector.tensor_copy(x1T[:, 1, 0:P * (NT - 1)], take2("x2T", 1)[:, 0:P * (NT - 1)]).then_inc(emptied2_v, 1)
            choose_groups(0, BEFORE)
            leave_groups(BEFORE)
            add_pair(NT - 1)
            dve.wait_ge(pair_sum, NT)
            norm_variance(x_sb, LAST)
            norm_output(x_sb, x1, 3, LAST)
            nc.vector.tensor_copy(x1T[:, :, P * (NT - 1):P * NT],
                                  take2("x2T", 2)[:, 0:CC * P].rearrange("p (c t) -> p c t", t=P)).then_inc(emptied2_v, 1)
            choose_experts(BEFORE)
            choose_groups(1, LAST)
            leave_groups(LAST)
            choose_experts(LAST)
            nc.vector.tensor_scalar(sel16[:], r2[:], valid[:, 0:1], None, ALU.mult).then_inc(routed, 1)
            dve.wait_ge(routed, 1)
            nc.vector.scalar_tensor_tensor(posm[:], sel16[:], -CHOSEN,
                                           take2("pos")[:, 0:NT * E].rearrange("p (j e) -> p j e", e=E),
                                           ALU.mult, ALU.add).then_inc(emptied2_v, 1)
            mid_wait(dve, "pos")

            def build(g, par, half):
                for j in (2 * half, 2 * half + 1):
                    last = nc.vector.tensor_tensor(disp[:, par, j, :, 0:CAP],
                                                   posm[:, j, bass.ds(GE * g, GE)].unsqueeze(2).to_broadcast([P, GE, CAP]),
                                                   slots[:].unsqueeze(1).to_broadcast([P, GE, CAP]), ALU.is_equal)
                last.then_inc(disp_built, 1)

            def group_weights(g, par):
                nc.vector.tensor_copy(w_grp[:, par], w16[:, :, bass.ds(GE * g, GE), :]).then_inc(w_built, 1)

            build(0, 0, 0)
            build(0, 0, 1)
            chained(nc.vector.tensor_tensor(r1[:], r1[:], r2[:], ALU.mult))
            chained(nc.vector.tensor_reduce(wsum[:], r1[:], AX.X, ALU.add))
            chained(nc.vector.reciprocal(wrec[:], wsum[:]))
            chained(nc.vector.scalar_tensor_tensor(r1[:], r1[:], SCALE, wrec[:].unsqueeze(2).to_broadcast([P, NT, E]),
                                                   ALU.mult, ALU.mult))
            chained(nc.vector.tensor_copy(w16[:, :, :, 0], r1[:]))
            chained(nc.vector.tensor_tensor(w16[:, :, :, 1], r1[:], w16[:, :, :, 0], ALU.subtract))
            group_weights(0, 0)
            build(1, 1, 0)

            gu_bank, misc2, dn_bank, dT_bank = ps[:, 0:2], ps[:, 3], ps[:, 4], ps[:, 7]

            def move_weights(g, par):
                dve.wait_ge(w_filled, g + 1)
                wv4 = misc2[:, C:C + 4 * GP].rearrange("p (q e s) -> p q e s", e=2, s=2)
                for s in range(2):
                    last = nc.vector.tensor_reduce(ws_slot[SLOT * s:SLOT * (s + 1), par, :],
                                                   wv4[SLOT * s:SLOT * (s + 1), :, s, :], AX.X, ALU.add)
                last.then_inc(w_copied, 1)

            def pair_step(i, q, first=False, parts="GTDBN"):
                n = 2 * GP * i + q
                if "T" in parts and not (first and q < 1):
                    dve.wait_ge(hT_filled, n)
                    if not (first and q < 3):
                        dve.wait_ge(dn_filled, n - 2)
                    nc.vector.tensor_copy(hT[:, (q - 1) % 2, :], misc2[0:F, 0:P]).then_inc(hT_copied, 1)
                if "G" in parts:
                    dve.wait_ge(dT_filled, n + 1)
                    if not (first and q < GP):
                        dve.wait_ge(comb_done, n - GP + 1)
                    nc.vector.tensor_copy(dispT[:, q % GP, :],
                                          dT_bank.bitcast(F16)[:, 512 * (q % 2):512 * (q % 2 + 1)]).then_inc(dT_copied, 1)
                    dve.wait_ge(silu_done, n + 1)
                    if not (first and q < 2):
                        dve.wait_ge(hT_filled, n - 1)
                    nc.vector.tensor_tensor(h_sb[:, q % 2, :], act_g[:, q % 2, :],
                                            gu_bank[:, q % 2, F:2 * F], ALU.mult).then_inc(h_ready, 1)
                if "D" in parts:
                    if q % GP == 0:
                        group_weights(2 * i + q // GP + 1, (q // GP + 1) % 2)
                        build(2 * i + q // GP + 1, (q // GP + 1) % 2, 1)
                    if q % GP == GP - 1:
                        move_weights(2 * i + q // GP + 1, (q // GP + 1) % 2)
                    if q % GP == GP - 1 and "B" in parts:
                        build(2 * i + q // GP + 2, (q // GP) % 2, 0)
                if "N" in parts and not (first and q < 1):
                    g1p, dq = ((q - 1) // GP) % 2, (q - 1) % GP
                    dve.wait_ge(o_high, n)
                    nc.vector.scalar_tensor_tensor(o_hl[:, (q - 1) % 2, 1, :], dn_bank[:, 0:C],
                                                   ws_slot[:, g1p, dq:dq + 1], o_hl[:, (q - 1) % 2, 0, :],
                                                   ALU.mult, ALU.subtract).then_inc(o_low, 1)

            move_weights(0, 0)
            for q in range(2 * GP):
                pair_step(0, q, first=True)
            with dve.Fori(1, NG // 2 - 1) as i:
                for q in range(2 * GP):
                    pair_step(i, q)
            for q in range(2 * GP):
                pair_step(NG // 2 - 1, q, parts="GTDN" if q < GP else "GTN")
            pair_step(NG // 2, 0, parts="TN")
            dve.wait_ge(y_filled, 2)
            nc.vector.tensor_copy(yT_sb[:, 1, :], ps[:, 6, :]).then_inc(y_copied, 1)
            dve.wait_ge(x2_summed, 1)
            dve.wait_ge(yb_filled, 1)
            for i in range(2):
                two = x_sb[:, 2 * i:2 * i + 2, :].rearrange("p a c -> p (a c)")
                last = nc.vector.tensor_tensor(two, two, ps[:, i, :], ALU.add)
            chained(last)
            norm_variance(x_sb)
            norm_output(x_sb, x1, 4)


_INS = ["x", "ctx_1024", "mask_BxS2_bf1", "L0_attn_w_qkv", "L0_attn_w_proj", "L0_attn_b_proj", "L0_xattn_Wq",
        "L0_xattn_Wk", "L0_xattn_Wv", "L0_xattn_Wo", "L0_ffn_gate_w", "L0_ffn_bias", "L0_ffn_w_gate", "L0_ffn_w_up",
        "L0_ffn_w_down", "L0_ffn_ws_gate", "L0_ffn_ws_up", "L0_ffn_ws_down"]


def kernel(**inputs):
    import numpy as np
    import concourse.bacc as bacc
    from concourse.bass_utils import run_bass_kernel_spmd

    nc = bacc.Bacc("TRN2", target_bir_lowering=False, num_devices=1)
    arrays, args = {}, []
    for name in _INS:
        a = np.ascontiguousarray(inputs[name])
        if a.dtype == np.bool_:
            a = a.view(np.uint8)
        arrays[f"in_{name}"] = a
        args.append(nc.dram_tensor(f"in_{name}", a.shape, mybir.dt.from_np(a.dtype), kind="ExternalInput").ap())
    y = nc.dram_tensor("y", (B, N, C), F32, kind="ExternalOutput").ap()
    decoder_kernel(nc, *args, y)
    r = run_bass_kernel_spmd(nc, [arrays], core_ids=[0])
    return r.results[0]["y"]
```
